# Optimizing a Trainium2 kernel written in Bass

```python
import numpy as np
import jax
import jax.numpy as jnp

def _softmax(x, axis=-1):
    return jax.nn.softmax(x, axis=axis)

def _gelu(x):
    return jax.nn.gelu(x, approximate=True)

def _silu(x):
    return jax.nn.silu(x)

def _sigmoid(x):
    return jax.nn.sigmoid(x)

def _layernorm(x, axis=-1, eps=1e-05):
    m = jnp.mean(x, axis=axis, keepdims=True)
    v = jnp.var(x, axis=axis, keepdims=True)
    return (x - m) / jnp.sqrt(v + eps)

def _scatter_add(tgt, idx, src, axis=0):
    return tgt.at[idx].add(src)

def _segment_sum(src, seg, n):
    return jax.ops.segment_sum(src, seg, n)
kernel_name = 'mk_decoder_preln_d1_seqx_r8_7953c6'

def setup_inputs(seed: int=0):
    np.random.seed(seed)
    _w = jnp.asarray

    def _rec_inputs():
        import jax
        import jax.numpy as jnp
        _rk = jax.random.key(seed)
        x = -0.0003929 + 0.9999 * jax.random.normal(jax.random.fold_in(_rk, 1), (32, 64, 512), jnp.float32)
        _lenS = 64 - jax.random.randint(jax.random.fold_in(_rk, 7), (32,), 0, max(1, 64 // 4) + 1, jnp.int32)
        _lenS2 = 64 - jax.random.randint(jax.random.fold_in(_rk, 8), (32,), 0, max(1, 64 // 4) + 1, jnp.int32)
        _ctx_4096P = jax.random.normal(jax.random.fold_in(_rk, 11), (32, 16, 512), jnp.float32)
        _ctx_4096c = jax.random.dirichlet(jax.random.fold_in(_rk, 511), 0.3 * jnp.ones((16,), jnp.float32), (32, 64))
        _ctx_4096t = jnp.einsum('bsk,bkd->bsd', _ctx_4096c, _ctx_4096P)
        _ctx_4096t = _ctx_4096t * jax.lax.rsqrt(jnp.mean(jnp.square(_ctx_4096t)) + 1e-12) * 0.953939
        ctx_4096 = 2.81802e-05 + 1.00001 * (_ctx_4096t + 0.3 * jax.random.normal(jax.random.fold_in(_rk, 611), (32, 64, 512), jnp.float32))
        pos_BxS2 = jnp.broadcast_to(jnp.arange(64, dtype=jnp.int32), (32, 64))
        _validS = jnp.arange(64)[None, :] < _lenS[:, None]
        _validS2 = jnp.arange(64)[None, :] < _lenS2[:, None]
        _causal = jnp.tril(jnp.ones((64, 64), dtype=bool))
        mask_BxSxS2_ik0 = jnp.where(jnp.broadcast_to(_validS2[:, None, :], (32, 64, 64)), 0, 1).astype(jnp.int32)
        return (x, ctx_4096, pos_BxS2, mask_BxSxS2_ik0)
    x, ctx_4096, pos_BxS2, mask_BxSxS2_ik0 = _rec_inputs()

    def _L0_attn_setup():
        import jax, jax.numpy as jnp
        import numpy as np
        HIDDEN = 512
        N_HEADS = 32
        N_KV = 8
        HEAD_DIM = HIDDEN // N_HEADS
        Q_PER_KV = N_HEADS // N_KV
        SEQ = 256
        ROPE_BASE = 1000000.0
        POS_SCALE = 1.0
        SM_SCALE = 1.0 / HEAD_DIM
        BLOCK = 64
        LOCAL_BLOCKS = 16
        VERT_STRIDE = 8

        def _blocksparse_mask(seq_len):
            nb = seq_len // BLOCK
            qb = np.arange(nb)[:, None]
            kb = np.arange(nb)[None, :]
            bmask = (kb <= qb) & ((qb - kb < LOCAL_BLOCKS) | ((kb + 1) % VERT_STRIDE == 0))
            emask = np.kron(bmask, np.ones((BLOCK, BLOCK), dtype=bool))
            i = np.arange(seq_len)
            emask &= i[:, None] >= i[None, :]
            return jnp.asarray(emask)

        def _rope(x, cos, sin):
            x1, x2 = jnp.split(x, 2, axis=-1)
            rot = jnp.concatenate([-x2, x1], axis=-1)
            return x * cos[None, :, None, :] + rot * sin[None, :, None, :]
        key = jax.random.key(seed)
        k1, k2, k3, k4, k5 = jax.random.split(key, 5)
        qkv_out = (N_HEADS + 2 * N_KV) * HEAD_DIM
        return {'hidden_states': jax.random.normal(k1, (1, SEQ, HIDDEN), dtype=jnp.float32), 'w_qkv': jax.random.normal(k2, (qkv_out, HIDDEN), dtype=jnp.float32) * 0.02, 'b_qkv': jnp.zeros((qkv_out,), dtype=jnp.float32), 'w_dense': jax.random.normal(k3, (HIDDEN, HIDDEN), dtype=jnp.float32) * 0.02, 'b_dense': jnp.zeros((HIDDEN,), dtype=jnp.float32)}
    _L0_attn_all = _L0_attn_setup()
    _L0_attn_in = {k: v for k, v in _L0_attn_all.items() if k in ('w_qkv', 'b_qkv', 'w_dense', 'b_dense')}
    del _L0_attn_all

    def _L0_xattn_setup():
        import jax, jax.numpy as jnp
        import numpy as np
        B, S, E = (2, 256, 512)
        H, KVH, D = (32, 8, 128)
        GROUPS = H // KVH
        MAX_POS = 512
        ROPE_THETA = 10000.0

        def _rope_tables(max_pos, dim, theta):
            inv_freq = 1.0 / theta ** (jnp.arange(0, dim, 2, dtype=jnp.float32) / dim)
            t = jnp.arange(max_pos, dtype=jnp.float32)
            freqs = jnp.einsum('i,j->ij', t, inv_freq)
            emb = jnp.concatenate([freqs, freqs], axis=-1)
            return (jnp.cos(emb), jnp.sin(emb))

        def _rotate_half(x):
            x1, x2 = (x[..., :x.shape[-1] // 2], x[..., x.shape[-1] // 2:])
            return jnp.concatenate([-x2, x1], axis=-1)
        key = jax.random.key(seed)
        ks = jax.random.split(key, 8)
        scale_w = 1.0 / np.sqrt(E)
        query = jax.random.normal(ks[0], (B, S, E), dtype=jnp.float32)
        k_in = jax.random.normal(ks[1], (B, S, E), dtype=jnp.float32)
        v_in = jax.random.normal(ks[2], (B, S, E), dtype=jnp.float32)
        position_ids = jnp.broadcast_to(jnp.arange(S, dtype=jnp.int64), (B, S))
        src_mask = jnp.tril(jnp.ones((S, S), dtype=jnp.int32))
        src_mask = jnp.broadcast_to(src_mask, (B, S, S))
        Wq = jax.random.normal(ks[3], (E, H * D), dtype=jnp.float32) * scale_w
        Wk = jax.random.normal(ks[4], (E, KVH * D), dtype=jnp.float32) * scale_w
        Wv = jax.random.normal(ks[5], (E, KVH * D), dtype=jnp.float32) * scale_w
        Wo = jax.random.normal(ks[6], (H * D, E), dtype=jnp.float32) * scale_w
        return {'query': query, 'key': k_in, 'value': v_in, 'position_ids': position_ids, 'src_mask': src_mask, 'Wq': Wq, 'Wk': Wk, 'Wv': Wv, 'Wo': Wo}
    _L0_xattn_all = _L0_xattn_setup()
    _L0_xattn_in = {k: v for k, v in _L0_xattn_all.items() if k in ('Wq', 'Wk', 'Wv', 'Wo')}
    del _L0_xattn_all

    def _L0_ffn_setup():
        import jax, jax.numpy as jnp
        import numpy as np
        H = 512
        I = 1792
        G = 128

        def dequant(q, s, g=G):
            O, In = q.shape
            return (q.reshape(O, In // g, g).astype(s.dtype) * s[:, :, None]).reshape(O, In)
        key = jax.random.key(seed)
        ks = jax.random.split(key, 7)
        x = jax.random.normal(ks[0], (2, 256, H), dtype=jnp.float32)

        def mk_qlinear(kq, ksc, out_d, in_d):
            q = jax.random.randint(kq, (out_d, in_d), -8, 8, dtype=jnp.int32)
            s = jax.random.uniform(ksc, (out_d, in_d // G), dtype=jnp.float32, minval=0.005, maxval=0.02)
            return (q, s)
        gate_q, gate_s = mk_qlinear(ks[1], ks[2], I, H)
        up_q, up_s = mk_qlinear(ks[3], ks[4], I, H)
        down_q, down_s = mk_qlinear(ks[5], ks[6], H, I)
        return {'x': x, 'gate_q': gate_q, 'gate_s': gate_s, 'up_q': up_q, 'up_s': up_s, 'down_q': down_q, 'down_s': down_s}
    _L0_ffn_all = _L0_ffn_setup()
    _L0_ffn_in = {k: v for k, v in _L0_ffn_all.items() if k in ('gate_q', 'gate_s', 'up_q', 'up_s', 'down_q', 'down_s')}
    del _L0_ffn_all
    return {'x': x, 'ctx_4096': ctx_4096, 'pos_BxS2': pos_BxS2, 'mask_BxSxS2_ik0': mask_BxSxS2_ik0, 'L0_attn_w_qkv': _L0_attn_in['w_qkv'], 'L0_attn_b_qkv': _L0_attn_in['b_qkv'], 'L0_attn_w_dense': _L0_attn_in['w_dense'], 'L0_attn_b_dense': _L0_attn_in['b_dense'], 'L0_xattn_Wq': _L0_xattn_in['Wq'], 'L0_xattn_Wk': _L0_xattn_in['Wk'], 'L0_xattn_Wv': _L0_xattn_in['Wv'], 'L0_xattn_Wo': _L0_xattn_in['Wo'], 'L0_ffn_gate_q': _L0_ffn_in['gate_q'], 'L0_ffn_gate_s': _L0_ffn_in['gate_s'], 'L0_ffn_up_q': _L0_ffn_in['up_q'], 'L0_ffn_up_s': _L0_ffn_in['up_s'], 'L0_ffn_down_q': _L0_ffn_in['down_q'], 'L0_ffn_down_s': _L0_ffn_in['down_s']}

def reference(x, ctx_4096, pos_BxS2, mask_BxSxS2_ik0, L0_attn_w_qkv, L0_attn_b_qkv, L0_attn_w_dense, L0_attn_b_dense, L0_xattn_Wq, L0_xattn_Wk, L0_xattn_Wv, L0_xattn_Wo, L0_ffn_gate_q, L0_ffn_gate_s, L0_ffn_up_q, L0_ffn_up_s, L0_ffn_down_q, L0_ffn_down_s):
    import jax
    import jax.numpy as jnp

    def _L0_attn_ref(hidden_states, w_qkv, b_qkv, w_dense, b_dense):
        import jax, jax.numpy as jnp
        import numpy as np
        HIDDEN = 512
        N_HEADS = 32
        N_KV = 8
        HEAD_DIM = HIDDEN // N_HEADS
        Q_PER_KV = N_HEADS // N_KV
        SEQ = 256
        ROPE_BASE = 1000000.0
        POS_SCALE = 1.0
        SM_SCALE = 1.0 / HEAD_DIM
        BLOCK = 64
        LOCAL_BLOCKS = 16
        VERT_STRIDE = 8

        def _blocksparse_mask(seq_len):
            nb = seq_len // BLOCK
            qb = np.arange(nb)[:, None]
            kb = np.arange(nb)[None, :]
            bmask = (kb <= qb) & ((qb - kb < LOCAL_BLOCKS) | ((kb + 1) % VERT_STRIDE == 0))
            emask = np.kron(bmask, np.ones((BLOCK, BLOCK), dtype=bool))
            i = np.arange(seq_len)
            emask &= i[:, None] >= i[None, :]
            return jnp.asarray(emask)

        def _rope(x, cos, sin):
            x1, x2 = jnp.split(x, 2, axis=-1)
            rot = jnp.concatenate([-x2, x1], axis=-1)
            return x * cos[None, :, None, :] + rot * sin[None, :, None, :]
        B, S, _ = hidden_states.shape
        qkv = jnp.einsum('bsh,oh->bso', hidden_states, w_qkv) + b_qkv
        qkv = qkv.reshape(B, S, N_KV, Q_PER_KV + 2, HEAD_DIM)
        q = qkv[:, :, :, :Q_PER_KV].reshape(B, S, N_HEADS, HEAD_DIM)
        k = qkv[:, :, :, Q_PER_KV]
        v = qkv[:, :, :, Q_PER_KV + 1]
        inv_freq = 1.0 / ROPE_BASE ** (jnp.arange(0, HEAD_DIM, 2, dtype=jnp.float32) / HEAD_DIM)
        t = jnp.arange(S, dtype=jnp.float32) * POS_SCALE
        freqs = jnp.outer(t, inv_freq)
        emb = jnp.concatenate([freqs, freqs], axis=-1)
        cos, sin = (jnp.cos(emb), jnp.sin(emb))
        q = _rope(q, cos, sin)
        k = _rope(k, cos, sin)
        k = jnp.repeat(k, Q_PER_KV, axis=2)
        v = jnp.repeat(v, Q_PER_KV, axis=2)
        mask = _blocksparse_mask(S)
        scores = jnp.einsum('bqhd,bkhd->bhqk', q, k) * SM_SCALE
        scores = jnp.where(mask[None, None], scores, jnp.finfo(scores.dtype).min)
        probs = jax.nn.softmax(scores, axis=-1)
        ctx = jnp.einsum('bhqk,bkhd->bqhd', probs, v).reshape(B, S, HIDDEN)
        out = jnp.einsum('bsh,oh->bso', ctx, w_dense) + b_dense
        return out

    def _L0_xattn_ref(query, key, value, position_ids, src_mask, Wq, Wk, Wv, Wo):
        import jax, jax.numpy as jnp
        import numpy as np
        B, S, E = (2, 256, 512)
        H, KVH, D = (32, 8, 128)
        GROUPS = H // KVH
        MAX_POS = 512
        ROPE_THETA = 10000.0

        def _rope_tables(max_pos, dim, theta):
            inv_freq = 1.0 / theta ** (jnp.arange(0, dim, 2, dtype=jnp.float32) / dim)
            t = jnp.arange(max_pos, dtype=jnp.float32)
            freqs = jnp.einsum('i,j->ij', t, inv_freq)
            emb = jnp.concatenate([freqs, freqs], axis=-1)
            return (jnp.cos(emb), jnp.sin(emb))

        def _rotate_half(x):
            x1, x2 = (x[..., :x.shape[-1] // 2], x[..., x.shape[-1] // 2:])
            return jnp.concatenate([-x2, x1], axis=-1)
        nb, q_len, _ = query.shape
        q = (query @ Wq).reshape(nb, q_len, H, D).transpose(0, 2, 1, 3)
        k = (key @ Wk).reshape(nb, q_len, KVH, D).transpose(0, 2, 1, 3)
        v = (value @ Wv).reshape(nb, q_len, KVH, D).transpose(0, 2, 1, 3)
        cos_t, sin_t = _rope_tables(MAX_POS, D, ROPE_THETA)
        cos = cos_t[position_ids][:, None]
        sin = sin_t[position_ids][:, None]
        q = q * cos + _rotate_half(q) * sin
        k = k * cos + _rotate_half(k) * sin
        k = jnp.repeat(k, GROUPS, axis=1)
        v = jnp.repeat(v, GROUPS, axis=1)
        scores = jnp.einsum('bhqd,bhkd->bhqk', q, k) / jnp.sqrt(jnp.float32(D))
        mask = src_mask[:, None]
        scores = jnp.where(mask == 0, jnp.float32(-1000000000.0), scores)
        attn = jax.nn.softmax(scores, axis=-1)
        x = jnp.einsum('bhqk,bhkd->bhqd', attn, v)
        x = x.transpose(0, 2, 1, 3).reshape(nb, q_len, H * D)
        return x @ Wo

    def _L0_ffn_ref(x, gate_q, gate_s, up_q, up_s, down_q, down_s):
        import jax, jax.numpy as jnp
        import numpy as np
        H = 512
        I = 1792
        G = 128

        def dequant(q, s, g=G):
            O, In = q.shape
            return (q.reshape(O, In // g, g).astype(s.dtype) * s[:, :, None]).reshape(O, In)
        Wg = dequant(gate_q, gate_s)
        Wu = dequant(up_q, up_s)
        Wd = dequant(down_q, down_s)
        gate_score = jax.nn.silu(jnp.einsum('bsh,ih->bsi', x, Wg))
        intermediate = gate_score * jnp.einsum('bsh,ih->bsi', x, Wu)
        return jnp.einsum('bsi,hi->bsh', intermediate, Wd)
    x = x + _L0_attn_ref(_layernorm(x, axis=-1), L0_attn_w_qkv, L0_attn_b_qkv, L0_attn_w_dense, L0_attn_b_dense)
    x = x + _L0_xattn_ref(_layernorm(x, axis=-1), ctx_4096, ctx_4096, pos_BxS2, mask_BxSxS2_ik0, L0_xattn_Wq, L0_xattn_Wk, L0_xattn_Wv, L0_xattn_Wo)
    x = x + _L0_ffn_ref(_layernorm(x, axis=-1), L0_ffn_gate_q, L0_ffn_gate_s, L0_ffn_up_q, L0_ffn_up_s, L0_ffn_down_q, L0_ffn_down_s)
    return x

_drawn_inputs = setup_inputs


def setup_inputs(seed=0):
    import zlib

    import numpy as np

    out = dict(_drawn_inputs(seed))
    spreads = {'L0_attn_b_qkv': (0.0, 0.1), 'L0_attn_b_dense': (0.0, 0.1)}
    factors = {}
    for name, (base, spread) in spreads.items():
        noise = np.random.default_rng([zlib.crc32(name.encode()), seed]).standard_normal(out[name].shape)
        drawn = base * np.exp(spread * noise) if base else spread * noise
        out[name] = jnp.asarray(drawn.astype(out[name].dtype))
    for name, factor in factors.items():
        out[name] = (out[name] * factor).astype(out[name].dtype)
    return out
```

```python
from contextlib import ExitStack

import numpy as np

import concourse.bass as bass
from concourse import mybir

F32 = mybir.dt.float32
F32R = mybir.dt.float32r
F16 = mybir.dt.float16
I32 = mybir.dt.int32
U8 = mybir.dt.uint8
ALU = mybir.AluOpType
ACT = mybir.ActivationFunctionType
AX_X = mybir.AxisListType.X

P = 128
B, S, D = 32, 64, 512
T = B * S
TILES = T // P
GROUP = 4
GROUPS = TILES // GROUP
GT = GROUP * P
KT = D // P
G = 8
HPG = 4
HD_SELF, HD_X = 16, 128
SCALE_SELF = 1.0 / HD_SELF
SCALE_X = float(np.float32(1.0) / np.sqrt(np.float32(HD_X)))
FILL_SELF = float(np.finfo(np.float32).min)
FILL_X = -1.0e9 / SCALE_X
MAX_POS = 512
FF = 1792
FCH = FF // 256
EPS = 1e-5


class Signal:

    def __init__(self, nc, ctx, name, per=0, step=1, base=0):
        self.sem = ctx.enter_context(nc.semaphore(name))
        self.per, self.step, self.base = per, step, base

    def at(self, turn, n):
        value = (turn * self.per + n + 1 + self.base) * self.step
        return max(value, self.base * self.step) if type(value) is int else value

    def two_before(self, turn, n):
        return self.at(turn, max(n - 2, -1))


def start(eng, *signals):
    for signal in signals:
        assert signal.base == 1
        eng.sem_inc(signal.sem, signal.step)


class Banks:

    def __init__(self, banks, order, readers):
        self.banks, self.order, self.readers = banks, order, readers

    def __getitem__(self, use):
        return self.banks[self.order.index(use) % len(self.banks)]

    def last_reads(self, turn, use):
        n = self.order.index(use) - len(self.banks)
        if n >= 0:
            return [(signal.sem, signal.at(turn, event)) for signal, event in self.readers(self.order[n])]
        return [(signal.sem, signal.at(turn, -1)) for old in self.order[-len(self.banks):] for signal, _ in self.readers(old)]


CONSTS = 7


def settle(eng, m):
    eng.sem_inc(m["settled"][eng.engine].sem, 1)


def split3(nc, out, wh, wl, xh, xl, first, last):
    nc.tensor.matmul(out, wh, xh, start=first, stop=False)
    nc.tensor.matmul(out, wh, xl, start=False, stop=False)
    return nc.tensor.matmul(out, wl, xh, start=False, stop=last)


def build(nc, io, out):
    KB = 1024
    BASE = 2 * KB
    outer = ExitStack()
    with outer:
        names = {}

        def at(name, kb, shape, dt):
            n = 1
            for s in shape:
                n *= s
            assert BASE + kb * KB + n * mybir.dt.size(dt) <= 229368, name
            names[name] = (kb, n)
            return nc.alloc_sbuf_tensor_at(name, [P, n], dt, offset=int(BASE + kb * KB))

        XR, XT, WR, ER, FR = 0, 32, 96, 128, 160
        x_res = at("x_res", XR, [TILES * D], F32)
        ident = at("ident", FR, [P], F32)
        small = at("small", FR + 0.5, [128], F32)
        mask8 = at("mask8", FR + 1, [B * S], U8)
        cosx = at("cosx", FR + 3, [T], F32)
        sinx = at("sinx", FR + 11, [T], F32)
        F0 = FR + 19
        stats = at("stats", FR + 61, [TILES * 6], F32)
        mv = at("mv", FR + 61.375, [TILES * 2], F32)
        rstd = at("rstd", FR + 61.5, [TILES], F32)
        kscr = nc.dram_tensor("k_scratch", (G, P, 2, T), F16, kind="Internal").ap()
        vscr = nc.dram_tensor("v_scratch", (T, G * HD_X), F32, kind="Internal").ap()

        q_b = small[:, 0:4]
        k_b = small[:, 4:8]
        q_bs = small[:, 8:12]
        k_bs = small[:, 12:16]
        hmask = small[:, 16:24]
        iota = small[:, 24:28]
        xr = lambda tile: x_res[:, bass.ds(tile * D, D)]

        wqk_h = at("wqk_h", WR, [KT * 1024], F32R)
        wqk_l = at("wqk_l", WR + 16, [KT * 1024], F32R)
        wd_h = at("wd_h", XT, [KT * D], F32R)
        wd_l = at("wd_l", XT + 8, [KT * D], F32R)
        wv_h = at("wv_h", XT + 48, [KT * P], F32R)
        wv_l = at("wv_l", XT + 50, [KT * P], F32R)
        cos_a = at("cos_a", F0, [S], F32)
        sin_a = at("sin_a", F0 + 0.25, [S], F32)
        causal = at("causal", F0 + 0.5, [S], I32)
        bv_row = at("bv_row", F0 + 0.75, [P], F32)
        bd_row = at("bd_row", F0 + 1.25, [D], F32)
        A0 = F0 + 3.25

        consts_in = Signal(nc, outer, "consts_in", step=16)

        settled = {e.engine: Signal(nc, outer, n) for e, n in ((nc.gpsimd, "settled_pool"), (nc.vector, "settled_dve"))}

        with ExitStack() as ctx:
            NCH = 15
            RING = 4
            stage = at("stage0", ER, [RING * 512], F32)
            pos_i = at("pos_i", ER + 8, [T], I32)
            pos_f = at("pos_f", ER + 16, [T], F32)
            pos_n = at("pos_n", A0, [T], F32)
            onehot = at("onehot", XT + 16, [4 * 512], F32R)
            tab_h = at("tab_h", XT + 24, [1024], F32R)
            tab_l = at("tab_l", XT + 28, [1024], F32R)
            mask_i = at("mask_i", ER + 24, [T], I32)
            psT = [ctx.enter_context(nc.psum_tensor(f"psT{n}", [P, 512], F32)) for n in range(4)]
            loaded = Signal(nc, ctx, "setup_loaded", step=16)
            pos_in = Signal(nc, ctx, "pos_in", step=16)
            mask_in = Signal(nc, ctx, "mask_in", step=16)
            x_in = Signal(nc, ctx, "x_in", step=16)
            w_in = [Signal(nc, ctx, f"w_in{r}", step=16) for r in range(RING)]
            w_hi = Signal(nc, ctx, "w_hi")
            w_lo = Signal(nc, ctx, "w_lo")
            poss = Signal(nc, ctx, "pos_ready")
            oh = Signal(nc, ctx, "onehot_ready")
            tabp = Signal(nc, ctx, "tables_in_psum")
            cosd = Signal(nc, ctx, "cos_ready")
            sind = Signal(nc, ctx, "sin_ready")
            dve = Signal(nc, ctx, "stats_step")
            rt = Signal(nc, ctx, "sqrt_ready")
            block = ctx.enter_context(nc.Block())

            chunks = []
            tabv = io["rope_x"].rearrange("(k p) n -> p k n", p=P)
            for k2 in range(2):
                chunks.append((tabv[:, 2 * k2:2 * k2 + 2, :], (2, 256), tab_h[:, k2 * 512:k2 * 512 + 512],
                               tab_l[:, k2 * 512:k2 * 512 + 512]))
            for k in range(KT):
                for h in range(2):
                    c = k * 1024 + h * 512
                    chunks.append((io["w_qkv"][k * P:(k + 1) * P, h * 512:(h + 1) * 512], None,
                                   wqk_h[:, c:c + 512], wqk_l[:, c:c + 512]))
            chunks.append((io["w_qkv"].rearrange("(k p) n -> p k n", p=P)[:, :, 1024:1152], (KT, P),
                           wv_h[:, :], wv_l[:, :]))
            for k in range(KT):
                chunks.append((io["w_dense"][k * P:(k + 1) * P, :], None,
                               wd_h[:, k * D:(k + 1) * D], wd_l[:, k * D:(k + 1) * D]))
            assert len(chunks) == NCH
            st = lambda c: stage[:, (c % RING) * 512:(c % RING) * 512 + 512]

            @block.sync
            def _(sp):
                sp.dma_start(pos_i[:, :], io["pos"].partition_broadcast(P)).then_inc(pos_in.sem, 16)
                xv = io["x"].rearrange("(t p) d -> p t d", p=P)
                for q in range(GROUPS):
                    sp.dma_start(x_res[:, q * 4 * D:(q + 1) * 4 * D].rearrange("p (t d) -> p t d", d=D),
                                 xv[:, 4 * q:4 * q + 4, :]).then_inc(x_in.sem, 16)
                for c, (src, shape, hi, lo) in enumerate(chunks):
                    if c >= RING:
                        sp.wait_ge(w_lo.sem, w_lo.at(0, c - RING))
                    dst = st(c) if shape is None else st(c).rearrange("p (a b) -> p a b", a=shape[0])
                    sp.dma_start(dst, src).then_inc(w_in[c % RING].sem, 16)

            @block.scalar
            def _(act):
                act.dma_start(ident[:, :], io["ident"]).then_inc(consts_in.sem, 16)
                act.dma_start(small[:, 0:28], io["small"]).then_inc(consts_in.sem, 16)
                act.dma_start(cos_a[:, :], io["rope_self"][0]).then_inc(consts_in.sem, 16)
                act.dma_start(sin_a[:, :], io["rope_self"][1]).then_inc(consts_in.sem, 16)
                act.dma_start(causal[:, :], io["causal"]).then_inc(consts_in.sem, 16)
                act.dma_start(bv_row[:, :], io["b_v"].partition_broadcast(P)).then_inc(consts_in.sem, 16)
                act.dma_start(bd_row[:, :], io["b_dense"].partition_broadcast(P)).then_inc(consts_in.sem, 16)
                for b in range(2):
                    act.dma_start(mask_i[b * S:(b + 1) * S, :].rearrange("q (b k) -> q b k", k=S),
                                  io["mask"].rearrange("b q k -> q b k")).then_inc(mask_in.sem, 16)
                for c, (src, shape, hi, lo) in enumerate(chunks):
                    act.wait_ge(w_in[c % RING].sem, w_in[c % RING].at(0, c // RING))
                    nc.scalar.activation(hi, st(c), ACT.Copy).then_inc(w_hi.sem, 1)
                    if c == 1:
                        for q in range(GROUPS):
                            act.wait_ge(tabp.sem, tabp.at(0, 2 * q))
                            nc.scalar.activation(cosx[:, q * GT:(q + 1) * GT], psT[0][:, :], ACT.Copy).then_inc(cosd.sem, 1)
                act.wait_ge(dve.sem, TILES * 2 + 1)
                nc.scalar.activation(rstd[:, :], rstd[:, :], ACT.Sqrt).then_inc(rt.sem, 1)
                act.wait_ge(consts_in.sem, CONSTS * 16)

            @block.vector
            def _(v):
                v.wait_ge(pos_in.sem, pos_in.at(0, 0))
                nc.vector.tensor_copy(pos_f[:, :], pos_i[:, :]).then_inc(poss.sem, 1)
                v.wait_ge(poss.sem, poss.at(0, 0))
                nc.vector.tensor_scalar(pos_n[:, :], pos_f[:, :], 0.0, float(MAX_POS), ALU.is_lt, ALU.mult).then_inc(poss.sem, 1)
                v.wait_ge(poss.sem, poss.at(0, 1))
                nc.vector.tensor_tensor(pos_f[:, :], pos_f[:, :], pos_n[:, :], ALU.add).then_inc(poss.sem, 1)
                v.wait_ge(poss.sem, poss.at(0, 2))
                nc.vector.tensor_scalar(pos_f[:, :], pos_f[:, :], 0.0, float(MAX_POS - 1), ALU.max, ALU.min).then_inc(poss.sem, 1)
                v.wait_ge(poss.sem, poss.at(0, 3))
                for c, (src, shape, hi, lo) in enumerate(chunks):
                    v.wait_ge(w_hi.sem, w_hi.at(0, c))
                    nc.vector.tensor_tensor(lo, st(c), hi.bitcast(F32), ALU.subtract).then_inc(w_lo.sem, 1)
                    if c == 1:
                        v.wait_ge(consts_in.sem, CONSTS * 16)
                        for q in range(GROUPS):
                            if q:
                                v.wait_ge(tabp.sem, tabp.at(0, 2 * q - 1))
                            for k in range(4):
                                nc.vector.tensor_scalar(onehot[:, k * 512:(k + 1) * 512], pos_f[:, q * GT:(q + 1) * GT],
                                                        iota[:, k:k + 1], None, ALU.is_equal).then_inc(oh.sem, 1)
                            v.wait_ge(tabp.sem, tabp.at(0, 2 * q + 1))
                            nc.vector.tensor_copy(sinx[:, q * GT:(q + 1) * GT], psT[1][:, :]).then_inc(sind.sem, 1)
                v.wait_ge(mask_in.sem, 32)
                nc.vector.tensor_scalar(mask8[:, :], mask_i[:, :], 0.0, None, ALU.not_equal).then_inc(sind.sem, 1)
                n = 0
                for t in range(TILES):
                    if t % 4 == 0:
                        v.wait_ge(x_in.sem, x_in.at(0, t // 4))
                    nc.vector.bn_stats(stats[:, 6 * t:6 * t + 6], xr(t)).then_inc(dve.sem, 1)
                for t in range(TILES):
                    v.wait_ge(dve.sem, t + 1)
                    nc.vector.bn_aggr(mv[:, 2 * t:2 * t + 2], stats[:, 6 * t:6 * t + 6]).then_inc(dve.sem, 1)
                v.wait_ge(dve.sem, 2 * TILES)
                nc.vector.tensor_scalar_add(rstd[:, :], mv[:, 1:2 * TILES:2], EPS).then_inc(dve.sem, 1)
                v.wait_ge(rt.sem, rt.at(0, 0))
                nc.vector.reciprocal(rstd[:, :], rstd[:, :]).then_inc(dve.sem, 1)

            @block.tensor
            def _(pe):
                pe.wait_ge(w_lo.sem, w_lo.at(0, 1))
                for q in range(GROUPS):
                    pe.wait_ge(oh.sem, oh.at(0, 4 * q + 3))
                    for m in range(2):
                        if q:
                            pe.wait_ge((cosd, sind)[m].sem, (cosd, sind)[m].at(0, q - 1))
                        for k in range(4):
                            c = k * 256 + m * P
                            nc.tensor.matmul(psT[m][:, :], tab_h[:, c:c + P], onehot[:, k * 512:(k + 1) * 512],
                                             start=(k == 0), stop=False)
                            last = nc.tensor.matmul(psT[m][:, :], tab_l[:, c:c + P], onehot[:, k * 512:(k + 1) * 512],
                                                    start=False, stop=(k == 3))
                        last.then_inc(tabp.sem, 1)

        self_attention(nc, at, io, locals())
        cross_keys_values(nc, at, io, locals())
        cross_attention(nc, at, io, locals())
        feed_forward(nc, at, io, out, locals())


def self_attention(nc, at, io, m):
    WR, XT, ER, A0 = m["WR"], m["XT"], m["ER"], m["A0"]
    wqk_h, wqk_l, wd_h, wd_l, wv_h, wv_l = (m[n] for n in ("wqk_h", "wqk_l", "wd_h", "wd_l", "wv_h", "wv_l"))
    xr, mv, rstd, stats, ident = m["xr"], m["mv"], m["rstd"], m["stats"], m["ident"]
    xt_h = at("xta_h", XT + 16, [KT * GT], F32R)
    xt_l = at("xta_l", XT + 24, [KT * GT], F32R)
    ct_h = at("cta_h", XT + 32, [2 * KT * P], F32R)
    ct_l = at("cta_l", XT + 36, [2 * KT * P], F32R)
    r16 = {n: at(n, A0 + 4 * i, [4 * GT], F16) for i, n in enumerate(("qa_h", "qa_l", "ka_h", "ka_l"))}
    A1 = A0 + 16
    t1 = at("t1a", A1, [2 * GT], F32)
    sw = at("swa", A1 + 4, [2 * GT], F32)
    va_h = at("va_h", A1 + 8, [GT], F16)
    va_l = at("va_l", A1 + 9, [GT], F16)
    v32 = at("v32a", A1 + 10, [GT], F32)
    xn = at("xna", A1 + 12, [2 * D], F32)
    on = at("ona", A1 + 16, [2 * D], F32)
    sums = at("sums_a", A1 + 20, [64], F32)
    rinv = at("rinv_a", A1 + 20.25, [64], F32)
    mx = at("mx_a", A1 + 20.5, [16], F32)
    qm_h = at("qm_h", ER, [2 * 2048], F16)
    qm_l = at("qm_l", ER + 8, [2 * 2048], F16)
    pr = at("pr_a", ER + 16, [2 * 512], F32)
    pt_h = at("pta_h", ER + 20, [2 * 512], F16)
    pt_l = at("pta_l", ER + 22, [2 * 512], F16)

    with ExitStack() as ctx:
        ps = [ctx.enter_context(nc.psum_tensor(f"psA{n}", [P, 512], F32)) for n in range(8)]
        psQ, psS, psP, psO = ps[0:2], ps[2:4], ps[4:6], ps[6:8]

        def sig(name, per):
            return Signal(nc, ctx, name, per, base=1)

        s_xn, s_xp, s_xh, s_xl = sig("a_xn", 4), sig("a_xnT_psum", 4), sig("a_xT_hi", 4), sig("a_xT_lo", 4)
        s_bd = sig("a_bias_added", 4)
        s_vp, s_v32, s_vh, s_vl = sig("a_v_psum", 1), sig("a_v", 1), sig("a_v_hi", 1), sig("a_v_lo", 1)
        s_qp = sig("a_proj_psum", 8)
        s_sw, s_t1, s_t2, s_r = sig("a_swapped", 8), sig("a_cos_term", 8), sig("a_sin_term", 8), sig("a_roped", 8)
        s_rh, s_rl = sig("a_roped_hi", 8), sig("a_roped_lo", 8)
        s_qm = sig("a_q_masked", 8)
        s_S = sig("a_scores_psum", 16)
        s_fill, s_pred, s_mx, s_sub = sig("a_filled", 16), sig("a_causal", 16), sig("a_max", 16), sig("a_less_max", 16)
        s_exp, s_sum, s_T = sig("a_exp", 16), sig("a_sum", 16), sig("a_pT_psum", 16)
        s_ph, s_pl, s_O = sig("a_pT_hi", 16), sig("a_pT_lo", 16), sig("a_o_psum", 16)
        s_ri, s_on = sig("a_inv_sum", 2), sig("a_o_normal", 4)
        s_cp, s_ch, s_cl = sig("a_oT_psum", 4), sig("a_oT_hi", 4), sig("a_oT_lo", 4)
        s_Y, s_xr, s_st = sig("a_dense_psum", 4), sig("a_residual", 4), sig("a_stats", 4)
        block = ctx.enter_context(nc.Block())

        steps = [("ln", t) for t in range(4)] + [("v", 0)] + [("proj", n) for n in range(4)]
        for n in range(16 + 3):
            if n in (2, 4):
                steps += [("proj", n + 2), ("proj", n + 3)]
            if n < 16:
                if n % 2 == 0:
                    steps.append(("mask", n // 2))
                steps.append(("score", n))
            if 1 <= n <= 16:
                steps.append(("turn", n - 1))
            if n in (10, 18):
                steps += [("norm", n // 8 * 2 - 2 + t) for t in range(2)]
            if 2 <= n <= 17:
                steps.append(("pv", n - 2))
            if n in (10, 18):
                u = 0 if n == 10 else 1
                for t in (2 * u, 2 * u + 1):
                    steps += [("dense", t), ("y", t)]
        order = [("oT" if kind == "dense" else kind, n) for kind, n in steps
                 if kind in ("ln", "v", "proj", "dense", "y")]

        def readers(use):
            kind, n = use
            return {"ln": [(s_xl, n)], "v": [(s_v32, n)], "proj": [(s_t1, n)], "oT": [(s_cl, n)], "y": [(s_xr, n)]}[kind]

        bank = Banks(psQ, order, readers)

        COL = lambda t, hp, b: ((t * 2 + hp) * 2 + b) * S

        @block.tensor
        def _(pe):
            start(pe, s_xp, s_vp, s_qp, s_S, s_T, s_O, s_cp, s_Y)
            with pe.Fori(0, GROUPS) as i:
                for kind, n in steps:
                    if kind == "ln":
                        for read, value in bank.last_reads(i, (kind, n)):
                            pe.wait_ge(read, value)
                        pe.wait_ge(s_xn.sem, s_xn.at(i, n))
                        for k in range(KT):
                            c = (n % 2) * D + k * P
                            last = nc.tensor.transpose(bank[kind, n][:, k * P:(k + 1) * P], xn[:, c:c + P], ident[:, :])
                        last.then_inc(s_xp.sem, 1)
                    if kind == "v":
                        pe.wait_ge(s_xl.sem, s_xl.at(i, 3))
                        for read, value in bank.last_reads(i, (kind, n)):
                            pe.wait_ge(read, value)
                        for t in range(4):
                            for k in range(KT):
                                c = k * GT + t * P
                                last = split3(nc, bank[kind, n][:, t * P:(t + 1) * P], xt_h[:, c:c + P], xt_l[:, c:c + P],
                                              wv_h[:, k * P:(k + 1) * P], wv_l[:, k * P:(k + 1) * P], k == 0, k == KT - 1)
                        last.then_inc(s_vp.sem, 1)
                    if kind == "proj":
                        for read, value in bank.last_reads(i, (kind, n)):
                            pe.wait_ge(read, value)
                        for k in range(KT):
                            c = k * 1024 + (n % 2) * 512 + (n // 2) * P
                            last = split3(nc, bank[kind, n][:, :], wqk_h[:, c:c + P], wqk_l[:, c:c + P],
                                          xt_h[:, k * GT:(k + 1) * GT], xt_l[:, k * GT:(k + 1) * GT], k == 0, k == KT - 1)
                        last.then_inc(s_qp.sem, 1)
                    if kind == "score":
                        u, g = n // 8, n % 8
                        j, ring = g // 2, (n // 2) % 2
                        pe.wait_ge(s_qm.sem, s_qm.at(i, n // 2))
                        pe.wait_ge(s_rl.sem, s_rl.at(i, 2 * j + 1))
                        pe.wait_ge(s_pred.sem, s_pred.two_before(i, n))
                        for t in range(2):
                            for hp in range(2):
                                for b in range(2):
                                    q = ring * 2048 + (t * 2 + b) * 512 + (4 * (g % 2) + 2 * hp) * S
                                    kk = j * GT + (2 * u + t) * P + b * S
                                    last = split3(nc, psS[n % 2][:, COL(t, hp, b):COL(t, hp, b) + S],
                                                  qm_h[:, q:q + P], qm_l[:, q:q + P],
                                                  r16["ka_h"][:, kk:kk + S], r16["ka_l"][:, kk:kk + S], True, True)
                        last.then_inc(s_S.sem, 1)
                    if kind == "turn":
                        pe.wait_ge(s_exp.sem, s_exp.at(i, n))
                        pe.wait_ge(s_pl.sem, s_pl.two_before(i, n))
                        for c in range(4):
                            last = nc.tensor.transpose(psP[n % 2][:, c * P:(c + 1) * P],
                                                       pr[:, (n % 2) * 512 + c * P:(n % 2) * 512 + (c + 1) * P], ident[:, :])
                        last.then_inc(s_T.sem, 1)
                    if kind == "pv":
                        u, g = n // 8, n % 8
                        pe.wait_ge(s_pl.sem, s_pl.at(i, n))
                        pe.wait_ge(s_vl.sem, s_vl.at(i, 0))
                        if g == 0:
                            pe.wait_ge(s_on.sem, s_on.at(i, 2 * u - 1))
                        for t in range(2):
                            for hp in range(2):
                                for b in range(2):
                                    rows = slice(b * S, (b + 1) * S)
                                    o = ((t * G + g) * 2 + hp) * HD_SELF
                                    c = (n % 2) * 512 + (t * 2 + hp) * P
                                    vc = (2 * u + t) * P + g * HD_SELF
                                    last = split3(nc, psO[b][:, o:o + HD_SELF], pt_h[rows, c:c + P], pt_l[rows, c:c + P],
                                                  va_h[rows, vc:vc + HD_SELF], va_l[rows, vc:vc + HD_SELF], True, True)
                        last.then_inc(s_O.sem, 1)
                    if kind == "dense":
                        pe.wait_ge(s_on.sem, s_on.at(i, n // 2 * 2 + 1))
                        for read, value in bank.last_reads(i, ("oT", n)):
                            pe.wait_ge(read, value)
                        src = on[:, (n % 2) * D:(n % 2 + 1) * D].rearrange("p (b g c) -> p b g c", b=2, g=2)
                        for gh in range(2):
                            for b in range(2):
                                dst = bank["oT", n][:, gh * 256:(gh + 1) * 256].rearrange("p (h t) -> p h t", h=2)
                                last = nc.tensor.transpose(dst[:, :, b * S:(b + 1) * S], src[:, b, gh, :], ident[:, :])
                        last.then_inc(s_cp.sem, 1)
                    if kind == "y":
                        pe.wait_ge(s_cl.sem, s_cl.at(i, n))
                        for read, value in bank.last_reads(i, (kind, n)):
                            pe.wait_ge(read, value)
                        for k in range(KT):
                            c = (n % 2) * 512 + k * P
                            last = split3(nc, bank["y", n][:, :], ct_h[:, c:c + P], ct_l[:, c:c + P],
                                          wd_h[:, k * D:(k + 1) * D], wd_l[:, k * D:(k + 1) * D], k == 0, k == KT - 1)
                        last.then_inc(s_Y.sem, 1)

        @block.scalar
        def _(act):
            start(act, s_xh, s_vh, s_sw, s_rh, s_exp, s_ph, s_ch)
            with act.Fori(0, GROUPS) as i:
                for kind, n in steps:
                    if kind == "ln":
                        act.wait_ge(s_xp.sem, s_xp.at(i, n))
                        act.wait_ge(s_qp.sem, s_qp.at(i, -1))
                        dst = xt_h[:, :].rearrange("p (k t) -> p k t", k=KT)[:, :, n * P:(n + 1) * P]
                        nc.scalar.activation(dst, bank[kind, n][:, :].rearrange("p (k t) -> p k t", k=KT),
                                             ACT.Copy).then_inc(s_xh.sem, 1)
                    if kind == "v":
                        act.wait_ge(s_v32.sem, s_v32.at(i, 0))
                        act.wait_ge(s_O.sem, s_O.at(i, -1))
                        nc.scalar.activation(va_h[:, :], v32[:, :], ACT.Copy).then_inc(s_vh.sem, 1)
                    if kind == "proj":
                        act.wait_ge(s_qp.sem, s_qp.at(i, n))
                        act.wait_ge(s_r.sem, s_r.two_before(i, n))
                        o = (n % 2) * GT
                        nc.scalar.activation(sw[0:64, o:o + GT], bank[kind, n][64:128, :], ACT.Copy)
                        nc.scalar.activation(sw[64:128, o:o + GT], bank[kind, n][0:64, :], ACT.Copy).then_inc(s_sw.sem, 1)
                        dst = r16["qa_h" if n % 2 == 0 else "ka_h"]
                        act.wait_ge(s_r.sem, s_r.at(i, n))
                        act.wait_ge(s_S.sem, s_S.at(i, -1))
                        nc.scalar.activation(dst[:, (n // 2) * GT:(n // 2 + 1) * GT], t1[:, o:o + GT],
                                             ACT.Copy).then_inc(s_rh.sem, 1)
                    if kind == "score":
                        act.wait_ge(s_sub.sem, s_sub.at(i, n))
                        o = (n % 2) * 512
                        nc.scalar.activation(pr[:, o:o + 512], pr[:, o:o + 512], ACT.Exp, scale=SCALE_SELF).then_inc(s_exp.sem, 1)
                    if kind == "pv":
                        o = (n % 2) * 512
                        act.wait_ge(s_T.sem, s_T.at(i, n))
                        act.wait_ge(s_O.sem, s_O.two_before(i, n))
                        nc.scalar.activation(pt_h[:, o:o + 512], psP[n % 2][:, :], ACT.Copy).then_inc(s_ph.sem, 1)
                    if kind == "dense":
                        act.wait_ge(s_cp.sem, s_cp.at(i, n))
                        act.wait_ge(s_Y.sem, s_Y.two_before(i, n))
                        c = (n % 2) * 512
                        nc.scalar.activation(ct_h[:, c:c + 512], bank["oT", n][:, :], ACT.Copy).then_inc(s_ch.sem, 1)

        @block.gpsimd
        def _(pool):
            start(pool, s_bd, s_r, s_fill, s_sub)
            with pool.Fori(0, GROUPS) as i:
                for kind, n in steps:
                    if kind == "ln":
                        pool.wait_ge(s_xn.sem, s_xn.at(i, n))
                        settle(pool, m)
                        nc.gpsimd.tensor_tensor(xr(i * 4 + n), xr(i * 4 + n), m["bd_row"][:, :], ALU.add).then_inc(s_bd.sem, 1)
                    if kind == "proj":
                        o = (n % 2) * GT
                        pool.wait_ge(s_t1.sem, s_t1.at(i, n))
                        pool.wait_ge(s_t2.sem, s_t2.at(i, n))
                        nc.gpsimd.tensor_tensor(t1[:, o:o + GT], t1[:, o:o + GT], sw[:, o:o + GT], ALU.add).then_inc(s_r.sem, 1)
                    if kind == "score":
                        o = (n % 2) * 512
                        pool.wait_ge(s_T.sem, s_T.two_before(i, n))
                        pool.wait_ge(s_sum.sem, s_sum.two_before(i, n))
                        settle(pool, m)
                        nc.gpsimd.memset(pr[:, o:o + 512], FILL_SELF).then_inc(s_fill.sem, 1)
                        pool.wait_ge(s_mx.sem, s_mx.at(i, n))
                        v3 = pr[:, o:o + 512].rearrange("p (c k) -> p c k", k=S)
                        mb = mx[:, (n % 2) * 8:(n % 2) * 8 + 8].rearrange("p (c k) -> p c k", k=1).to_broadcast([P, 8, S])
                        nc.gpsimd.tensor_tensor(v3, v3, mb, ALU.subtract).then_inc(s_sub.sem, 1)

        @block.vector
        def _(v):
            start(v, s_xn, s_xl, s_v32, s_vl, s_t1, s_t2, s_rl, s_qm, s_pred, s_mx, s_sum, s_pl, s_ri, s_on, s_cl, s_xr, s_st)
            with v.Fori(0, GROUPS) as i:
                for kind, n in steps:
                    if kind == "ln":
                        v.wait_ge(s_xp.sem, s_xp.two_before(i, n))
                        mcol = mv[:, bass.ds((i * 4 + n) * 2, 1)]
                        rcol = rstd[:, bass.ds(i * 4 + n, 1)]
                        nc.vector.tensor_scalar(xn[:, (n % 2) * D:(n % 2 + 1) * D], xr(i * 4 + n), mcol, rcol,
                                                ALU.subtract, ALU.mult).then_inc(s_xn.sem, 1)
                        v.wait_ge(s_xh.sem, s_xh.at(i, n))
                        hi = xt_h[:, :].rearrange("p (k t) -> p k t", k=KT)[:, :, n * P:(n + 1) * P]
                        lo = xt_l[:, :].rearrange("p (k t) -> p k t", k=KT)[:, :, n * P:(n + 1) * P]
                        nc.vector.tensor_tensor(lo, bank[kind, n][:, :].rearrange("p (k t) -> p k t", k=KT), hi.bitcast(F32),
                                                ALU.subtract).then_inc(s_xl.sem, 1)
                    if kind == "v":
                        v.wait_ge(s_vp.sem, s_vp.at(i, 0))
                        bb = m["bv_row"][:, :].rearrange("p (t c) -> p t c", t=1).to_broadcast([P, 4, P])
                        nc.vector.tensor_tensor(v32[:, :].rearrange("p (t c) -> p t c", t=4),
                                                bank[kind, n][:, :].rearrange("p (t c) -> p t c", t=4), bb,
                                                ALU.add).then_inc(s_v32.sem, 1)
                        v.wait_ge(s_vh.sem, s_vh.at(i, 0))
                        nc.vector.tensor_tensor(va_l[:, :], v32[:, :], va_h[:, :], ALU.subtract).then_inc(s_vl.sem, 1)
                    if kind == "proj":
                        o = (n % 2) * GT
                        j = n // 2
                        bias = (m["q_b"], m["k_b"])[n % 2][:, j:j + 1]
                        bias_s = (m["q_bs"], m["k_bs"])[n % 2][:, j:j + 1]
                        b3 = lambda tab: tab[:, :].rearrange("p (c s) -> p c s", c=1).to_broadcast([P, 8, S])
                        r3 = lambda ap: ap.rearrange("p (c s) -> p c s", s=S)
                        v.wait_ge(s_sw.sem, s_sw.at(i, n))
                        v.wait_ge(s_rl.sem, s_rl.two_before(i, n))
                        nc.vector.scalar_tensor_tensor(r3(t1[:, o:o + GT]), r3(bank[kind, n][:, :]), bias, b3(m["cos_a"]),
                                                       ALU.add, ALU.mult).then_inc(s_t1.sem, 1)
                        nc.vector.scalar_tensor_tensor(r3(sw[:, o:o + GT]), r3(sw[:, o:o + GT]), bias_s, b3(m["sin_a"]),
                                                       ALU.add, ALU.mult).then_inc(s_t2.sem, 1)
                        v.wait_ge(s_rh.sem, s_rh.at(i, n))
                        a, c_ = ("qa_h", "qa_l") if n % 2 == 0 else ("ka_h", "ka_l")
                        jj = slice(j * GT, (j + 1) * GT)
                        nc.vector.tensor_tensor(r16[c_][:, jj], t1[:, o:o + GT], r16[a][:, jj], ALU.subtract).then_inc(s_rl.sem, 1)
                    if kind == "mask":
                        u, j, ring = n // 4, n % 4, n % 2
                        v.wait_ge(s_rl.sem, s_rl.at(i, 2 * j))
                        v.wait_ge(s_S.sem, s_S.at(i, max(2 * n - 3, -1)))
                        for half, qm in (("qa_h", qm_h), ("qa_l", qm_l)):
                            src = r16[half][:, j * GT + u * 256:j * GT + (u + 1) * 256].rearrange("p (c q) -> p c q", q=S)
                            dst = qm[:, ring * 2048:(ring + 1) * 2048].rearrange("p (c h q) -> p c h q", h=8, q=S)
                            for h in range(8):
                                last = nc.vector.tensor_scalar(dst[:, :, h, :], src, m["hmask"][:, h:h + 1], None, ALU.mult)
                        last.then_inc(s_qm.sem, 1)
                    if kind == "score":
                        o = (n % 2) * 512
                        v.wait_ge(s_S.sem, s_S.at(i, n))
                        v.wait_ge(s_fill.sem, s_fill.at(i, n))
                        cm = m["causal"][:, :].rearrange("p (c k) -> p c k", c=1).to_broadcast([P, 8, S])
                        v3 = pr[:, o:o + 512].rearrange("p (c k) -> p c k", k=S)
                        settle(v, m)
                        nc.vector.copy_predicated(v3, cm, psS[n % 2][:, :].rearrange("p (c k) -> p c k", k=S)).then_inc(s_pred.sem, 1)
                        v.wait_ge(s_pred.sem, s_pred.at(i, n))
                        v.wait_ge(s_sub.sem, s_sub.two_before(i, n))
                        nc.vector.tensor_reduce(mx[:, (n % 2) * 8:(n % 2) * 8 + 8], v3, AX_X, ALU.max).then_inc(s_mx.sem, 1)
                    if kind == "turn":
                        u, g = n // 8, n % 8
                        v.wait_ge(s_exp.sem, s_exp.at(i, n))
                        if g == 0:
                            v.wait_ge(s_ri.sem, s_ri.at(i, u - 1))
                        o = (n % 2) * 512
                        dst = sums[:, :].rearrange("p (t g c) -> p t g c", t=2, g=G)[:, :, g, :]
                        nc.vector.tensor_reduce(dst, pr[:, o:o + 512].rearrange("p (t c k) -> p t c k", t=2, k=S), AX_X,
                                                ALU.add).then_inc(s_sum.sem, 1)
                        if g == 7:
                            v.wait_ge(s_sum.sem, s_sum.at(i, n))
                            v.wait_ge(s_on.sem, s_on.at(i, 2 * u - 1))
                            nc.vector.reciprocal(rinv[:, :].rearrange("p (t b c) -> p t c b", t=2, b=2),
                                                 sums[:, :].rearrange("p (t c b) -> p t c b", t=2, b=2)).then_inc(s_ri.sem, 1)
                    if kind == "pv":
                        o = (n % 2) * 512
                        v.wait_ge(s_ph.sem, s_ph.at(i, n))
                        nc.vector.tensor_tensor(pt_l[:, o:o + 512], psP[n % 2][:, :], pt_h[:, o:o + 512],
                                                ALU.subtract).then_inc(s_pl.sem, 1)
                    if kind == "norm":
                        u, b = n // 2, n % 2
                        v.wait_ge(s_O.sem, s_O.at(i, 8 * u + 7))
                        v.wait_ge(s_ri.sem, s_ri.at(i, u))
                        v.wait_ge(s_cp.sem, s_cp.at(i, 2 * u - 1))
                        rb = rinv[:, :].rearrange("p (t b c x) -> p t b c x", t=2, b=2, x=1)[:, :, b, :, :].to_broadcast([P, 2, 16, HD_SELF])
                        dst = on[:, :].rearrange("p (t b c d) -> p t b c d", t=2, b=2, d=HD_SELF)[:, :, b, :, :]
                        nc.vector.tensor_tensor(dst, psO[b][:, :].rearrange("p (t c d) -> p t c d", t=2, d=HD_SELF), rb,
                                                ALU.mult).then_inc(s_on.sem, 1)
                    if kind == "dense":
                        c = (n % 2) * 512
                        v.wait_ge(s_ch.sem, s_ch.at(i, n))
                        nc.vector.tensor_tensor(ct_l[:, c:c + 512], bank["oT", n][:, :], ct_h[:, c:c + 512].bitcast(F32),
                                                ALU.subtract).then_inc(s_cl.sem, 1)
                    if kind == "y":
                        v.wait_ge(s_Y.sem, s_Y.at(i, n))
                        v.wait_ge(s_bd.sem, s_bd.at(i, n))
                        nc.vector.tensor_tensor(xr(i * 4 + n), bank["y", n][:, :], xr(i * 4 + n), ALU.add).then_inc(s_xr.sem, 1)
                        v.wait_ge(s_xr.sem, s_xr.at(i, n))
                        nc.vector.bn_stats(stats[:, bass.ds((i * 4 + n) * 6, 6)], xr(i * 4 + n)).then_inc(s_st.sem, 1)
            v.wait_ge(s_st.sem, s_st.at(0, TILES - 1))


def cross_keys_values(nc, at, io, m):
    WR, XT, ER, F0 = m["WR"], m["XT"], m["ER"], m["F0"]
    cosx, sinx, ident, kscr, vscr = m["cosx"], m["sinx"], m["ident"], m["kscr"], m["vscr"]
    wk_h = at("wkx_h", WR, [G * KT * P], F32R)
    wk_l = at("wkx_l", WR + 16, [G * KT * P], F32R)
    wv_h = at("wvx_h", ER, [KT * 1024], F32R)
    wv_l = at("wvx_l", ER + 16, [KT * 1024], F32R)
    ct_h = at("ctx_h", XT, [KT * GT], F32R)
    ct_l = at("ctx_l", XT + 8, [KT * GT], F32R)
    cin = at("ctx_in", F0, [4 * D], F32)
    RING = 4
    stage = at("stage_kv", F0 + 8, [RING * 512], F32)
    t1 = at("t1k", F0 + 16, [2 * GT], F32)
    sw = at("swk", F0 + 20, [2 * GT], F32)
    ks = at("k_out", F0 + 24, [2 * 2 * GT], F16)
    vs = at("v_out", F0 + 28, [2 * 512], F32)
    with ExitStack() as ctx:
        ps = [ctx.enter_context(nc.psum_tensor(f"psK{n}", [P, 512], F32)) for n in range(4)]

        def sig(name, per, step=1):
            return Signal(nc, ctx, name, per, step, base=1)

        w_in = [sig(f"k_w_in{r}", 0, 16) for r in range(RING)]
        w_hi, w_lo = sig("k_w_hi", 0), sig("k_w_lo", 0)
        c_in = [sig(f"ctx_in{t}", 1, 16) for t in range(4)]
        s_cp, s_ch, s_cl = sig("k_ctxT_psum", 4), sig("k_ctxT_hi", 4), sig("k_ctxT_lo", 4)
        s_kp, s_sw, s_t1, s_t2, s_r = sig("k_psum", 8), sig("k_swapped", 8), sig("k_cos_term", 8), sig("k_sin_term", 8), sig("k_roped", 8)
        s_rh, s_rl = sig("k_hi", 8), sig("k_lo", 8)
        s_ko = [sig(f"k_stored{r}", 4, 16) for r in range(2)]
        s_vp, s_v = sig("v_psum", 8), sig("v_sbuf", 8)
        s_vo = [sig(f"v_stored{r}", 4, 16) for r in range(2)]
        block = ctx.enter_context(nc.Block())

        steps = [("ct", t) for t in range(4)]
        for n in range(8):
            steps += [("k", n), ("v", n)]
        order = steps

        def readers(use):
            kind, n = use
            return {"ct": [(s_cl, n)], "k": [(s_t1, n)], "v": [(s_v, n)]}[kind]

        bank = Banks(ps, order, readers)
        chunks = []
        for g in range(G):
            src = io["wk"].rearrange("(k p) n -> p k n", p=P)[:, :, g * P:(g + 1) * P]
            chunks.append((src, KT, wk_h[:, g * 512:(g + 1) * 512], wk_l[:, g * 512:(g + 1) * 512]))
        for c in range(2 * KT):
            src = io["wv"][(c // 2) * P:(c // 2 + 1) * P, (c % 2) * 512:(c % 2 + 1) * 512]
            chunks.append((src, 1, wv_h[:, c * 512:(c + 1) * 512], wv_l[:, c * 512:(c + 1) * 512]))
        st = lambda c: stage[:, (c % RING) * 512:(c % RING + 1) * 512]

        @block.sync
        def _(sp):
            start(sp, *c_in, *w_in, *s_ko, *s_vo)
            def load_ctx(tile, t):
                sp.dma_start(cin[:, t * D:(t + 1) * D], io["ctx"][bass.ds(tile * P, P), :]).then_inc(c_in[t].sem, 16)

            for t in range(4):
                load_ctx(t, t)
            for c, (src, a, hi, lo) in enumerate(chunks):
                sp.wait_ge(w_lo.sem, w_lo.at(0, c - RING))
                dst = st(c) if a == 1 else st(c).rearrange("p (a b) -> p a b", a=a)
                sp.dma_start(dst, src).then_inc(w_in[c % RING].sem, 16)

            def turn(i, more):
                for kind, n in steps:
                    if kind == "ct" and more:
                        sp.wait_ge(s_cp.sem, s_cp.at(i, n))
                        load_ctx((i + 1) * 4 + n, n)
                    if kind == "k":
                        sp.wait_ge(s_rl.sem, s_rl.at(i, n))
                        sp.dma_start(kscr[n][:, :, bass.ds(i * GT, GT)],
                                     ks[:, (n % 2) * 2 * GT:(n % 2 + 1) * 2 * GT].rearrange("p (a t) -> p a t", a=2)
                                     ).then_inc(s_ko[n % 2].sem, 16)
                    if kind == "v":
                        sp.wait_ge(s_v.sem, s_v.at(i, n))
                        sp.dma_start(vscr[bass.ds(i * GT + (n // 2) * P, P), (n % 2) * 512:(n % 2 + 1) * 512],
                                     vs[:, (n % 2) * 512:(n % 2 + 1) * 512]).then_inc(s_vo[n % 2].sem, 16)

            with sp.Fori(0, GROUPS - 1) as i:
                turn(i, True)
            turn(GROUPS - 1, False)
            for r in range(2):
                sp.wait_ge(s_ko[r].sem, s_ko[r].at(GROUPS, -1))
                sp.wait_ge(s_vo[r].sem, s_vo[r].at(GROUPS, -1))

        @block.gpsimd
        def _(pool):
            start(pool, s_t2)
            with pool.Fori(0, GROUPS) as i:
                for kind, n in steps:
                    if kind == "k":
                        o = (n % 2) * GT
                        pool.wait_ge(s_sw.sem, s_sw.at(i, n))
                        settle(pool, m)
                        nc.gpsimd.tensor_tensor(sw[:, o:o + GT], sw[:, o:o + GT], sinx[:, bass.ds(i * GT, GT)],
                                                ALU.mult).then_inc(s_t2.sem, 1)

        @block.scalar
        def _(act):
            start(act, w_hi, s_ch, s_sw, s_rh, s_v)
            for c, (src, a, hi, lo) in enumerate(chunks):
                act.wait_ge(w_in[c % RING].sem, w_in[c % RING].at(0, c // RING))
                nc.scalar.activation(hi, st(c), ACT.Copy).then_inc(w_hi.sem, 1)
            with act.Fori(0, GROUPS) as i:
                for kind, n in steps:
                    if kind == "ct":
                        act.wait_ge(s_cp.sem, s_cp.at(i, n))
                        act.wait_ge(s_vp.sem, s_vp.at(i, -1))
                        dst = ct_h[:, :].rearrange("p (k t) -> p k t", k=KT)[:, :, n * P:(n + 1) * P]
                        nc.scalar.activation(dst, bank[kind, n][:, :].rearrange("p (k t) -> p k t", k=KT),
                                             ACT.Copy).then_inc(s_ch.sem, 1)
                    if kind == "k":
                        o = (n % 2) * GT
                        act.wait_ge(s_kp.sem, s_kp.at(i, n))
                        act.wait_ge(s_r.sem, s_r.two_before(i, n))
                        nc.scalar.activation(sw[0:64, o:o + GT], bank[kind, n][64:128, :], ACT.Copy)
                        nc.scalar.activation(sw[64:128, o:o + GT], bank[kind, n][0:64, :], ACT.Copy).then_inc(s_sw.sem, 1)
                    if kind == "v":
                        act.wait_ge(s_vp.sem, s_vp.at(i, n))
                        act.wait_ge(s_vo[n % 2].sem, s_vo[n % 2].at(i, n // 2 - 1))
                        nc.scalar.activation(vs[:, (n % 2) * 512:(n % 2 + 1) * 512], bank[kind, n][:, :],
                                             ACT.Copy).then_inc(s_v.sem, 1)
                        act.wait_ge(s_r.sem, s_r.at(i, n))
                        act.wait_ge(s_ko[n % 2].sem, s_ko[n % 2].at(i, n // 2 - 1))
                        nc.scalar.activation(ks[:, (n % 2) * 2 * GT:(n % 2) * 2 * GT + GT], t1[:, (n % 2) * GT:(n % 2 + 1) * GT],
                                             ACT.Copy).then_inc(s_rh.sem, 1)

        @block.vector
        def _(v):
            start(v, w_lo, s_cl, s_t1, s_r, s_rl)
            for c, (src, a, hi, lo) in enumerate(chunks):
                v.wait_ge(w_hi.sem, w_hi.at(0, c))
                nc.vector.tensor_tensor(lo, st(c), hi.bitcast(F32), ALU.subtract).then_inc(w_lo.sem, 1)
            with v.Fori(0, GROUPS) as i:
                for kind, n in steps:
                    if kind == "ct":
                        v.wait_ge(s_ch.sem, s_ch.at(i, n))
                        hi = ct_h[:, :].rearrange("p (k t) -> p k t", k=KT)[:, :, n * P:(n + 1) * P]
                        lo = ct_l[:, :].rearrange("p (k t) -> p k t", k=KT)[:, :, n * P:(n + 1) * P]
                        nc.vector.tensor_tensor(lo, bank[kind, n][:, :].rearrange("p (k t) -> p k t", k=KT), hi.bitcast(F32),
                                                ALU.subtract).then_inc(s_cl.sem, 1)
                    if kind == "k":
                        o = (n % 2) * GT
                        v.wait_ge(s_sw.sem, s_sw.at(i, n))
                        v.wait_ge(s_rl.sem, s_rl.two_before(i, n))
                        nc.vector.tensor_tensor(t1[:, o:o + GT], bank[kind, n][:, :], cosx[:, bass.ds(i * GT, GT)],
                                                ALU.mult).then_inc(s_t1.sem, 1)
                    if kind == "v":
                        o = (n % 2) * GT
                        v.wait_ge(s_t2.sem, s_t2.at(i, n))
                        v.wait_ge(s_t1.sem, s_t1.at(i, n))
                        nc.vector.tensor_tensor(t1[:, o:o + GT], t1[:, o:o + GT], sw[:, o:o + GT], ALU.add).then_inc(s_r.sem, 1)
                        v.wait_ge(s_rh.sem, s_rh.at(i, n))
                        v.wait_ge(s_r.sem, s_r.at(i, n))
                        nc.vector.tensor_tensor(ks[:, 2 * o + GT:2 * o + 2 * GT], t1[:, o:o + GT], ks[:, 2 * o:2 * o + GT],
                                                ALU.subtract).then_inc(s_rl.sem, 1)

        @block.tensor
        def _(pe):
            start(pe, s_cp, s_kp, s_vp)
            with pe.Fori(0, GROUPS) as i:
                for kind, n in steps:
                    for read, value in bank.last_reads(i, (kind, n)):
                        pe.wait_ge(read, value)
                    if kind == "ct":
                        pe.wait_ge(c_in[n].sem, c_in[n].at(i, 0))
                        for k in range(KT):
                            last = nc.tensor.transpose(bank[kind, n][:, k * P:(k + 1) * P],
                                                       cin[:, n * D + k * P:n * D + (k + 1) * P], ident[:, :])
                        last.then_inc(s_cp.sem, 1)
                    if kind == "k":
                        pe.wait_ge(w_lo.sem, w_lo.at(0, len(chunks) - 1))
                        pe.wait_ge(s_cl.sem, s_cl.at(i, 3))
                        for k in range(KT):
                            c = (n * KT + k) * P
                            last = split3(nc, bank[kind, n][:, :], wk_h[:, c:c + P], wk_l[:, c:c + P],
                                          ct_h[:, k * GT:(k + 1) * GT], ct_l[:, k * GT:(k + 1) * GT], k == 0, k == KT - 1)
                        last.then_inc(s_kp.sem, 1)
                    if kind == "v":
                        t, h = n // 2, n % 2
                        for k in range(KT):
                            c, w = k * GT + t * P, k * 1024 + h * 512
                            last = split3(nc, bank[kind, n][:, :], ct_h[:, c:c + P], ct_l[:, c:c + P],
                                          wv_h[:, w:w + 512], wv_l[:, w:w + 512], k == 0, k == KT - 1)
                        last.then_inc(s_vp.sem, 1)


def normalise_and_transpose(nc, ctx, m, xt_h, xt_l, xn, banks, tag):
    mv, rstd, stats, ident, xr = m["mv"], m["rstd"], m["stats"], m["ident"], m["xr"]
    names = ("var", "sqrt", "rstd", "xn", "xnT_psum", "xT_hi", "xT_lo")
    s_var, s_sq, s_rs, s_xn, s_xp, s_xh, s_xl = (Signal(nc, ctx, f"{tag}_{n}", 4) for n in names)
    R = len(banks)

    def halves(dst, n, i):
        return dst[:, :].rearrange("p (k t) -> p k t", k=KT)[:, :, n * P:(n + 1) * P]

    def vector(v):
        for t in range(TILES):
            nc.vector.bn_aggr(mv[:, 2 * t:2 * t + 2], stats[:, 6 * t:6 * t + 6]).then_inc(s_var.sem, 1)
        v.wait_ge(s_var.sem, TILES)
        nc.vector.tensor_scalar_add(rstd[:, :], mv[:, 1:2 * TILES:2], EPS).then_inc(s_var.sem, 1)
        v.wait_ge(s_sq.sem, 1)
        nc.vector.reciprocal(rstd[:, :], rstd[:, :]).then_inc(s_rs.sem, 1)
        v.wait_ge(s_rs.sem, 1)
        for n in range(TILES + 1):
            if n < TILES:
                if n >= 2:
                    v.wait_ge(s_xp.sem, s_xp.at(0, n - 2))
                nc.vector.tensor_scalar(xn[:, (n % 2) * D:(n % 2 + 1) * D], xr(n), mv[:, 2 * n:2 * n + 1], rstd[:, n:n + 1],
                                        ALU.subtract, ALU.mult).then_inc(s_xn.sem, 1)
            if n >= 1:
                v.wait_ge(s_xh.sem, s_xh.at(0, n - 1))
                nc.vector.tensor_tensor(halves(xt_l, n - 1, 0), banks[(n - 1) % R][:, :].rearrange("p (k t) -> p k t", k=KT),
                                        halves(xt_h, n - 1, 0).bitcast(F32), ALU.subtract).then_inc(s_xl.sem, 1)

    def scalar(act):
        act.wait_ge(s_var.sem, TILES + 1)
        nc.scalar.activation(rstd[:, :], rstd[:, :], ACT.Sqrt).then_inc(s_sq.sem, 1)
        for n in range(TILES):
            act.wait_ge(s_xp.sem, s_xp.at(0, n))
            nc.scalar.activation(halves(xt_h, n, 0), banks[n % R][:, :].rearrange("p (k t) -> p k t", k=KT),
                                 ACT.Copy).then_inc(s_xh.sem, 1)

    def tensor(pe):
        for n in range(TILES):
            pe.wait_ge(s_xn.sem, s_xn.at(0, n))
            if n >= R:
                pe.wait_ge(s_xl.sem, s_xl.at(0, n - R))
            for k in range(KT):
                c = (n % 2) * D + k * P
                last = nc.tensor.transpose(banks[n % R][:, k * P:(k + 1) * P], xn[:, c:c + P], ident[:, :])
            last.then_inc(s_xp.sem, 1)
        pe.wait_ge(s_xl.sem, s_xl.at(0, TILES - 1))

    return vector, scalar, tensor


def cross_attention(nc, at, io, m):
    WR, XT, ER, F0 = m["WR"], m["XT"], m["ER"], m["F0"]
    cosx, sinx, ident, kscr, vscr, mask8 = (m[n] for n in ("cosx", "sinx", "ident", "kscr", "vscr", "mask8"))
    xr, stats = m["xr"], m["stats"]
    xt_h = at("xtx_h", XT, [KT * T], F32R)
    xt_l = at("xtx_l", XT + 32, [KT * T], F32R)
    w1_h, w1_l = at("wq_h", WR, [KT * 512], F32R), at("wq_l", WR + 8, [KT * 512], F32R)
    w2_h, w2_l = at("wo_h", WR + 16, [HPG * D], F32R), at("wo_l", WR + 24, [HPG * D], F32R)
    ot_h, ot_l = at("ot_h", ER, [GROUP * HPG * P], F32R), at("ot_l", ER + 8, [GROUP * HPG * P], F32R)
    q_h, q_l = at("q_h", ER + 16, [2 * HPG * GT], F16), at("q_l", ER + 24, [2 * HPG * GT], F16)
    RING = 4
    stage = at("stage_x", F0, [RING * 512], F32)
    t1, sw = at("t1x", F0 + 8, [2 * GT], F32), at("swx", F0 + 12, [2 * GT], F32)
    kt = at("k_x", F0 + 16, [2 * 2 * GT], F16)
    vt = at("v_x", F0 + 20, [2 * GROUP * HD_X], F32)
    pr = at("pr_x", F0 + 24, [2 * 512], F32)
    pt = at("pt_x", F0 + 28, [2 * 512], F32)
    xn = at("xn_x", F0 + 32, [2 * D], F32)
    sums, rinv, mx = (at(f"{n}_x", F0 + 36 + 0.0625 * i, [16], F32) for i, n in enumerate(("sums", "rinv", "mx")))

    with ExitStack() as ctx:
        ps = [ctx.enter_context(nc.psum_tensor(f"psX{n}", [P, 512], F32)) for n in range(8)]
        psQ, psS, psP, psO, psY = ps[0:2], ps[2], ps[3], ps[4:6], ps[6:8]

        def sig(name, per, step=1):
            return Signal(nc, ctx, name, per, step, base=1)

        w_in = [sig(f"x_w_in{r}", 2, 16) for r in range(RING)]
        w_hi, w_lo = sig("x_w_hi", 8), sig("x_w_lo", 8)
        kv_in = [sig(f"x_kv_in{r}", 4, 16) for r in range(2)]
        s_qp, s_sw, s_t1, s_t2, s_r = (sig(f"x_{n}", 16) for n in ("q_psum", "q_swapped", "q_cos_term", "q_sin_term", "q_roped"))
        s_rh, s_rl = sig("x_q_hi", 16), sig("x_q_lo", 16)
        s_S, s_fill, s_pred, s_mx, s_sub, s_exp = (sig(f"x_{n}", 8) for n in ("scores", "filled", "kept", "max", "less_max", "exp"))
        s_sum, s_ri, s_nm, s_T, s_pt, s_O = (sig(f"x_{n}", 8) for n in ("sum", "inv_sum", "normal", "pT_psum", "pT", "oT_psum"))
        s_oh, s_ol = sig("x_oT_hi", 8), sig("x_oT_lo", 8)
        s_Y, s_xr, s_st = sig("x_out_psum", 16), sig("x_residual", 16), sig("x_stats", 16)
        ln_v, ln_a, ln_p = normalise_and_transpose(nc, ctx, m, xt_h, xt_l, xn, psQ + [psS, psP], "x_ln")
        block = ctx.enter_context(nc.Block())

        def section(tg, more):
            nxt = [("q", tg + 1, h) for h in range(HPG)]
            rope = [("rope", tg + 1, h) for h in range(HPG)]
            if tg == GROUPS - 1 and not more:
                nxt, rope = [[]] * 4, [[]] * 4
            out = []
            if tg == GROUPS - 1 and more:
                out.append(("w1", 0, 0))
            out += [("S", tg, 0), nxt[0], ("S", tg, 1), ("N", tg, 0), rope[0]]
            if tg == 0:
                out.append(("w2", 0, 0))
            out += [nxt[1], ("T", tg, 0), ("N", tg, 1), rope[1], nxt[2], ("T", tg, 1), ("PV", tg, 0), rope[2], nxt[3],
                    ("PV", tg, 1), rope[3]]
            out += [("Y", tg, t) for t in range(GROUP)]
            return [s for s in out if s]

        def program(eng, step, prologue):
            prologue()
            for h in range(HPG):
                step(-1, "q", GROUPS, h, True)
                step(-1, "rope", GROUPS, h, True)

            def turn(i, more):
                for tg in range(GROUPS):
                    for kind, g_, n in section(tg, more):
                        step(i, kind, g_, n, more)

            with eng.Fori(0, G - 1) as i:
                turn(i, True)
            turn(G - 1, False)

        def q_event(i, tg, h):
            return (i + 1, h) if tg == GROUPS else (i, tg * HPG + h)

        @block.sync
        def _(sp):
            start(sp, *w_in, *kv_in)
            def load_w1(g, c):
                sp.dma_start(stage[:, c * 512:(c + 1) * 512], io["wq"][c * P:(c + 1) * P, bass.ds(g * 512, 512)]).then_inc(w_in[c].sem, 16)

            def load_w2(g, c):
                sp.dma_start(stage[:, c * 512:(c + 1) * 512], io["wo"][bass.ds(g * 512 + c * P, P), :]).then_inc(w_in[c].sem, 16)

            def load_kv(g, tg):
                r = tg % 2
                sp.dma_start(kt[:, r * 2 * GT:(r + 1) * 2 * GT].rearrange("p (a t) -> p a t", a=2),
                             kscr[bass.ds(g, 1), :, :, tg * GT:(tg + 1) * GT].rearrange("g p a t -> (g p) a t")
                             ).then_inc(kv_in[r].sem, 16)
                sp.dma_start(vt[:, r * 512:(r + 1) * 512].rearrange("p (t d) -> p t d", t=GROUP),
                             vscr[tg * GT:(tg + 1) * GT, bass.ds(g * HD_X, HD_X)].rearrange("(t p) d -> p t d", p=P)
                             ).then_inc(kv_in[r].sem, 16)

            for c in range(RING):
                load_w1(0, c)
            load_kv(0, 0)

            def turn(i, more):
                for tg in range(GROUPS):
                    if tg == 0:
                        for c in range(RING):
                            sp.wait_ge(w_lo.sem, w_lo.at(i, c))
                            load_w2(i, c)
                    if tg == 2 and more:
                        for c in range(RING):
                            sp.wait_ge(w_lo.sem, w_lo.at(i, 4 + c))
                            load_w1(i + 1, c)
                    if tg < GROUPS - 1 or more:
                        sp.wait_ge(s_O.sem, s_O.at(i, 2 * tg - 1))
                        if tg < GROUPS - 1:
                            load_kv(i, tg + 1)
                        else:
                            load_kv(i + 1, 0)

            with sp.Fori(0, G - 1) as i:
                turn(i, True)
            turn(G - 1, False)

        @block.tensor
        def _(pe):
            start(pe, s_qp, s_S, s_T, s_O, s_Y)
            def step(i, kind, tg, n, more):
                if kind == "q":
                    j, e = q_event(i, tg, n)
                    if tg == GROUPS:
                        pe.wait_ge(w_lo.sem, w_lo.at(j, 3))
                    pe.wait_ge(s_t1.sem, s_t1.at(j, e - 2))
                    for k in range(KT):
                        c, w = k * T + (tg % GROUPS) * GT, k * 512 + n * P
                        last = split3(nc, psQ[n % 2][:, :], w1_h[:, w:w + P], w1_l[:, w:w + P],
                                      xt_h[:, c:c + GT], xt_l[:, c:c + GT], k == 0, k == KT - 1)
                    last.then_inc(s_qp.sem, 1)
                if kind == "S":
                    u = 2 * tg + n
                    if n == 0:
                        pe.wait_ge(s_rl.sem, s_rl.at(i, tg * HPG + 3))
                        pe.wait_ge(kv_in[tg % 2].sem, kv_in[tg % 2].at(i, 2 * (tg // 2) + 1))
                    pe.wait_ge(s_pred.sem, s_pred.at(i, u - 1))
                    for t in range(2):
                        for hp in range(2):
                            for b in range(2):
                                tb = (2 * n + t) * 2 + b
                                q = (tg % 2) * 2048 + tb * 256 + hp * P
                                c, o = (tg % 2) * 2 * GT + tb * S, ((t * 2 + hp) * 2 + b) * S
                                last = split3(nc, psS[:, o:o + S], q_h[:, q:q + P], q_l[:, q:q + P],
                                              kt[:, c:c + S], kt[:, c + GT:c + GT + S], True, True)
                    last.then_inc(s_S.sem, 1)
                if kind == "T":
                    u = 2 * tg + n
                    pe.wait_ge(s_nm.sem, s_nm.at(i, u))
                    pe.wait_ge(s_pt.sem, s_pt.at(i, u - 1))
                    for c in range(4):
                        last = nc.tensor.transpose(psP[:, c * P:(c + 1) * P],
                                                   pr[:, n * 512 + c * P:n * 512 + (c + 1) * P], ident[:, :])
                    last.then_inc(s_T.sem, 1)
                if kind == "PV":
                    u = 2 * tg + n
                    pe.wait_ge(s_pt.sem, s_pt.at(i, u))
                    pe.wait_ge(s_ol.sem, s_ol.at(i, u - 1))
                    for b in range(2):
                        for t in range(2):
                            rows = slice(b * S, (b + 1) * S)
                            vc = (tg % 2) * 512 + (2 * n + t) * HD_X
                            last = nc.tensor.matmul(psO[b][:, t * 256:(t + 1) * 256], vt[rows, vc:vc + HD_X],
                                                    pt[rows, n * 512 + t * 256:n * 512 + (t + 1) * 256], start=True, stop=True)
                    last.then_inc(s_O.sem, 1)
                if kind == "Y":
                    y = tg * 4 + n
                    pe.wait_ge(s_ol.sem, s_ol.at(i, 2 * tg + n // 2))
                    if y == 0:
                        pe.wait_ge(w_lo.sem, w_lo.at(i, 7))
                    pe.wait_ge(s_xr.sem, s_xr.at(i, max(y - 2, -1)))
                    for h in range(HPG):
                        c = (n * HPG + h) * P
                        last = split3(nc, psY[n % 2][:, :], ot_h[:, c:c + P], ot_l[:, c:c + P],
                                      w2_h[:, h * D:(h + 1) * D], w2_l[:, h * D:(h + 1) * D], h == 0, h == HPG - 1)
                    last.then_inc(s_Y.sem, 1)

            program(pe, step, lambda: ln_p(pe))

        def split_hi(act, turn, load, dst):
            for c in range(RING):
                act.wait_ge(w_in[c].sem, w_in[c].at(turn, load))
                nc.scalar.activation(dst[:, c * 512:(c + 1) * 512], stage[:, c * 512:(c + 1) * 512], ACT.Copy).then_inc(w_hi.sem, 1)

        def split_lo(v, turn, first, hi, lo):
            for c in range(RING):
                v.wait_ge(w_hi.sem, w_hi.at(turn, first + c))
                sl = slice(c * 512, (c + 1) * 512)
                nc.vector.tensor_tensor(lo[:, sl], stage[:, sl], hi[:, sl].bitcast(F32), ALU.subtract).then_inc(w_lo.sem, 1)

        @block.scalar
        def _(act):
            start(act, w_hi, s_sw, s_rh, s_exp, s_pt, s_oh)
            def step(i, kind, tg, n, more):
                if kind == "w1":
                    act.wait_ge(s_qp.sem, s_qp.at(i, 15))
                    split_hi(act, i, 2, w1_h)
                if kind == "w2":
                    act.wait_ge(s_Y.sem, s_Y.at(i, -1))
                    split_hi(act, i, 1, w2_h)
                if kind == "q":
                    j, e = q_event(i, tg, n)
                    o = (n % 2) * GT
                    act.wait_ge(s_qp.sem, s_qp.at(j, e))
                    act.wait_ge(s_r.sem, s_r.at(j, e - 2))
                    nc.scalar.activation(sw[0:64, o:o + GT], psQ[n % 2][64:128, :], ACT.Copy)
                    nc.scalar.activation(sw[64:128, o:o + GT], psQ[n % 2][0:64, :], ACT.Copy).then_inc(s_sw.sem, 1)
                if kind == "rope":
                    j, e = q_event(i, tg, n)
                    act.wait_ge(s_r.sem, s_r.at(j, e))
                    if not (type(i) is int and i < 0):
                        act.wait_ge(s_S.sem, s_S.at(i, 2 * (tg - 1) - 1))
                    dst = q_h[:, (tg % 2) * 2048:(tg % 2 + 1) * 2048].rearrange("p (c h q) -> p c h q", h=HPG, q=S)
                    nc.scalar.activation(dst[:, :, n, :], t1[:, (n % 2) * GT:(n % 2 + 1) * GT].rearrange("p (c q) -> p c q", q=S),
                                         ACT.Copy).then_inc(s_rh.sem, 1)
                if kind == "S":
                    act.wait_ge(s_sub.sem, s_sub.at(i, 2 * tg + n))
                    nc.scalar.activation(pr[:, n * 512:(n + 1) * 512], pr[:, n * 512:(n + 1) * 512], ACT.Exp,
                                         scale=SCALE_X).then_inc(s_exp.sem, 1)
                if kind == "T":
                    u = 2 * tg + n
                    act.wait_ge(s_T.sem, s_T.at(i, u))
                    act.wait_ge(s_O.sem, s_O.at(i, max(u - 2, -1)))
                    nc.scalar.activation(pt[:, n * 512:(n + 1) * 512], psP[:, :], ACT.Copy).then_inc(s_pt.sem, 1)
                if kind == "PV":
                    u = 2 * tg + n
                    act.wait_ge(s_O.sem, s_O.at(i, u))
                    act.wait_ge(s_Y.sem, s_Y.at(i, 4 * tg - 1))
                    for b in range(2):
                        dst = ot_h[:, n * 1024:(n + 1) * 1024].rearrange("p (c q) -> p c q", q=P)[:, :, b * S:(b + 1) * S]
                        last = nc.scalar.activation(dst, psO[b][:, :].rearrange("p (c q) -> p c q", q=S), ACT.Copy)
                    last.then_inc(s_oh.sem, 1)

            def prologue():
                ln_a(act)
                split_hi(act, 0, 0, w1_h)

            program(act, step, prologue)

        @block.gpsimd
        def _(pool):
            start(pool, s_t2, s_fill, s_sub)
            def step(i, kind, tg, n, more):
                if kind == "q":
                    j, e = q_event(i, tg, n)
                    o = (n % 2) * GT
                    c = (tg % GROUPS) * GT
                    pool.wait_ge(s_sw.sem, s_sw.at(j, e))
                    nc.gpsimd.tensor_tensor(sw[:, o:o + GT], sw[:, o:o + GT], sinx[:, c:c + GT], ALU.mult).then_inc(s_t2.sem, 1)
                if kind == "S":
                    u = 2 * tg + n
                    pool.wait_ge(s_T.sem, s_T.at(i, max(u - 2, -1)))
                    settle(pool, m)
                    nc.gpsimd.memset(pr[:, n * 512:(n + 1) * 512], FILL_X).then_inc(s_fill.sem, 1)
                    pool.wait_ge(s_mx.sem, s_mx.at(i, u))
                    v3 = pr[:, n * 512:(n + 1) * 512].rearrange("p (c k) -> p c k", k=S)
                    mb = mx[:, n * 8:n * 8 + 8].rearrange("p (c k) -> p c k", k=1).to_broadcast([P, 8, S])
                    nc.gpsimd.tensor_tensor(v3, v3, mb, ALU.subtract).then_inc(s_sub.sem, 1)

            program(pool, step, lambda: None)

        @block.vector
        def _(v):
            start(v, w_lo, s_t1, s_r, s_rl, s_pred, s_mx, s_sum, s_ri, s_nm, s_ol, s_xr, s_st)
            def step(i, kind, tg, n, more):
                if kind == "w1":
                    split_lo(v, i, 8, w1_h, w1_l)
                if kind == "w2":
                    split_lo(v, i, 4, w2_h, w2_l)
                if kind == "q":
                    j, e = q_event(i, tg, n)
                    o, c = (n % 2) * GT, (tg % GROUPS) * GT
                    v.wait_ge(s_sw.sem, s_sw.at(j, e))
                    v.wait_ge(s_rl.sem, s_rl.at(j, e - 2))
                    nc.vector.tensor_tensor(t1[:, o:o + GT], psQ[n % 2][:, :], cosx[:, c:c + GT], ALU.mult).then_inc(s_t1.sem, 1)
                if kind == "rope":
                    j, e = q_event(i, tg, n)
                    o = (n % 2) * GT
                    v.wait_ge(s_t2.sem, s_t2.at(j, e))
                    v.wait_ge(s_t1.sem, s_t1.at(j, e))
                    nc.vector.tensor_tensor(t1[:, o:o + GT], t1[:, o:o + GT], sw[:, o:o + GT], ALU.add).then_inc(s_r.sem, 1)
                    sl = slice((tg % 2) * 2048, (tg % 2 + 1) * 2048)
                    hi = q_h[:, sl].rearrange("p (c h q) -> p c h q", h=HPG, q=S)[:, :, n, :]
                    lo = q_l[:, sl].rearrange("p (c h q) -> p c h q", h=HPG, q=S)[:, :, n, :]
                    v.wait_ge(s_rh.sem, s_rh.at(j, e))
                    v.wait_ge(s_r.sem, s_r.at(j, e))
                    nc.vector.tensor_tensor(lo, t1[:, o:o + GT].rearrange("p (c q) -> p c q", q=S), hi,
                                            ALU.subtract).then_inc(s_rl.sem, 1)
                if kind == "S":
                    u = 2 * tg + n
                    c = (tg * 8 + n * 4) * S
                    mk = mask8[:, c:c + 256].rearrange("p (t x c) -> p t x c", t=2, x=1).to_broadcast([P, 2, 2, P])
                    p4 = lambda ap: ap.rearrange("p (t x c) -> p t x c", t=2, x=2)
                    v.wait_ge(s_S.sem, s_S.at(i, u))
                    v.wait_ge(s_fill.sem, s_fill.at(i, u))
                    settle(v, m)
                    nc.vector.copy_predicated(p4(pr[:, n * 512:(n + 1) * 512]), mk, p4(psS[:, :])).then_inc(s_pred.sem, 1)
                    v.wait_ge(s_pred.sem, s_pred.at(i, u))
                    v.wait_ge(s_sub.sem, s_sub.at(i, max(u - 2, -1)))
                    nc.vector.tensor_reduce(mx[:, n * 8:n * 8 + 8], pr[:, n * 512:(n + 1) * 512].rearrange("p (c k) -> p c k", k=S),
                                            AX_X, ALU.max).then_inc(s_mx.sem, 1)
                if kind == "N":
                    u = 2 * tg + n
                    v3 = pr[:, n * 512:(n + 1) * 512].rearrange("p (c k) -> p c k", k=S)
                    v.wait_ge(s_exp.sem, s_exp.at(i, u))
                    nc.vector.tensor_reduce(sums[:, n * 8:n * 8 + 8], v3, AX_X, ALU.add).then_inc(s_sum.sem, 1)
                    v.wait_ge(s_sum.sem, s_sum.at(i, u))
                    nc.vector.reciprocal(rinv[:, n * 8:n * 8 + 8], sums[:, n * 8:n * 8 + 8]).then_inc(s_ri.sem, 1)
                    v.wait_ge(s_ri.sem, s_ri.at(i, u))
                    rb = rinv[:, n * 8:n * 8 + 8].rearrange("p (c k) -> p c k", k=1).to_broadcast([P, 8, S])
                    nc.vector.tensor_tensor(v3, v3, rb, ALU.mult).then_inc(s_nm.sem, 1)
                if kind == "PV":
                    u = 2 * tg + n
                    v.wait_ge(s_oh.sem, s_oh.at(i, u))
                    for b in range(2):
                        sl = slice(n * 1024, (n + 1) * 1024)
                        hi = ot_h[:, sl].rearrange("p (c q) -> p c q", q=P)[:, :, b * S:(b + 1) * S]
                        lo = ot_l[:, sl].rearrange("p (c q) -> p c q", q=P)[:, :, b * S:(b + 1) * S]
                        last = nc.vector.tensor_tensor(lo, psO[b][:, :].rearrange("p (c q) -> p c q", q=S), hi.bitcast(F32),
                                                       ALU.subtract)
                    last.then_inc(s_ol.sem, 1)
                if kind == "Y":
                    y = tg * 4 + n
                    v.wait_ge(s_Y.sem, s_Y.at(i, y))
                    nc.vector.tensor_tensor(xr(y), psY[n % 2][:, :], xr(y), ALU.add).then_inc(s_xr.sem, 1)
                    if not more:
                        v.wait_ge(s_xr.sem, s_xr.at(i, y))
                        nc.vector.bn_stats(stats[:, 6 * y:6 * y + 6], xr(y)).then_inc(s_st.sem, 1)

            def prologue():
                ln_v(v)
                split_lo(v, 0, 0, w1_h, w1_l)

            program(v, step, prologue)
            v.wait_ge(s_st.sem, s_st.at(0, TILES - 1))


def feed_forward(nc, at, io, out, m):
    WR, XT, ER, F0 = m["WR"], m["XT"], m["ER"], m["F0"]
    xr, x_res = m["xr"], m["x_res"]
    xt_h = at("xtf_h", XT, [KT * T], F32R)
    xt_l = at("xtf_l", XT + 32, [KT * T], F32R)
    wgu_h, wgu_l = at("wgu_h", WR, [2 * KT * 256], F32R), at("wgu_l", WR + 8, [2 * KT * 256], F32R)
    wdn_h, wdn_l = at("wdn_h", WR + 16, [2 * D], F32R), at("wdn_l", WR + 20, [2 * D], F32R)
    h_h, h_l = at("h_h", ER, [2 * 2 * GT], F32R), at("h_l", ER + 8, [2 * 2 * GT], F32R)
    NCH = 6
    q_st = at("q_stage", F0, [NCH * 512], I32)
    s_st = at("s_stage", F0 + 12, [NCH * 512], F32)
    w32 = at("w32", F0 + 24, [2 * 512], F32)
    xn = at("xn_f", F0 + 28, [2 * D], F32)
    sg = at("silu", F0 + 32, [2 * GT], F32)
    hf = at("hf", F0 + 36, [2 * GT], F32)

    with ExitStack() as ctx:
        ps = [ctx.enter_context(nc.psum_tensor(f"psF{n}", [P, 512], F32)) for n in range(8)]
        psG, psU, psY = ps[0:2], ps[2:4], ps[4:6]

        def sig(name, per, step=1):
            return Signal(nc, ctx, name, per, step, base=1)

        w_in = [sig(f"f_w_in{c}", 2, 16) for c in range(NCH)]
        w_32, w_hi, w_lo = sig("f_w", NCH), sig("f_w_hi", NCH), sig("f_w_lo", NCH)
        s_gp, s_up, s_sg, s_h, s_hh, s_hl = (sig(f"f_{n}", 8) for n in ("gate", "up", "silu", "hidden", "hidden_hi", "hidden_lo"))
        s_Y, s_xr = sig("f_out_psum", 16), sig("f_residual", 16)
        s_out = Signal(nc, ctx, "stored", 0, 16)
        ln_v, ln_a, ln_p = normalise_and_transpose(nc, ctx, m, xt_h, xt_l, xn, ps[0:4], "f_ln")
        block = ctx.enter_context(nc.Block())

        def section(tg, more):
            out_ = [("Y", tg, 0), ("Y", tg, 1), ("gu", tg + 1, 1), ("Y", tg, 2), ("Y", tg, 3)]
            if tg < GROUPS - 1 or more:
                out_.insert(0, ("gu", tg + 1, 0))
            else:
                out_.remove(("gu", tg + 1, 1))
            if tg == GROUPS - 1 and more:
                out_ = [("Y", tg, 0), ("w", 0, 0), ("Y", tg, 1), ("Y", tg, 2), ("Y", tg, 3), ("wd", 0, 0),
                        ("gu", tg + 1, 0), ("gu", tg + 1, 1)]
            return out_

        def program(eng, step, prologue):
            prologue()
            for n in range(2):
                step(-1, "gu", GROUPS, n, True)

            def turn(i, more):
                for tg in range(GROUPS):
                    for kind, g_, n in section(tg, more):
                        step(i, kind, g_, n, more)

            with eng.Fori(0, FCH - 1) as i:
                turn(i, True)
            turn(FCH - 1, False)

        def event(i, tg, n):
            return (i + 1, n) if tg == GROUPS else (i, tg * 2 + n)

        def halves(c):
            h, l = (wgu_h, wgu_l) if c < 4 else (wdn_h, wdn_l)
            o = c * 512 if c < 4 else (c - 4) * 512
            return h[:, o:o + 512], l[:, o:o + 512]

        @block.sync
        def _(sp):
            start(sp, *w_in)
            def load(i, c):
                o = slice(c * 512, (c + 1) * 512)
                if c < 4:
                    q, s_ = (("gate_q", "gate_s"), ("up_q", "up_s"))[c // 2]
                    k = 2 * (c % 2)
                    sp.dma_start(q_st[:, o].rearrange("p (k n) -> p k n", k=2),
                                 io[q].rearrange("(k p) n -> p k n", p=P)[:, k:k + 2, bass.ds(i * 256, 256)]).then_inc(w_in[c].sem, 16)
                    sp.dma_start(s_st[:, o].rearrange("p (k n) -> p k n", k=2),
                                 io[s_][k:k + 2, bass.ds(i * 256, 256)].partition_broadcast(P)).then_inc(w_in[c].sem, 16)
                else:
                    sp.dma_start(q_st[:, o], io["down_q"][bass.ds(i * 256 + (c - 4) * P, P), :]).then_inc(w_in[c].sem, 16)
                    sp.dma_start(s_st[:, o], io["down_s"][bass.ds(i * 2 + (c - 4), 1), :].rearrange("a n -> (a n)").partition_broadcast(P)
                                 ).then_inc(w_in[c].sem, 16)

            for c in range(NCH):
                load(0, c)
            with sp.Fori(0, FCH - 1) as i:
                for c in range(NCH):
                    sp.wait_ge(w_32.sem, w_32.at(i, c))
                    load(i + 1, c)
            for y in range(TILES):
                sp.wait_ge(s_xr.sem, s_xr.at(FCH - 1, y))
                sp.dma_start(out[y * P:(y + 1) * P, :], xr(y)).then_inc(s_out.sem, 16)
            sp.wait_ge(s_out.sem, TILES * 16)

        @block.tensor
        def _(pe):
            start(pe, s_gp, s_up, s_Y)
            def step(i, kind, tg, n, more):
                if kind == "gu":
                    j, e = event(i, tg, n)
                    if tg == GROUPS:
                        pe.wait_ge(w_lo.sem, w_lo.at(j, 3))
                    pe.wait_ge(s_h.sem, s_h.at(j, e - 2))
                    for bank, w0, s_ in ((psG[n], 0, s_gp), (psU[n], 1024, s_up)):
                        for k in range(KT):
                            c, w = k * T + (tg % GROUPS) * GT, w0 + k * 256 + n * P
                            last = split3(nc, bank[:, :], wgu_h[:, w:w + P], wgu_l[:, w:w + P],
                                          xt_h[:, c:c + GT], xt_l[:, c:c + GT], k == 0, k == KT - 1)
                        last.then_inc(s_.sem, 1)
                if kind == "Y":
                    y = tg * 4 + n
                    if n == 0:
                        pe.wait_ge(s_hl.sem, s_hl.at(i, tg * 2 + 1))
                        pe.wait_ge(w_lo.sem, w_lo.at(i, NCH - 1))
                    pe.wait_ge(s_xr.sem, s_xr.at(i, max(y - 2, -1)))
                    for k in range(2):
                        c = (tg % 2) * 1024 + k * GT + n * P
                        last = split3(nc, psY[n % 2][:, :], h_h[:, c:c + P], h_l[:, c:c + P],
                                      wdn_h[:, k * D:(k + 1) * D], wdn_l[:, k * D:(k + 1) * D], k == 0, k == 1)
                    last.then_inc(s_Y.sem, 1)

            program(pe, step, lambda: ln_p(pe))

        @block.scalar
        def _(act):
            start(act, w_hi, s_sg, s_hh)
            def split_hi(turn, chunks):
                for c in chunks:
                    act.wait_ge(w_32.sem, w_32.at(turn, c))
                    nc.scalar.activation(halves(c)[0], w32[:, (c % 2) * 512:(c % 2 + 1) * 512], ACT.Copy).then_inc(w_hi.sem, 1)

            def step(i, kind, tg, n, more):
                if kind == "w":
                    act.wait_ge(s_up.sem, s_up.at(i, 7))
                    split_hi(i + 1, range(4))
                if kind == "wd":
                    act.wait_ge(s_Y.sem, s_Y.at(i, 15))
                    split_hi(i + 1, range(4, NCH))
                if kind == "gu":
                    j, e = event(i, tg, n)
                    o = n * GT
                    act.wait_ge(s_gp.sem, s_gp.at(j, e))
                    act.wait_ge(s_h.sem, s_h.at(j, e - 2))
                    nc.scalar.activation(sg[:, o:o + GT], psG[n][:, :], ACT.Silu).then_inc(s_sg.sem, 1)
                    act.wait_ge(s_h.sem, s_h.at(j, e))
                    if not (type(i) is int and i < 0):
                        act.wait_ge(s_Y.sem, s_Y.at(i, 4 * (tg - 1) - 1))
                    c = (tg % 2) * 1024 + n * GT
                    nc.scalar.activation(h_h[:, c:c + GT], hf[:, o:o + GT], ACT.Copy).then_inc(s_hh.sem, 1)

            def prologue():
                ln_a(act)
                split_hi(0, range(NCH))

            program(act, step, prologue)

        @block.vector
        def _(v):
            start(v, w_32, w_lo, s_h, s_hl, s_xr)
            def dequantise(turn, chunks):
                for c in chunks:
                    sl, w = slice(c * 512, (c + 1) * 512), w32[:, (c % 2) * 512:(c % 2 + 1) * 512]
                    v.wait_ge(w_in[c].sem, w_in[c].at(turn, 1))
                    if c >= 2:
                        v.wait_ge(w_lo.sem, w_lo.at(turn, c - 2))
                    nc.vector.tensor_tensor(w, q_st[:, sl], s_st[:, sl], ALU.mult).then_inc(w_32.sem, 1)
                    v.wait_ge(w_hi.sem, w_hi.at(turn, c))
                    hi, lo = halves(c)
                    nc.vector.tensor_tensor(lo, w, hi.bitcast(F32), ALU.subtract).then_inc(w_lo.sem, 1)

            def step(i, kind, tg, n, more):
                if kind == "w":
                    dequantise(i + 1, range(4))
                if kind == "wd":
                    dequantise(i + 1, range(4, NCH))
                if kind == "gu":
                    j, e = event(i, tg, n)
                    o = n * GT
                    v.wait_ge(s_sg.sem, s_sg.at(j, e))
                    v.wait_ge(s_up.sem, s_up.at(j, e))
                    nc.vector.tensor_tensor(hf[:, o:o + GT], psU[n][:, :], sg[:, o:o + GT], ALU.mult).then_inc(s_h.sem, 1)
                    v.wait_ge(s_hh.sem, s_hh.at(j, e))
                    c = (tg % 2) * 1024 + n * GT
                    nc.vector.tensor_tensor(h_l[:, c:c + GT], hf[:, o:o + GT], h_h[:, c:c + GT].bitcast(F32),
                                            ALU.subtract).then_inc(s_hl.sem, 1)
                if kind == "Y":
                    y = tg * 4 + n
                    v.wait_ge(s_Y.sem, s_Y.at(i, y))
                    nc.vector.tensor_tensor(xr(y), psY[n % 2][:, :], xr(y), ALU.add).then_inc(s_xr.sem, 1)

            def prologue():
                ln_v(v)
                dequantise(0, range(NCH))

            program(v, step, prologue)


def kernel(**inputs):
    import concourse.bacc as bacc
    from concourse.bass_utils import run_bass_kernel_spmd as run

    a = {n: np.asarray(v) for n, v in inputs.items()}
    p = np.arange(P)
    half, head, d8 = p // 64, p % 64 // 8, p % 8
    g = lambda j: 2 * j + head // HPG
    q_rows = np.concatenate([g(j) * 96 + head % HPG * 16 + half * 8 + d8 for j in range(4)])
    k_rows = np.concatenate([g(j) * 96 + 64 + half * 8 + d8 for j in range(4)])
    v_rows = (np.arange(G)[:, None] * 96 + 80 + np.arange(16)[None, :]).ravel()
    rows = np.concatenate([q_rows, k_rows, v_rows])
    d_rows = np.concatenate([((gh * 4 + p // 32) * 4 + p % 32 // 16 * 2 + par) * 16 + p % 16
                             for gh in range(2) for par in range(2)])
    swap = (p + 64) % P
    b = a["L0_attn_b_qkv"]
    bq, bk = b[q_rows].reshape(4, P).T, b[k_rows].reshape(4, P).T
    hmask = (head[:, None] == np.arange(8)[None, :]).astype(np.float32)
    iota = (p[:, None] + P * np.arange(4)[None, :]).astype(np.float32)
    small = np.concatenate([bq, bk, bq[swap], bk[swap], hmask, iota], axis=1).astype(np.float32)

    def angles(n, dim, base):
        inv = np.float32(1.0) / np.float32(base) ** (np.arange(0, dim, 2, dtype=np.float32) / np.float32(dim))
        return np.arange(n, dtype=np.float32)[:, None] * inv[None, :].astype(np.float32)

    an = angles(S, HD_SELF, 1000000.0).T[d8]
    sign = np.where(half == 0, -1.0, 1.0).astype(np.float32)[:, None]
    rope_self = np.stack([np.cos(an), sign * np.sin(an)]).astype(np.float32)
    ax = angles(MAX_POS, HD_X, 10000.0)
    rope_x = np.concatenate([np.cos(ax), np.cos(ax), -np.sin(ax), np.sin(ax)], axis=1).astype(np.float32)
    causal = (np.arange(S)[None, :] <= (p % S)[:, None]).astype(np.int32)

    arrays = {
        "x": a["x"].reshape(T, D), "ctx": a["ctx_4096"].reshape(T, D), "pos": a["pos_BxS2"].reshape(T),
        "mask": a["mask_BxSxS2_ik0"], "w_qkv": a["L0_attn_w_qkv"].T[:, rows], "b_v": b[v_rows],
        "w_dense": a["L0_attn_w_dense"].T[d_rows], "b_dense": a["L0_attn_b_dense"],
        "wq": a["L0_xattn_Wq"], "wk": a["L0_xattn_Wk"], "wv": a["L0_xattn_Wv"], "wo": a["L0_xattn_Wo"],
        "gate_q": a["L0_ffn_gate_q"].T, "gate_s": a["L0_ffn_gate_s"].T, "up_q": a["L0_ffn_up_q"].T,
        "up_s": a["L0_ffn_up_s"].T, "down_q": a["L0_ffn_down_q"].T, "down_s": a["L0_ffn_down_s"].T,
        "small": small, "ident": np.eye(P, dtype=np.float32), "rope_self": rope_self, "rope_x": rope_x,
        "causal": causal,
    }
    arrays = {n: np.ascontiguousarray(v) for n, v in arrays.items()}
    nc = bacc.Bacc("TRN2", target_bir_lowering=False, num_devices=1, dynamic_dma_scratch_size=1024)
    io = {n: nc.dram_tensor("in_" + n, v.shape, mybir.dt.from_np(v.dtype), kind="ExternalInput").ap()
          for n, v in arrays.items()}
    out = nc.dram_tensor("out_x", (T, D), F32, kind="ExternalOutput").ap()
    build(nc, io, out)
    r = run(nc, [{"in_" + n: v for n, v in arrays.items()}], core_ids=[0])
    return r.results[0]["out_x"].reshape(B, S, D)
```

```python
from contextlib import ExitStack

import numpy as np

import concourse.bass as bass
from concourse import mybir

F32 = mybir.dt.float32
F32R = mybir.dt.float32r
F16 = mybir.dt.float16
I32 = mybir.dt.int32
U8 = mybir.dt.uint8
ALU = mybir.AluOpType
ACT = mybir.ActivationFunctionType
AX_X = mybir.AxisListType.X

P = 128
B, S, D = 32, 64, 512
T = B * S
TILES = T // P
GROUP = 4
GROUPS = TILES // GROUP
GT = GROUP * P
KT = D // P
G = 8
HPG = 4
HD_SELF, HD_X = 16, 128
SCALE_SELF = 1.0 / HD_SELF
SCALE_X = float(np.float32(1.0) / np.sqrt(np.float32(HD_X)))
FILL_SELF = float(np.finfo(np.float32).min)
FILL_X = -1.0e9 / SCALE_X
MAX_POS = 512
FF = 1792
FCH = FF // 256
EPS = 1e-5


class Signal:

    def __init__(self, nc, ctx, name, per=0, step=1, base=0):
        self.sem = ctx.enter_context(nc.semaphore(name))
        self.per, self.step, self.base = per, step, base

    def at(self, turn, n):
        value = (turn * self.per + n + 1 + self.base) * self.step
        return max(value, self.base * self.step) if type(value) is int else value

    def ring(self, turn, n, slots):
        return self.at(turn, max(n - slots, -1))


def start(eng, *signals):
    for signal in signals:
        assert signal.base == 1
        eng.sem_inc(signal.sem, signal.step)


class Banks:

    def __init__(self, banks, order, readers):
        self.banks, self.order, self.readers = banks, order, readers

    def __getitem__(self, use):
        return self.banks[self.order.index(use) % len(self.banks)]

    def last_reads(self, turn, use):
        n = self.order.index(use) - len(self.banks)
        if n >= 0:
            return [(signal.sem, signal.at(turn, event)) for signal, event in self.readers(self.order[n])]
        return [(signal.sem, signal.at(turn, -1)) for old in self.order[-len(self.banks):] for signal, _ in self.readers(old)]


CONSTS = 7


def settle(eng, m):
    eng.sem_inc(m["settled"][eng.engine].sem, 1)


def split3(nc, out, wh, wl, xh, xl, first, last):
    nc.tensor.matmul(out, wh, xh, start=first, stop=False)
    nc.tensor.matmul(out, wh, xl, start=False, stop=False)
    return nc.tensor.matmul(out, wl, xh, start=False, stop=last)


def build(nc, io, out):
    KB = 1024
    BASE = 2 * KB
    outer = ExitStack()
    with outer:
        names = {}

        def at(name, kb, shape, dt):
            n = 1
            for s in shape:
                n *= s
            assert BASE + kb * KB + n * mybir.dt.size(dt) <= 229368, name
            names[name] = (kb, n)
            return nc.alloc_sbuf_tensor_at(name, [P, n], dt, offset=int(BASE + kb * KB))

        XR, XT, WR, ER, FR = 0, 32, 96, 128, 160
        x_res = at("x_res", XR, [TILES * D], F32)
        ident = at("ident", FR, [P], F32)
        small = at("small", FR + 0.5, [128], F32)
        mask8 = at("mask8", FR + 1, [B * S], U8)
        cosx = at("cosx", FR + 3, [T], F32)
        sinx = at("sinx", FR + 11, [T], F32)
        F0 = FR + 19
        stats = at("stats", FR + 61, [TILES * 6], F32)
        mv = at("mv", FR + 61.375, [TILES * 2], F32)
        rstd = at("rstd", FR + 61.5, [TILES], F32)
        kscr = nc.dram_tensor("k_scratch", (G, P, 2, T), F16, kind="Internal").ap()
        vscr = nc.dram_tensor("v_scratch", (T, G * HD_X), F32, kind="Internal").ap()

        q_b = small[:, 0:4]
        k_b = small[:, 4:8]
        q_bs = small[:, 8:12]
        k_bs = small[:, 12:16]
        hmask = small[:, 16:24]
        iota = small[:, 24:28]
        xr = lambda tile: x_res[:, bass.ds(tile * D, D)]

        wqk_h = at("wqk_h", WR, [KT * 1024], F32R)
        wqk_l = at("wqk_l", WR + 16, [KT * 1024], F32R)
        wd_h = at("wd_h", XT, [KT * D], F32R)
        wd_l = at("wd_l", XT + 8, [KT * D], F32R)
        wv_h = at("wv_h", XT + 48, [KT * P], F32R)
        wv_l = at("wv_l", XT + 50, [KT * P], F32R)
        cos_a = at("cos_a", F0, [S], F32)
        sin_a = at("sin_a", F0 + 0.25, [S], F32)
        causal = at("causal", F0 + 0.5, [S], I32)
        bv_row = at("bv_row", F0 + 0.75, [P], F32)
        bd_row = at("bd_row", F0 + 1.25, [D], F32)
        A0 = F0 + 3.25

        consts_in = Signal(nc, outer, "consts_in", step=16)

        settled = {e.engine: Signal(nc, outer, n) for e, n in ((nc.gpsimd, "settled_pool"), (nc.vector, "settled_dve"))}

        with ExitStack() as ctx:
            NCH = 15
            RING = 4
            stage = at("stage0", ER, [RING * 512], F32)
            pos_i = at("pos_i", ER + 8, [T], I32)
            pos_f = at("pos_f", ER + 16, [T], F32)
            pos_n = at("pos_n", A0, [T], F32)
            onehot = at("onehot", XT + 16, [4 * 512], F32R)
            tab_h = at("tab_h", XT + 24, [1024], F32R)
            tab_l = at("tab_l", XT + 28, [1024], F32R)
            mask_i = at("mask_i", ER + 24, [T], I32)
            psT = [ctx.enter_context(nc.psum_tensor(f"psT{n}", [P, 512], F32)) for n in range(4)]
            loaded = Signal(nc, ctx, "setup_loaded", step=16)
            pos_in = Signal(nc, ctx, "pos_in", step=16)
            mask_in = Signal(nc, ctx, "mask_in", step=16)
            x_in = Signal(nc, ctx, "x_in", step=16)
            w_in = [Signal(nc, ctx, f"w_in{r}", step=16) for r in range(RING)]
            w_hi = Signal(nc, ctx, "w_hi")
            w_lo = Signal(nc, ctx, "w_lo")
            poss = Signal(nc, ctx, "pos_ready")
            oh = Signal(nc, ctx, "onehot_ready")
            tabp = Signal(nc, ctx, "tables_in_psum")
            cosd = Signal(nc, ctx, "cos_ready")
            sind = Signal(nc, ctx, "sin_ready")
            dve = Signal(nc, ctx, "stats_step")
            rt = Signal(nc, ctx, "sqrt_ready")
            block = ctx.enter_context(nc.Block())

            chunks = []
            tabv = io["rope_x"].rearrange("(k p) n -> p k n", p=P)
            for k2 in range(2):
                chunks.append((tabv[:, 2 * k2:2 * k2 + 2, :], (2, 256), tab_h[:, k2 * 512:k2 * 512 + 512],
                               tab_l[:, k2 * 512:k2 * 512 + 512]))
            for k in range(KT):
                for h in range(2):
                    c = k * 1024 + h * 512
                    chunks.append((io["w_qkv"][k * P:(k + 1) * P, h * 512:(h + 1) * 512], None,
                                   wqk_h[:, c:c + 512], wqk_l[:, c:c + 512]))
            chunks.append((io["w_qkv"].rearrange("(k p) n -> p k n", p=P)[:, :, 1024:1152], (KT, P),
                           wv_h[:, :], wv_l[:, :]))
            for k in range(KT):
                chunks.append((io["w_dense"][k * P:(k + 1) * P, :], None,
                               wd_h[:, k * D:(k + 1) * D], wd_l[:, k * D:(k + 1) * D]))
            assert len(chunks) == NCH
            st = lambda c: stage[:, (c % RING) * 512:(c % RING) * 512 + 512]

            @block.sync
            def _(sp):
                sp.dma_start(pos_i[:, :], io["pos"].partition_broadcast(P)).then_inc(pos_in.sem, 16)
                xv = io["x"].rearrange("(t p) d -> p t d", p=P)
                for q in range(GROUPS):
                    sp.dma_start(x_res[:, q * 4 * D:(q + 1) * 4 * D].rearrange("p (t d) -> p t d", d=D),
                                 xv[:, 4 * q:4 * q + 4, :]).then_inc(x_in.sem, 16)
                for c, (src, shape, hi, lo) in enumerate(chunks):
                    if c >= RING:
                        sp.wait_ge(w_lo.sem, w_lo.at(0, c - RING))
                    dst = st(c) if shape is None else st(c).rearrange("p (a b) -> p a b", a=shape[0])
                    sp.dma_start(dst, src).then_inc(w_in[c % RING].sem, 16)

            @block.scalar
            def _(act):
                act.dma_start(ident[:, :], io["ident"]).then_inc(consts_in.sem, 16)
                act.dma_start(small[:, 0:28], io["small"]).then_inc(consts_in.sem, 16)
                act.dma_start(cos_a[:, :], io["rope_self"][0]).then_inc(consts_in.sem, 16)
                act.dma_start(sin_a[:, :], io["rope_self"][1]).then_inc(consts_in.sem, 16)
                act.dma_start(causal[:, :], io["causal"]).then_inc(consts_in.sem, 16)
                act.dma_start(bv_row[:, :], io["b_v"].partition_broadcast(P)).then_inc(consts_in.sem, 16)
                act.dma_start(bd_row[:, :], io["b_dense"].partition_broadcast(P)).then_inc(consts_in.sem, 16)
                for b in range(2):
                    act.dma_start(mask_i[b * S:(b + 1) * S, :].rearrange("q (b k) -> q b k", k=S),
                                  io["mask"].rearrange("b q k -> q b k")).then_inc(mask_in.sem, 16)
                for c, (src, shape, hi, lo) in enumerate(chunks):
                    act.wait_ge(w_in[c % RING].sem, w_in[c % RING].at(0, c // RING))
                    nc.scalar.activation(hi, st(c), ACT.Copy).then_inc(w_hi.sem, 1)
                    if c == 1:
                        for q in range(GROUPS):
                            act.wait_ge(tabp.sem, tabp.at(0, 2 * q))
                            nc.scalar.activation(cosx[:, q * GT:(q + 1) * GT], psT[0][:, :], ACT.Copy).then_inc(cosd.sem, 1)
                act.wait_ge(dve.sem, TILES * 2 + 1)
                nc.scalar.activation(rstd[:, :], rstd[:, :], ACT.Sqrt).then_inc(rt.sem, 1)
                act.wait_ge(consts_in.sem, CONSTS * 16)

            @block.vector
            def _(v):
                v.wait_ge(pos_in.sem, pos_in.at(0, 0))
                nc.vector.tensor_copy(pos_f[:, :], pos_i[:, :]).then_inc(poss.sem, 1)
                v.wait_ge(poss.sem, poss.at(0, 0))
                nc.vector.tensor_scalar(pos_n[:, :], pos_f[:, :], 0.0, float(MAX_POS), ALU.is_lt, ALU.mult).then_inc(poss.sem, 1)
                v.wait_ge(poss.sem, poss.at(0, 1))
                nc.vector.tensor_tensor(pos_f[:, :], pos_f[:, :], pos_n[:, :], ALU.add).then_inc(poss.sem, 1)
                v.wait_ge(poss.sem, poss.at(0, 2))
                nc.vector.tensor_scalar(pos_f[:, :], pos_f[:, :], 0.0, float(MAX_POS - 1), ALU.max, ALU.min).then_inc(poss.sem, 1)
                v.wait_ge(poss.sem, poss.at(0, 3))
                for c, (src, shape, hi, lo) in enumerate(chunks):
                    v.wait_ge(w_hi.sem, w_hi.at(0, c))
                    nc.vector.tensor_tensor(lo, st(c), hi.bitcast(F32), ALU.subtract).then_inc(w_lo.sem, 1)
                    if c == 1:
                        v.wait_ge(consts_in.sem, CONSTS * 16)
                        for q in range(GROUPS):
                            if q:
                                v.wait_ge(tabp.sem, tabp.at(0, 2 * q - 1))
                            for k in range(4):
                                nc.vector.tensor_scalar(onehot[:, k * 512:(k + 1) * 512], pos_f[:, q * GT:(q + 1) * GT],
                                                        iota[:, k:k + 1], None, ALU.is_equal).then_inc(oh.sem, 1)
                            v.wait_ge(tabp.sem, tabp.at(0, 2 * q + 1))
                            nc.vector.tensor_copy(sinx[:, q * GT:(q + 1) * GT], psT[1][:, :]).then_inc(sind.sem, 1)
                v.wait_ge(mask_in.sem, 32)
                nc.vector.tensor_scalar(mask8[:, :], mask_i[:, :], 0.0, None, ALU.not_equal).then_inc(sind.sem, 1)
                n = 0
                for t in range(TILES):
                    if t % 4 == 0:
                        v.wait_ge(x_in.sem, x_in.at(0, t // 4))
                    nc.vector.bn_stats(stats[:, 6 * t:6 * t + 6], xr(t)).then_inc(dve.sem, 1)
                for t in range(TILES):
                    v.wait_ge(dve.sem, t + 1)
                    nc.vector.bn_aggr(mv[:, 2 * t:2 * t + 2], stats[:, 6 * t:6 * t + 6]).then_inc(dve.sem, 1)
                v.wait_ge(dve.sem, 2 * TILES)
                nc.vector.tensor_scalar_add(rstd[:, :], mv[:, 1:2 * TILES:2], EPS).then_inc(dve.sem, 1)
                v.wait_ge(rt.sem, rt.at(0, 0))
                nc.vector.reciprocal(rstd[:, :], rstd[:, :]).then_inc(dve.sem, 1)

            @block.tensor
            def _(pe):
                pe.wait_ge(w_lo.sem, w_lo.at(0, 1))
                for q in range(GROUPS):
                    pe.wait_ge(oh.sem, oh.at(0, 4 * q + 3))
                    for m in range(2):
                        if q:
                            pe.wait_ge((cosd, sind)[m].sem, (cosd, sind)[m].at(0, q - 1))
                        for k in range(4):
                            c = k * 256 + m * P
                            nc.tensor.matmul(psT[m][:, :], tab_h[:, c:c + P], onehot[:, k * 512:(k + 1) * 512],
                                             start=(k == 0), stop=False)
                            last = nc.tensor.matmul(psT[m][:, :], tab_l[:, c:c + P], onehot[:, k * 512:(k + 1) * 512],
                                                    start=False, stop=(k == 3))
                        last.then_inc(tabp.sem, 1)

        self_attention(nc, at, io, locals())
        cross_keys_values(nc, at, io, locals())
        cross_attention(nc, at, io, locals())
        feed_forward(nc, at, io, out, locals())


def self_attention(nc, at, io, m):
    WR, XT, ER, A0 = m["WR"], m["XT"], m["ER"], m["A0"]
    wqk_h, wqk_l, wd_h, wd_l, wv_h, wv_l = (m[n] for n in ("wqk_h", "wqk_l", "wd_h", "wd_l", "wv_h", "wv_l"))
    xr, mv, rstd, stats, ident = m["xr"], m["mv"], m["rstd"], m["stats"], m["ident"]
    xt_h = at("xta_h", XT + 16, [KT * GT], F32R)
    xt_l = at("xta_l", XT + 24, [KT * GT], F32R)
    ct_h = at("cta_h", XT + 32, [2 * KT * P], F32R)
    ct_l = at("cta_l", XT + 36, [2 * KT * P], F32R)
    on = at("ona", XT + 40, [GROUP * D], F32)
    r16 = {n: at(n, A0 + 4 * i, [4 * GT], F16) for i, n in enumerate(("qa_h", "qa_l", "ka_h", "ka_l"))}
    A1 = A0 + 16
    t1 = at("t1a", A1, [2 * GT], F32)
    sw = at("swa", A1 + 4, [2 * GT], F32)
    va_h = at("va_h", A1 + 8, [GT], F16)
    va_l = at("va_l", A1 + 9, [GT], F16)
    v32 = at("v32a", A1 + 10, [GT], F32)
    xn = at("xna", A1 + 12, [2 * D], F32)
    sums = at("sums_a", A1 + 16, [32], F32)
    rinv = at("rinv_a", A1 + 16.25, [32], F32)
    mx = at("mx_a", A1 + 16.5, [4 * 8], F32)
    qm_h = at("qm_h", ER, [2 * 2048], F16)
    qm_l = at("qm_l", ER + 8, [2 * 2048], F16)
    pr = at("pr_a", ER + 16, [4 * 512], F32)
    pt_h = at("pta_h", ER + 24, [4 * 512], F16)
    pt_l = at("pta_l", ER + 28, [4 * 512], F16)

    with ExitStack() as ctx:
        ps = [ctx.enter_context(nc.psum_tensor(f"psA{n}", [P, 512], F32)) for n in range(8)]
        psQ, psS, psP, psO = ps[0:2], ps[2:4], ps[4:6], ps[6:8]

        def sig(name, per):
            return Signal(nc, ctx, name, per, base=1)

        s_xn, s_xp, s_xh, s_xl = sig("a_xn", 4), sig("a_xnT_psum", 4), sig("a_xT_hi", 4), sig("a_xT_lo", 4)
        s_bd = sig("a_bias_added", 4)
        s_vp, s_v32, s_vh, s_vl = sig("a_v_psum", 1), sig("a_v", 1), sig("a_v_hi", 1), sig("a_v_lo", 1)
        s_qp = sig("a_proj_psum", 8)
        s_sw, s_t1, s_t2, s_r = sig("a_swapped", 8), sig("a_cos_term", 8), sig("a_sin_term", 8), sig("a_roped", 8)
        s_rh, s_rl = sig("a_roped_hi", 8), sig("a_roped_lo", 8)
        s_qmh, s_qml = sig("a_q_masked_hi", 8), sig("a_q_masked_lo", 8)
        s_S = sig("a_scores_psum", 16)
        s_fill, s_pred, s_mx, s_sub = sig("a_filled", 16), sig("a_causal", 16), sig("a_max", 16), sig("a_less_max", 16)
        s_exp, s_sum, s_T = sig("a_exp", 16), sig("a_sum", 16), sig("a_pT_psum", 16)
        s_ph, s_pl, s_O = sig("a_pT_hi", 16), sig("a_pT_lo", 16), sig("a_o_psum", 16)
        s_ri, s_on = sig("a_inv_sum", 8), sig("a_o_normal", 8)
        s_cp, s_ch, s_cl = sig("a_oT_psum", 4), sig("a_oT_hi", 4), sig("a_oT_lo", 4)
        s_Y, s_xr, s_st = sig("a_dense_psum", 4), sig("a_residual", 4), sig("a_stats", 4)
        block = ctx.enter_context(nc.Block())

        PROJ = {7: 0, 8: 1, 9: 2, 10: 3, 12: 4, 13: 5, 14: 6, 15: 7}
        steps = []
        for s in range(21):
            own = lambda kind, n, last=15: steps.append((kind, n, 0)) if 0 <= n <= last else None
            nxt = lambda kind, n: steps.append((kind, n, 1))
            if s >= 4 and s % 2 == 0:
                own("norm", s // 2 - 2, 7)
            own("turn", s - 1)
            if s + 1 >= 1:
                own("fill", s + 1)
                own("score", s + 1)
            own("split_pT", s - 2)
            own("softmax", s)
            own("sum", s - 1)
            own("pv", s - 2)
            if s % 2 == 0:
                own("mask", s // 2 + 1, 7)
            if s - 1 in PROJ:
                nxt("rope", PROJ[s - 1])
            if s - 2 in PROJ:
                nxt("rope_lo", PROJ[s - 2])
            if 2 <= s <= 5:
                nxt("ln_lo", s - 2)
            if s <= 3:
                nxt("ln", s)
            if 1 <= s <= 4:
                nxt("lnT", s - 1)
            if s == 6:
                nxt("v", 0)
            if s == 7:
                nxt("v32", 0)
            if s in PROJ:
                nxt("proj", PROJ[s])
            if s == 18:
                nxt("v_split", 0)
                nxt("mask", 0)
                nxt("fill", 0)
                nxt("score", 0)
            own("dense", s - 16, 3)
            own("y", s - 17, 3)

        def turn_steps(i):
            if type(i) is int:
                return [x for x in steps if x[2] == (1 if i < 0 else 0)]
            return steps

        def readers(kind, n):
            return {"lnT": (s_xl, n), "v": (s_v32, n), "proj": (s_t1, n), "dense": (s_cl, n), "y": (s_xr, n)}[kind]

        class Products:

            def __init__(self, i):
                self.turn = i
                self.uses = [x for x in turn_steps(i) if x[0] in ("lnT", "v", "proj", "dense", "y")]

            def __getitem__(self, use):
                return psQ[self.uses.index(use) % 2]

            def last_reads(self, use):
                n = self.uses.index(use) - 2
                if n >= 0:
                    kind, event, ahead = self.uses[n]
                    signal, event = readers(kind, event)
                    return [(signal.sem, signal.at(self.turn + ahead, event))]
                return [(s_t1.sem, s_t1.at(self.turn + 1, -1)), (s_cl.sem, s_cl.at(self.turn, -1)),
                        (s_xr.sem, s_xr.at(self.turn, -1))]

        def program(eng, step):
            def turn(i):
                bank = Products(i)
                for kind, n, ahead in turn_steps(i):
                    step(i + ahead, kind, n, bank, (kind, n, ahead))

            turn(-1)
            with eng.Fori(0, GROUPS - 1) as i:
                turn(i)
            turn(GROUPS - 1)

        COL = lambda t, hp, b: ((t * 2 + hp) * 2 + b) * S

        @block.tensor
        def _(pe):
            start(pe, s_xp, s_vp, s_qp, s_S, s_T, s_O, s_cp, s_Y)

            def step(i, kind, n, bank, use):
                if kind in ("lnT", "v", "proj", "dense", "y"):
                    for read, value in bank.last_reads(use):
                        pe.wait_ge(read, value)
                if kind == "lnT":
                    pe.wait_ge(s_xn.sem, s_xn.at(i, n))
                    for k in range(KT):
                        c = (n % 2) * D + k * P
                        last = nc.tensor.transpose(bank[use][:, k * P:(k + 1) * P], xn[:, c:c + P], ident[:, :])
                    last.then_inc(s_xp.sem, 1)
                if kind == "v":
                    pe.wait_ge(s_xl.sem, s_xl.at(i, 3))
                    for t in range(4):
                        for k in range(KT):
                            c = k * GT + t * P
                            last = split3(nc, bank[use][:, t * P:(t + 1) * P], xt_h[:, c:c + P], xt_l[:, c:c + P],
                                          wv_h[:, k * P:(k + 1) * P], wv_l[:, k * P:(k + 1) * P], k == 0, k == KT - 1)
                    last.then_inc(s_vp.sem, 1)
                if kind == "proj":
                    for k in range(KT):
                        c = k * 1024 + (n % 2) * 512 + (n // 2) * P
                        last = split3(nc, bank[use][:, :], wqk_h[:, c:c + P], wqk_l[:, c:c + P],
                                      xt_h[:, k * GT:(k + 1) * GT], xt_l[:, k * GT:(k + 1) * GT], k == 0, k == KT - 1)
                    last.then_inc(s_qp.sem, 1)
                if kind == "score":
                    j, u, g, ring = n // 4, n // 2 % 2, n % 2, n // 2 % 2
                    pe.wait_ge(s_qmh.sem, s_qmh.at(i, n // 2))
                    pe.wait_ge(s_qml.sem, s_qml.at(i, n // 2))
                    if n % 4 == 0:
                        pe.wait_ge(s_rl.sem, s_rl.at(i, 2 * j + 1))
                    pe.wait_ge(s_pred.sem, s_pred.ring(i, n, 2))
                    for t in range(2):
                        for hp in range(2):
                            for b in range(2):
                                q = ring * 2048 + (t * 2 + b) * 512 + (4 * g + 2 * hp) * S
                                kk = j * GT + (2 * u + t) * P + b * S
                                last = split3(nc, psS[n % 2][:, COL(t, hp, b):COL(t, hp, b) + S],
                                              qm_h[:, q:q + P], qm_l[:, q:q + P],
                                              r16["ka_h"][:, kk:kk + S], r16["ka_l"][:, kk:kk + S], True, True)
                    last.then_inc(s_S.sem, 1)
                if kind == "turn":
                    pe.wait_ge(s_exp.sem, s_exp.at(i, n))
                    pe.wait_ge(s_pl.sem, s_pl.ring(i, n, 2))
                    for c in range(4):
                        last = nc.tensor.transpose(psP[n % 2][:, c * P:(c + 1) * P],
                                                   pr[:, (n % 4) * 512 + c * P:(n % 4) * 512 + (c + 1) * P], ident[:, :])
                    last.then_inc(s_T.sem, 1)
                if kind == "pv":
                    j, u, g = n // 4, n // 2 % 2, n % 2
                    pe.wait_ge(s_pl.sem, s_pl.at(i, n))
                    if n == 0:
                        pe.wait_ge(s_vl.sem, s_vl.at(i, 0))
                    if g == 0:
                        pe.wait_ge(s_on.sem, s_on.ring(i, n // 2, 1))
                    for t in range(2):
                        for hp in range(2):
                            for b in range(2):
                                rows = slice(b * S, (b + 1) * S)
                                o = ((t * 2 + g) * 2 + hp) * HD_SELF
                                c = (n % 4) * 512 + (t * 2 + hp) * P
                                vc = (2 * u + t) * P + (2 * j + g) * HD_SELF
                                last = split3(nc, psO[b][:, o:o + HD_SELF], pt_h[rows, c:c + P], pt_l[rows, c:c + P],
                                              va_h[rows, vc:vc + HD_SELF], va_l[rows, vc:vc + HD_SELF], True, True)
                    last.then_inc(s_O.sem, 1)
                if kind == "dense":
                    pe.wait_ge(s_on.sem, s_on.at(i, 6 + n // 2))
                    src = on[:, n * D:(n + 1) * D].rearrange("p (b g c) -> p b g c", b=2, g=2)
                    for gh in range(2):
                        for b in range(2):
                            dst = bank[use][:, gh * 256:(gh + 1) * 256].rearrange("p (h t) -> p h t", h=2)
                            last = nc.tensor.transpose(dst[:, :, b * S:(b + 1) * S], src[:, b, gh, :], ident[:, :])
                    last.then_inc(s_cp.sem, 1)
                if kind == "y":
                    pe.wait_ge(s_cl.sem, s_cl.at(i, n))
                    for k in range(KT):
                        c = (n % 2) * 512 + k * P
                        last = split3(nc, bank[use][:, :], ct_h[:, c:c + P], ct_l[:, c:c + P],
                                      wd_h[:, k * D:(k + 1) * D], wd_l[:, k * D:(k + 1) * D], k == 0, k == KT - 1)
                    last.then_inc(s_Y.sem, 1)

            program(pe, step)

        def mask_heads(engine_op, half, qm, n):
            j, u, ring = n // 2, n % 2, n % 2
            src = r16[half][:, j * GT + u * 256:j * GT + (u + 1) * 256].rearrange("p (c q) -> p c q", q=S)
            dst = qm[:, ring * 2048:(ring + 1) * 2048].rearrange("p (c h q) -> p c h q", h=8, q=S)
            for h in range(8):
                last = engine_op(dst[:, :, h, :], src, m["hmask"][:, h:h + 1])
            return last

        @block.scalar
        def _(act):
            start(act, s_xh, s_vh, s_sw, s_rh, s_exp, s_ph, s_ch, s_qml)

            def step(i, kind, n, bank, use):
                if kind == "lnT":
                    act.wait_ge(s_xp.sem, s_xp.at(i, n))
                    act.wait_ge(s_qp.sem, s_qp.at(i, -1))
                    dst = xt_h[:, :].rearrange("p (k t) -> p k t", k=KT)[:, :, n * P:(n + 1) * P]
                    nc.scalar.activation(dst, bank[use][:, :].rearrange("p (k t) -> p k t", k=KT), ACT.Copy).then_inc(s_xh.sem, 1)
                if kind == "v_split":
                    act.wait_ge(s_v32.sem, s_v32.at(i, 0))
                    act.wait_ge(s_O.sem, s_O.at(i, -1))
                    nc.scalar.activation(va_h[:, :], v32[:, :], ACT.Copy).then_inc(s_vh.sem, 1)
                if kind == "proj":
                    act.wait_ge(s_qp.sem, s_qp.at(i, n))
                    act.wait_ge(s_r.sem, s_r.ring(i, n, 2))
                    o = (n % 2) * GT
                    nc.scalar.activation(sw[0:64, o:o + GT], bank[use][64:128, :], ACT.Copy)
                    nc.scalar.activation(sw[64:128, o:o + GT], bank[use][0:64, :], ACT.Copy).then_inc(s_sw.sem, 1)
                if kind == "rope":
                    o, j = (n % 2) * GT, n // 2
                    dst = r16["qa_h" if n % 2 == 0 else "ka_h"]
                    act.wait_ge(s_r.sem, s_r.at(i, n))
                    act.wait_ge(s_S.sem, s_S.at(i - 1, 4 * j + 3))
                    act.wait_ge(s_qmh.sem, s_qmh.at(i - 1, 2 * j + 1))
                    nc.scalar.activation(dst[:, j * GT:(j + 1) * GT], t1[:, o:o + GT], ACT.Copy).then_inc(s_rh.sem, 1)
                if kind == "mask":
                    act.wait_ge(s_rl.sem, s_rl.at(i, n // 2 * 2))
                    act.wait_ge(s_S.sem, s_S.at(i, max(2 * n - 3, -1)))
                    mask_heads(lambda dst, src, h: nc.scalar.activation(dst, src, ACT.Copy, scale=h), "qa_l", qm_l, n
                               ).then_inc(s_qml.sem, 1)
                if kind == "softmax":
                    o = (n % 4) * 512
                    act.wait_ge(s_sub.sem, s_sub.at(i, n))
                    nc.scalar.activation(pr[:, o:o + 512], pr[:, o:o + 512], ACT.Exp, scale=SCALE_SELF).then_inc(s_exp.sem, 1)
                if kind == "turn":
                    o = (n % 4) * 512
                    act.wait_ge(s_T.sem, s_T.at(i, n))
                    act.wait_ge(s_O.sem, s_O.ring(i, n, 4))
                    nc.scalar.activation(pt_h[:, o:o + 512], psP[n % 2][:, :], ACT.Copy).then_inc(s_ph.sem, 1)
                if kind == "dense":
                    act.wait_ge(s_cp.sem, s_cp.at(i, n))
                    act.wait_ge(s_Y.sem, s_Y.ring(i, n, 2))
                    c = (n % 2) * 512
                    nc.scalar.activation(ct_h[:, c:c + 512], bank[use][:, :], ACT.Copy).then_inc(s_ch.sem, 1)

            program(act, step)

        @block.gpsimd
        def _(pool):
            start(pool, s_bd, s_r, s_fill, s_sub)

            def step(i, kind, n, bank, use):
                if kind == "lnT":
                    pool.wait_ge(s_xn.sem, s_xn.at(i, n))
                    settle(pool, m)
                    nc.gpsimd.tensor_tensor(xr(i * 4 + n), xr(i * 4 + n), m["bd_row"][:, :], ALU.add).then_inc(s_bd.sem, 1)
                if kind == "rope":
                    o = (n % 2) * GT
                    pool.wait_ge(s_t1.sem, s_t1.at(i, n))
                    pool.wait_ge(s_t2.sem, s_t2.at(i, n))
                    nc.gpsimd.tensor_tensor(t1[:, o:o + GT], t1[:, o:o + GT], sw[:, o:o + GT], ALU.add).then_inc(s_r.sem, 1)
                if kind == "fill":
                    o = (n % 4) * 512
                    pool.wait_ge(s_T.sem, s_T.ring(i, n, 4))
                    pool.wait_ge(s_sum.sem, s_sum.ring(i, n, 4))
                    settle(pool, m)
                    nc.gpsimd.memset(pr[:, o:o + 512], FILL_SELF).then_inc(s_fill.sem, 1)
                if kind == "softmax":
                    o = (n % 4) * 512
                    pool.wait_ge(s_mx.sem, s_mx.at(i, n))
                    v3 = pr[:, o:o + 512].rearrange("p (c k) -> p c k", k=S)
                    mb = mx[:, (n % 4) * 8:(n % 4) * 8 + 8].rearrange("p (c k) -> p c k", k=1).to_broadcast([P, 8, S])
                    nc.gpsimd.tensor_tensor(v3, v3, mb, ALU.subtract).then_inc(s_sub.sem, 1)

            program(pool, step)

        @block.vector
        def _(v):
            start(v, s_xn, s_xl, s_v32, s_vl, s_t1, s_t2, s_rl, s_qmh, s_pred, s_mx, s_sum, s_pl, s_ri, s_on, s_cl, s_xr, s_st)

            def step(i, kind, n, bank, use):
                if kind == "ln":
                    v.wait_ge(s_xp.sem, s_xp.ring(i, n, 2))
                    mcol = mv[:, bass.ds((i * 4 + n) * 2, 1)]
                    rcol = rstd[:, bass.ds(i * 4 + n, 1)]
                    nc.vector.tensor_scalar(xn[:, (n % 2) * D:(n % 2 + 1) * D], xr(i * 4 + n), mcol, rcol,
                                            ALU.subtract, ALU.mult).then_inc(s_xn.sem, 1)
                if kind == "ln_lo":
                    v.wait_ge(s_xh.sem, s_xh.at(i, n))
                    hi = xt_h[:, :].rearrange("p (k t) -> p k t", k=KT)[:, :, n * P:(n + 1) * P]
                    lo = xt_l[:, :].rearrange("p (k t) -> p k t", k=KT)[:, :, n * P:(n + 1) * P]
                    nc.vector.tensor_tensor(lo, bank["lnT", n, 1][:, :].rearrange("p (k t) -> p k t", k=KT), hi.bitcast(F32),
                                            ALU.subtract).then_inc(s_xl.sem, 1)
                if kind == "v32":
                    v.wait_ge(s_vp.sem, s_vp.at(i, 0))
                    bb = m["bv_row"][:, :].rearrange("p (t c) -> p t c", t=1).to_broadcast([P, 4, P])
                    nc.vector.tensor_tensor(v32[:, :].rearrange("p (t c) -> p t c", t=4),
                                            bank["v", 0, 1][:, :].rearrange("p (t c) -> p t c", t=4), bb,
                                            ALU.add).then_inc(s_v32.sem, 1)
                if kind == "v_split":
                    v.wait_ge(s_vh.sem, s_vh.at(i, 0))
                    nc.vector.tensor_tensor(va_l[:, :], v32[:, :], va_h[:, :], ALU.subtract).then_inc(s_vl.sem, 1)
                if kind == "rope":
                    o = (n % 2) * GT
                    j = n // 2
                    bias = (m["q_b"], m["k_b"])[n % 2][:, j:j + 1]
                    bias_s = (m["q_bs"], m["k_bs"])[n % 2][:, j:j + 1]
                    b3 = lambda tab: tab[:, :].rearrange("p (c s) -> p c s", c=1).to_broadcast([P, 8, S])
                    r3 = lambda ap: ap.rearrange("p (c s) -> p c s", s=S)
                    v.wait_ge(s_sw.sem, s_sw.at(i, n))
                    v.wait_ge(s_rl.sem, s_rl.ring(i, n, 2))
                    nc.vector.scalar_tensor_tensor(r3(t1[:, o:o + GT]), r3(bank["proj", n, 1][:, :]), bias, b3(m["cos_a"]),
                                                   ALU.add, ALU.mult).then_inc(s_t1.sem, 1)
                    nc.vector.scalar_tensor_tensor(r3(sw[:, o:o + GT]), r3(sw[:, o:o + GT]), bias_s, b3(m["sin_a"]),
                                                   ALU.add, ALU.mult).then_inc(s_t2.sem, 1)
                if kind == "rope_lo":
                    o, jj = (n % 2) * GT, slice(n // 2 * GT, (n // 2 + 1) * GT)
                    v.wait_ge(s_rh.sem, s_rh.at(i, n))
                    if n % 2 == 0:
                        v.wait_ge(s_qml.sem, s_qml.at(i - 1, n + 1))
                    hi, lo = ("qa_h", "qa_l") if n % 2 == 0 else ("ka_h", "ka_l")
                    nc.vector.tensor_tensor(r16[lo][:, jj], t1[:, o:o + GT], r16[hi][:, jj], ALU.subtract).then_inc(s_rl.sem, 1)
                if kind == "mask":
                    v.wait_ge(s_rl.sem, s_rl.at(i, n // 2 * 2))
                    v.wait_ge(s_S.sem, s_S.at(i, max(2 * n - 3, -1)))
                    mask_heads(lambda dst, src, h: nc.vector.tensor_scalar(dst, src, h, None, ALU.mult), "qa_h", qm_h, n
                               ).then_inc(s_qmh.sem, 1)
                if kind == "softmax":
                    o = (n % 4) * 512
                    v.wait_ge(s_S.sem, s_S.at(i, n))
                    v.wait_ge(s_fill.sem, s_fill.at(i, n))
                    cm = m["causal"][:, :].rearrange("p (c k) -> p c k", c=1).to_broadcast([P, 8, S])
                    v3 = pr[:, o:o + 512].rearrange("p (c k) -> p c k", k=S)
                    settle(v, m)
                    nc.vector.copy_predicated(v3, cm, psS[n % 2][:, :].rearrange("p (c k) -> p c k", k=S)).then_inc(s_pred.sem, 1)
                    v.wait_ge(s_pred.sem, s_pred.at(i, n))
                    v.wait_ge(s_sub.sem, s_sub.ring(i, n, 4))
                    nc.vector.tensor_reduce(mx[:, (n % 4) * 8:(n % 4) * 8 + 8], v3, AX_X, ALU.max).then_inc(s_mx.sem, 1)
                if kind == "sum":
                    j, u, g, ring = n // 4, n // 2 % 2, n % 2, n // 2 % 2
                    v.wait_ge(s_exp.sem, s_exp.at(i, n))
                    if g == 0:
                        v.wait_ge(s_ri.sem, s_ri.ring(i, n // 2, 2))
                    dst = sums[:, ring * 16:(ring + 1) * 16].rearrange("p (t g c) -> p t g c", t=2, g=2)[:, :, g, :]
                    src = pr[:, (n % 4) * 512:(n % 4 + 1) * 512].rearrange("p (t c k) -> p t c k", t=2, k=S)
                    nc.vector.tensor_reduce(dst, src, AX_X, ALU.add).then_inc(s_sum.sem, 1)
                    if g == 1:
                        v.wait_ge(s_sum.sem, s_sum.at(i, n))
                        v.wait_ge(s_on.sem, s_on.ring(i, n // 2, 2))
                        nc.vector.reciprocal(rinv[:, ring * 16:(ring + 1) * 16].rearrange("p (t b c) -> p t c b", t=2, b=2),
                                             sums[:, ring * 16:(ring + 1) * 16].rearrange("p (t c b) -> p t c b", t=2, b=2)
                                             ).then_inc(s_ri.sem, 1)
                if kind == "split_pT":
                    o = (n % 4) * 512
                    v.wait_ge(s_ph.sem, s_ph.at(i, n))
                    nc.vector.tensor_tensor(pt_l[:, o:o + 512], psP[n % 2][:, :], pt_h[:, o:o + 512],
                                            ALU.subtract).then_inc(s_pl.sem, 1)
                if kind == "norm":
                    j, u, ring = n // 2, n % 2, n % 2
                    v.wait_ge(s_O.sem, s_O.at(i, 2 * n + 1))
                    v.wait_ge(s_ri.sem, s_ri.at(i, n))
                    v.wait_ge(s_cp.sem, s_cp.at(i, -1))
                    for b in range(2):
                        rb = rinv[:, ring * 16:(ring + 1) * 16].rearrange("p (t b c x) -> p t b c x", t=2, b=2, x=1)[:, :, b, :, :]
                        dst = on[:, 2 * u * D:(2 * u + 2) * D].rearrange("p (t b j c) -> p t b j c", t=2, b=2, j=4)[:, :, b, j, :]
                        last = nc.vector.tensor_tensor(dst.rearrange("p t (c d) -> p t c d", d=HD_SELF),
                                                       psO[b][:, 0:128].rearrange("p (t c d) -> p t c d", t=2, d=HD_SELF),
                                                       rb.to_broadcast([P, 2, 4, HD_SELF]), ALU.mult)
                    last.then_inc(s_on.sem, 1)
                if kind == "dense":
                    c = (n % 2) * 512
                    v.wait_ge(s_ch.sem, s_ch.at(i, n))
                    nc.vector.tensor_tensor(ct_l[:, c:c + 512], bank[use][:, :], ct_h[:, c:c + 512].bitcast(F32),
                                            ALU.subtract).then_inc(s_cl.sem, 1)
                if kind == "y":
                    v.wait_ge(s_Y.sem, s_Y.at(i, n))
                    v.wait_ge(s_bd.sem, s_bd.at(i, n))
                    nc.vector.tensor_tensor(xr(i * 4 + n), bank[use][:, :], xr(i * 4 + n), ALU.add).then_inc(s_xr.sem, 1)
                    v.wait_ge(s_xr.sem, s_xr.at(i, n))
                    nc.vector.bn_stats(stats[:, bass.ds((i * 4 + n) * 6, 6)], xr(i * 4 + n)).then_inc(s_st.sem, 1)

            program(v, step)
            v.wait_ge(s_st.sem, s_st.at(0, TILES - 1))


def cross_keys_values(nc, at, io, m):
    WR, XT, ER, F0 = m["WR"], m["XT"], m["ER"], m["F0"]
    cosx, sinx, ident, kscr, vscr = m["cosx"], m["sinx"], m["ident"], m["kscr"], m["vscr"]
    wk_h = at("wkx_h", WR, [G * KT * P], F32R)
    wk_l = at("wkx_l", WR + 16, [G * KT * P], F32R)
    wv_h = at("wvx_h", ER, [KT * 1024], F32R)
    wv_l = at("wvx_l", ER + 16, [KT * 1024], F32R)
    ct_h = at("ctx_h", XT, [KT * GT], F32R)
    ct_l = at("ctx_l", XT + 8, [KT * GT], F32R)
    cin = at("ctx_in", F0, [4 * D], F32)
    RING = 4
    stage = at("stage_kv", F0 + 8, [RING * 512], F32)
    t1 = at("t1k", F0 + 16, [2 * GT], F32)
    sw = at("swk", F0 + 20, [2 * GT], F32)
    ks = at("k_out", F0 + 24, [2 * 2 * GT], F16)
    vs = at("v_out", F0 + 28, [2 * 512], F32)
    with ExitStack() as ctx:
        ps = [ctx.enter_context(nc.psum_tensor(f"psK{n}", [P, 512], F32)) for n in range(4)]

        def sig(name, per, step=1):
            return Signal(nc, ctx, name, per, step, base=1)

        w_in = [sig(f"k_w_in{r}", 0, 16) for r in range(RING)]
        w_hi, w_lo = sig("k_w_hi", 0), sig("k_w_lo", 0)
        c_in = [sig(f"ctx_in{t}", 1, 16) for t in range(4)]
        s_cp, s_ch, s_cl = sig("k_ctxT_psum", 4), sig("k_ctxT_hi", 4), sig("k_ctxT_lo", 4)
        s_kp, s_sw, s_t1, s_t2, s_r = sig("k_psum", 8), sig("k_swapped", 8), sig("k_cos_term", 8), sig("k_sin_term", 8), sig("k_roped", 8)
        s_rh, s_rl = sig("k_hi", 8), sig("k_lo", 8)
        s_ko = [sig(f"k_stored{r}", 4, 16) for r in range(2)]
        s_vp, s_v = sig("v_psum", 8), sig("v_sbuf", 8)
        s_vo = [sig(f"v_stored{r}", 4, 16) for r in range(2)]
        block = ctx.enter_context(nc.Block())

        steps = [("ct", t) for t in range(4)]
        for n in range(8):
            steps += [("k", n), ("v", n)]
        order = steps

        def readers(use):
            kind, n = use
            return {"ct": [(s_cl, n)], "k": [(s_t1, n)], "v": [(s_v, n)]}[kind]

        bank = Banks(ps, order, readers)
        chunks = []
        for g in range(G):
            src = io["wk"].rearrange("(k p) n -> p k n", p=P)[:, :, g * P:(g + 1) * P]
            chunks.append((src, KT, wk_h[:, g * 512:(g + 1) * 512], wk_l[:, g * 512:(g + 1) * 512]))
        for c in range(2 * KT):
            src = io["wv"][(c // 2) * P:(c // 2 + 1) * P, (c % 2) * 512:(c % 2 + 1) * 512]
            chunks.append((src, 1, wv_h[:, c * 512:(c + 1) * 512], wv_l[:, c * 512:(c + 1) * 512]))
        st = lambda c: stage[:, (c % RING) * 512:(c % RING + 1) * 512]

        @block.sync
        def _(sp):
            start(sp, *c_in, *w_in, *s_ko, *s_vo)
            def load_ctx(tile, t):
                sp.dma_start(cin[:, t * D:(t + 1) * D], io["ctx"][bass.ds(tile * P, P), :]).then_inc(c_in[t].sem, 16)

            for t in range(4):
                load_ctx(t, t)
            for c, (src, a, hi, lo) in enumerate(chunks):
                sp.wait_ge(w_lo.sem, w_lo.at(0, c - RING))
                dst = st(c) if a == 1 else st(c).rearrange("p (a b) -> p a b", a=a)
                sp.dma_start(dst, src).then_inc(w_in[c % RING].sem, 16)

            def turn(i, more):
                for kind, n in steps:
                    if kind == "ct" and more:
                        sp.wait_ge(s_cp.sem, s_cp.at(i, n))
                        load_ctx((i + 1) * 4 + n, n)
                    if kind == "k":
                        sp.wait_ge(s_rl.sem, s_rl.at(i, n))
                        sp.dma_start(kscr[n][:, :, bass.ds(i * GT, GT)],
                                     ks[:, (n % 2) * 2 * GT:(n % 2 + 1) * 2 * GT].rearrange("p (a t) -> p a t", a=2)
                                     ).then_inc(s_ko[n % 2].sem, 16)
                    if kind == "v":
                        sp.wait_ge(s_v.sem, s_v.at(i, n))
                        sp.dma_start(vscr[bass.ds(i * GT + (n // 2) * P, P), (n % 2) * 512:(n % 2 + 1) * 512],
                                     vs[:, (n % 2) * 512:(n % 2 + 1) * 512]).then_inc(s_vo[n % 2].sem, 16)

            with sp.Fori(0, GROUPS - 1) as i:
                turn(i, True)
            turn(GROUPS - 1, False)
            for r in range(2):
                sp.wait_ge(s_ko[r].sem, s_ko[r].at(GROUPS, -1))
                sp.wait_ge(s_vo[r].sem, s_vo[r].at(GROUPS, -1))

        @block.gpsimd
        def _(pool):
            start(pool, s_t2)
            with pool.Fori(0, GROUPS) as i:
                for kind, n in steps:
                    if kind == "k":
                        o = (n % 2) * GT
                        pool.wait_ge(s_sw.sem, s_sw.at(i, n))
                        settle(pool, m)
                        nc.gpsimd.tensor_tensor(sw[:, o:o + GT], sw[:, o:o + GT], sinx[:, bass.ds(i * GT, GT)],
                                                ALU.mult).then_inc(s_t2.sem, 1)

        @block.scalar
        def _(act):
            start(act, w_hi, s_ch, s_sw, s_rh, s_v)
            for c, (src, a, hi, lo) in enumerate(chunks):
                act.wait_ge(w_in[c % RING].sem, w_in[c % RING].at(0, c // RING))
                nc.scalar.activation(hi, st(c), ACT.Copy).then_inc(w_hi.sem, 1)
            with act.Fori(0, GROUPS) as i:
                for kind, n in steps:
                    if kind == "ct":
                        act.wait_ge(s_cp.sem, s_cp.at(i, n))
                        act.wait_ge(s_vp.sem, s_vp.at(i, -1))
                        dst = ct_h[:, :].rearrange("p (k t) -> p k t", k=KT)[:, :, n * P:(n + 1) * P]
                        nc.scalar.activation(dst, bank[kind, n][:, :].rearrange("p (k t) -> p k t", k=KT),
                                             ACT.Copy).then_inc(s_ch.sem, 1)
                    if kind == "k":
                        o = (n % 2) * GT
                        act.wait_ge(s_kp.sem, s_kp.at(i, n))
                        act.wait_ge(s_r.sem, s_r.ring(i, n, 2))
                        nc.scalar.activation(sw[0:64, o:o + GT], bank[kind, n][64:128, :], ACT.Copy)
                        nc.scalar.activation(sw[64:128, o:o + GT], bank[kind, n][0:64, :], ACT.Copy).then_inc(s_sw.sem, 1)
                    if kind == "v":
                        act.wait_ge(s_vp.sem, s_vp.at(i, n))
                        act.wait_ge(s_vo[n % 2].sem, s_vo[n % 2].at(i, n // 2 - 1))
                        nc.scalar.activation(vs[:, (n % 2) * 512:(n % 2 + 1) * 512], bank[kind, n][:, :],
                                             ACT.Copy).then_inc(s_v.sem, 1)
                        act.wait_ge(s_r.sem, s_r.at(i, n))
                        act.wait_ge(s_ko[n % 2].sem, s_ko[n % 2].at(i, n // 2 - 1))
                        nc.scalar.activation(ks[:, (n % 2) * 2 * GT:(n % 2) * 2 * GT + GT], t1[:, (n % 2) * GT:(n % 2 + 1) * GT],
                                             ACT.Copy).then_inc(s_rh.sem, 1)

        @block.vector
        def _(v):
            start(v, w_lo, s_cl, s_t1, s_r, s_rl)
            for c, (src, a, hi, lo) in enumerate(chunks):
                v.wait_ge(w_hi.sem, w_hi.at(0, c))
                nc.vector.tensor_tensor(lo, st(c), hi.bitcast(F32), ALU.subtract).then_inc(w_lo.sem, 1)
            with v.Fori(0, GROUPS) as i:
                for kind, n in steps:
                    if kind == "ct":
                        v.wait_ge(s_ch.sem, s_ch.at(i, n))
                        hi = ct_h[:, :].rearrange("p (k t) -> p k t", k=KT)[:, :, n * P:(n + 1) * P]
                        lo = ct_l[:, :].rearrange("p (k t) -> p k t", k=KT)[:, :, n * P:(n + 1) * P]
                        nc.vector.tensor_tensor(lo, bank[kind, n][:, :].rearrange("p (k t) -> p k t", k=KT), hi.bitcast(F32),
                                                ALU.subtract).then_inc(s_cl.sem, 1)
                    if kind == "k":
                        o = (n % 2) * GT
                        v.wait_ge(s_sw.sem, s_sw.at(i, n))
                        v.wait_ge(s_rl.sem, s_rl.ring(i, n, 2))
                        nc.vector.tensor_tensor(t1[:, o:o + GT], bank[kind, n][:, :], cosx[:, bass.ds(i * GT, GT)],
                                                ALU.mult).then_inc(s_t1.sem, 1)
                    if kind == "v":
                        o = (n % 2) * GT
                        v.wait_ge(s_t2.sem, s_t2.at(i, n))
                        v.wait_ge(s_t1.sem, s_t1.at(i, n))
                        nc.vector.tensor_tensor(t1[:, o:o + GT], t1[:, o:o + GT], sw[:, o:o + GT], ALU.add).then_inc(s_r.sem, 1)
                        v.wait_ge(s_rh.sem, s_rh.at(i, n))
                        v.wait_ge(s_r.sem, s_r.at(i, n))
                        nc.vector.tensor_tensor(ks[:, 2 * o + GT:2 * o + 2 * GT], t1[:, o:o + GT], ks[:, 2 * o:2 * o + GT],
                                                ALU.subtract).then_inc(s_rl.sem, 1)

        @block.tensor
        def _(pe):
            start(pe, s_cp, s_kp, s_vp)
            with pe.Fori(0, GROUPS) as i:
                for kind, n in steps:
                    for read, value in bank.last_reads(i, (kind, n)):
                        pe.wait_ge(read, value)
                    if kind == "ct":
                        pe.wait_ge(c_in[n].sem, c_in[n].at(i, 0))
                        for k in range(KT):
                            last = nc.tensor.transpose(bank[kind, n][:, k * P:(k + 1) * P],
                                                       cin[:, n * D + k * P:n * D + (k + 1) * P], ident[:, :])
                        last.then_inc(s_cp.sem, 1)
                    if kind == "k":
                        pe.wait_ge(w_lo.sem, w_lo.at(0, len(chunks) - 1))
                        pe.wait_ge(s_cl.sem, s_cl.at(i, 3))
                        for k in range(KT):
                            c = (n * KT + k) * P
                            last = split3(nc, bank[kind, n][:, :], wk_h[:, c:c + P], wk_l[:, c:c + P],
                                          ct_h[:, k * GT:(k + 1) * GT], ct_l[:, k * GT:(k + 1) * GT], k == 0, k == KT - 1)
                        last.then_inc(s_kp.sem, 1)
                    if kind == "v":
                        t, h = n // 2, n % 2
                        for k in range(KT):
                            c, w = k * GT + t * P, k * 1024 + h * 512
                            last = split3(nc, bank[kind, n][:, :], ct_h[:, c:c + P], ct_l[:, c:c + P],
                                          wv_h[:, w:w + 512], wv_l[:, w:w + 512], k == 0, k == KT - 1)
                        last.then_inc(s_vp.sem, 1)


def normalise_and_transpose(nc, ctx, m, xt_h, xt_l, xn, banks, tag):
    mv, rstd, stats, ident, xr = m["mv"], m["rstd"], m["stats"], m["ident"], m["xr"]
    names = ("var", "sqrt", "rstd", "xn", "xnT_psum", "xT_hi", "xT_lo")
    s_var, s_sq, s_rs, s_xn, s_xp, s_xh, s_xl = (Signal(nc, ctx, f"{tag}_{n}", 4) for n in names)
    R = len(banks)

    def halves(dst, n, i):
        return dst[:, :].rearrange("p (k t) -> p k t", k=KT)[:, :, n * P:(n + 1) * P]

    def vector(v):
        for t in range(TILES):
            nc.vector.bn_aggr(mv[:, 2 * t:2 * t + 2], stats[:, 6 * t:6 * t + 6]).then_inc(s_var.sem, 1)
        v.wait_ge(s_var.sem, TILES)
        nc.vector.tensor_scalar_add(rstd[:, :], mv[:, 1:2 * TILES:2], EPS).then_inc(s_var.sem, 1)
        v.wait_ge(s_sq.sem, 1)
        nc.vector.reciprocal(rstd[:, :], rstd[:, :]).then_inc(s_rs.sem, 1)
        v.wait_ge(s_rs.sem, 1)
        for n in range(TILES + 1):
            if n < TILES:
                if n >= 2:
                    v.wait_ge(s_xp.sem, s_xp.at(0, n - 2))
                nc.vector.tensor_scalar(xn[:, (n % 2) * D:(n % 2 + 1) * D], xr(n), mv[:, 2 * n:2 * n + 1], rstd[:, n:n + 1],
                                        ALU.subtract, ALU.mult).then_inc(s_xn.sem, 1)
            if n >= 1:
                v.wait_ge(s_xh.sem, s_xh.at(0, n - 1))
                nc.vector.tensor_tensor(halves(xt_l, n - 1, 0), banks[(n - 1) % R][:, :].rearrange("p (k t) -> p k t", k=KT),
                                        halves(xt_h, n - 1, 0).bitcast(F32), ALU.subtract).then_inc(s_xl.sem, 1)

    def scalar(act):
        act.wait_ge(s_var.sem, TILES + 1)
        nc.scalar.activation(rstd[:, :], rstd[:, :], ACT.Sqrt).then_inc(s_sq.sem, 1)
        for n in range(TILES):
            act.wait_ge(s_xp.sem, s_xp.at(0, n))
            nc.scalar.activation(halves(xt_h, n, 0), banks[n % R][:, :].rearrange("p (k t) -> p k t", k=KT),
                                 ACT.Copy).then_inc(s_xh.sem, 1)

    def tensor(pe):
        for n in range(TILES):
            pe.wait_ge(s_xn.sem, s_xn.at(0, n))
            if n >= R:
                pe.wait_ge(s_xl.sem, s_xl.at(0, n - R))
            for k in range(KT):
                c = (n % 2) * D + k * P
                last = nc.tensor.transpose(banks[n % R][:, k * P:(k + 1) * P], xn[:, c:c + P], ident[:, :])
            last.then_inc(s_xp.sem, 1)
        pe.wait_ge(s_xl.sem, s_xl.at(0, TILES - 1))

    return vector, scalar, tensor


def cross_attention(nc, at, io, m):
    WR, XT, ER, F0 = m["WR"], m["XT"], m["ER"], m["F0"]
    cosx, sinx, ident, kscr, vscr, mask8 = (m[n] for n in ("cosx", "sinx", "ident", "kscr", "vscr", "mask8"))
    xr, stats = m["xr"], m["stats"]
    xt_h = at("xtx_h", XT, [KT * T], F32R)
    xt_l = at("xtx_l", XT + 32, [KT * T], F32R)
    w1_h, w1_l = at("wq_h", WR, [KT * 512], F32R), at("wq_l", WR + 8, [KT * 512], F32R)
    w2_h, w2_l = at("wo_h", WR + 16, [HPG * D], F32R), at("wo_l", WR + 24, [HPG * D], F32R)
    ot_h, ot_l = at("ot_h", ER, [GROUP * HPG * P], F32R), at("ot_l", ER + 8, [GROUP * HPG * P], F32R)
    q_h, q_l = at("q_h", ER + 16, [2 * HPG * GT], F16), at("q_l", ER + 24, [2 * HPG * GT], F16)
    RING = 4
    stage = at("stage_x", F0, [RING * 512], F32)
    t1, sw = at("t1x", F0 + 8, [2 * GT], F32), at("swx", F0 + 12, [2 * GT], F32)
    kt = at("k_x", F0 + 16, [2 * 2 * GT], F16)
    vt = at("v_x", F0 + 20, [2 * GROUP * HD_X], F32)
    pr = at("pr_x", F0 + 24, [2 * 512], F32)
    pt = at("pt_x", F0 + 28, [2 * 512], F32)
    xn = at("xn_x", F0 + 32, [2 * D], F32)
    sums, rinv, mx = (at(f"{n}_x", F0 + 36 + 0.0625 * i, [16], F32) for i, n in enumerate(("sums", "rinv", "mx")))

    with ExitStack() as ctx:
        ps = [ctx.enter_context(nc.psum_tensor(f"psX{n}", [P, 512], F32)) for n in range(8)]
        psQ, psS, psP, psO, psY = ps[0:2], ps[2], ps[3], ps[4:6], ps[6:8]

        def sig(name, per, step=1):
            return Signal(nc, ctx, name, per, step, base=1)

        w_in = [sig(f"x_w_in{r}", 2, 16) for r in range(RING)]
        w_hi, w_lo = sig("x_w_hi", 8), sig("x_w_lo", 8)
        kv_in = [sig(f"x_kv_in{r}", 4, 16) for r in range(2)]
        s_qp, s_sw, s_t1, s_t2, s_r = (sig(f"x_{n}", 16) for n in ("q_psum", "q_swapped", "q_cos_term", "q_sin_term", "q_roped"))
        s_rh, s_rl = sig("x_q_hi", 16), sig("x_q_lo", 16)
        s_S, s_fill, s_pred, s_mx, s_sub, s_exp = (sig(f"x_{n}", 8) for n in ("scores", "filled", "kept", "max", "less_max", "exp"))
        s_sum, s_ri, s_nm, s_T, s_pt, s_O = (sig(f"x_{n}", 8) for n in ("sum", "inv_sum", "normal", "pT_psum", "pT", "oT_psum"))
        s_oh, s_ol = sig("x_oT_hi", 16), sig("x_oT_lo", 8)
        s_Y, s_xr, s_st = sig("x_out_psum", 16), sig("x_residual", 16), sig("x_stats", 16)
        ln_v, ln_a, ln_p = normalise_and_transpose(nc, ctx, m, xt_h, xt_l, xn, psQ + [psS, psP], "x_ln")
        block = ctx.enter_context(nc.Block())

        def section(tg, more):
            nxt = tg + 1
            out = [("w2", tg, 0), ("N", tg, 1), ("q", nxt, 0), ("w2", tg, 1), ("T", tg, 0), ("q", nxt, 1),
                   ("w2", tg, 2), ("rope", nxt, 0), ("PV", tg, 0), ("w2", tg, 3), ("q", nxt, 2), ("T", tg, 1),
                   ("rope", nxt, 1), ("q", nxt, 3), ("rope", nxt, 2), ("PV", tg, 1), ("Y", tg, 0),
                   ("rope", nxt, 3), ("w1", tg, 0), ("Y", tg, 1), ("w1", tg, 1), ("Y", tg, 2), ("w1", tg, 2),
                   ("w1", tg, 3), ("S", nxt, 0), ("Y", tg, 3), ("S", nxt, 1), ("N", nxt, 0)]
            return [s for s in out if (s[1] < GROUPS or more) and (s[0] != "w2" or tg == 0)
                    and (s[0] != "w1" or (tg == GROUPS - 2 and more))]

        def program(eng, step, prologue):
            prologue()
            for h in range(HPG):
                step(-1, "q", GROUPS, h, True)
                step(-1, "rope", GROUPS, h, True)
            for kind, n in (("S", 0), ("S", 1), ("N", 0)):
                step(-1, kind, GROUPS, n, True)

            def turn(i, more):
                for tg in range(GROUPS):
                    for kind, g_, n in section(tg, more):
                        step(i, kind, g_, n, more)

            with eng.Fori(0, G - 1) as i:
                turn(i, True)
            turn(G - 1, False)

        def q_event(i, tg, h):
            return (i + 1, h) if tg == GROUPS else (i, tg * HPG + h)

        def s_event(i, tg, n):
            return (i + 1, n) if tg == GROUPS else (i, 2 * tg + n)

        @block.sync
        def _(sp):
            start(sp, *w_in, *kv_in)
            def load_w1(g, c):
                sp.dma_start(stage[:, c * 512:(c + 1) * 512], io["wq"][c * P:(c + 1) * P, bass.ds(g * 512, 512)]).then_inc(w_in[c].sem, 16)

            def load_w2(g, c):
                sp.dma_start(stage[:, c * 512:(c + 1) * 512], io["wo"][bass.ds(g * 512 + c * P, P), :]).then_inc(w_in[c].sem, 16)

            def load_kv(g, tg):
                r = tg % 2
                sp.dma_start(kt[:, r * 2 * GT:(r + 1) * 2 * GT].rearrange("p (a t) -> p a t", a=2),
                             kscr[bass.ds(g, 1), :, :, tg * GT:(tg + 1) * GT].rearrange("g p a t -> (g p) a t")
                             ).then_inc(kv_in[r].sem, 16)
                sp.dma_start(vt[:, r * 512:(r + 1) * 512].rearrange("p (t d) -> p t d", t=GROUP),
                             vscr[tg * GT:(tg + 1) * GT, bass.ds(g * HD_X, HD_X)].rearrange("(t p) d -> p t d", p=P)
                             ).then_inc(kv_in[r].sem, 16)

            for c in range(RING):
                load_w1(0, c)
            load_kv(0, 0)
            for c in range(RING):
                sp.wait_ge(w_lo.sem, w_lo.at(0, c))
                load_w2(0, c)

            def turn(i, more):
                for tg in range(GROUPS):
                    if tg == 1 and more:
                        for c in range(RING):
                            sp.wait_ge(w_lo.sem, w_lo.at(i, 4 + c))
                            load_w1(i + 1, c)
                    if tg == 3 and more:
                        for c in range(RING):
                            sp.wait_ge(w_lo.sem, w_lo.at(i + 1, c))
                            load_w2(i + 1, c)
                    if tg < GROUPS - 1 or more:
                        sp.wait_ge(s_O.sem, s_O.at(i, 2 * tg - 1))
                        if tg < GROUPS - 1:
                            load_kv(i, tg + 1)
                        else:
                            load_kv(i + 1, 0)

            with sp.Fori(0, G - 1) as i:
                turn(i, True)
            turn(G - 1, False)

        @block.tensor
        def _(pe):
            start(pe, s_qp, s_S, s_T, s_O, s_Y)
            def step(i, kind, tg, n, more):
                if kind == "q":
                    j, e = q_event(i, tg, n)
                    if tg == GROUPS:
                        pe.wait_ge(w_lo.sem, w_lo.at(j, 3))
                    pe.wait_ge(s_t1.sem, s_t1.at(j, e - 2))
                    for k in range(KT):
                        c, w = k * T + (tg % GROUPS) * GT, k * 512 + n * P
                        last = split3(nc, psQ[n % 2][:, :], w1_h[:, w:w + P], w1_l[:, w:w + P],
                                      xt_h[:, c:c + GT], xt_l[:, c:c + GT], k == 0, k == KT - 1)
                    last.then_inc(s_qp.sem, 1)
                if kind == "S":
                    j, u = s_event(i, tg, n)
                    if n == 0:
                        pe.wait_ge(s_rl.sem, s_rl.at(j, 2 * u + 3))
                        pe.wait_ge(kv_in[tg % 2].sem, kv_in[tg % 2].at(j, 2 * (u // 4) + 1))
                    pe.wait_ge(s_pred.sem, s_pred.at(j, u - 1))
                    for t in range(2):
                        for hp in range(2):
                            for b in range(2):
                                tb = (2 * n + t) * 2 + b
                                q = (tg % 2) * 2048 + tb * 256 + hp * P
                                c, o = (tg % 2) * 2 * GT + tb * S, ((t * 2 + hp) * 2 + b) * S
                                last = split3(nc, psS[:, o:o + S], q_h[:, q:q + P], q_l[:, q:q + P],
                                              kt[:, c:c + S], kt[:, c + GT:c + GT + S], True, True)
                    last.then_inc(s_S.sem, 1)
                if kind == "T":
                    u = 2 * tg + n
                    pe.wait_ge(s_nm.sem, s_nm.at(i, u))
                    pe.wait_ge(s_pt.sem, s_pt.at(i, u - 1))
                    for c in range(4):
                        last = nc.tensor.transpose(psP[:, c * P:(c + 1) * P],
                                                   pr[:, n * 512 + c * P:n * 512 + (c + 1) * P], ident[:, :])
                    last.then_inc(s_T.sem, 1)
                if kind == "PV":
                    u = 2 * tg + n
                    pe.wait_ge(s_pt.sem, s_pt.at(i, u))
                    pe.wait_ge(s_ol.sem, s_ol.at(i, u - 1))
                    for b in range(2):
                        for t in range(2):
                            rows = slice(b * S, (b + 1) * S)
                            vc = (tg % 2) * 512 + (2 * n + t) * HD_X
                            last = nc.tensor.matmul(psO[b][:, t * 256:(t + 1) * 256], vt[rows, vc:vc + HD_X],
                                                    pt[rows, n * 512 + t * 256:n * 512 + (t + 1) * 256], start=True, stop=True)
                    last.then_inc(s_O.sem, 1)
                if kind == "Y":
                    y = tg * 4 + n
                    pe.wait_ge(s_ol.sem, s_ol.at(i, 2 * tg + n // 2))
                    if y == 0:
                        pe.wait_ge(w_lo.sem, w_lo.at(i, 7))
                    pe.wait_ge(s_xr.sem, s_xr.at(i, max(y - 2, -1)))
                    for h in range(HPG):
                        c = (n * HPG + h) * P
                        last = split3(nc, psY[n % 2][:, :], ot_h[:, c:c + P], ot_l[:, c:c + P],
                                      w2_h[:, h * D:(h + 1) * D], w2_l[:, h * D:(h + 1) * D], h == 0, h == HPG - 1)
                    last.then_inc(s_Y.sem, 1)

            program(pe, step, lambda: ln_p(pe))

        def split_hi(act, turn, load, dst, c):
            act.wait_ge(w_in[c].sem, w_in[c].at(turn, load))
            nc.scalar.activation(dst[:, c * 512:(c + 1) * 512], stage[:, c * 512:(c + 1) * 512], ACT.Copy).then_inc(w_hi.sem, 1)

        def split_lo(v, turn, load, hi, lo, c):
            v.wait_ge(w_hi.sem, w_hi.at(turn, load * RING + c))
            sl = slice(c * 512, (c + 1) * 512)
            nc.vector.tensor_tensor(lo[:, sl], stage[:, sl], hi[:, sl].bitcast(F32), ALU.subtract).then_inc(w_lo.sem, 1)

        @block.scalar
        def _(act):
            start(act, w_hi, s_sw, s_rh, s_exp, s_pt, s_oh)
            def step(i, kind, tg, n, more):
                if kind == "w1":
                    act.wait_ge(s_qp.sem, s_qp.at(i, 15))
                    split_hi(act, i + 1, 0, w1_h, n)
                if kind == "w2":
                    act.wait_ge(s_Y.sem, s_Y.at(i, -1))
                    split_hi(act, i, 1, w2_h, n)
                if kind == "q":
                    j, e = q_event(i, tg, n)
                    o = (n % 2) * GT
                    act.wait_ge(s_qp.sem, s_qp.at(j, e))
                    act.wait_ge(s_r.sem, s_r.at(j, e - 2))
                    nc.scalar.activation(sw[0:64, o:o + GT], psQ[n % 2][64:128, :], ACT.Copy)
                    nc.scalar.activation(sw[64:128, o:o + GT], psQ[n % 2][0:64, :], ACT.Copy).then_inc(s_sw.sem, 1)
                if kind == "rope":
                    j, e = q_event(i, tg, n)
                    act.wait_ge(s_r.sem, s_r.at(j, e))
                    if not (type(i) is int and i < 0):
                        act.wait_ge(s_S.sem, s_S.at(i, 2 * (tg - 1) - 1))
                    dst = q_h[:, (tg % 2) * 2048:(tg % 2 + 1) * 2048].rearrange("p (c h q) -> p c h q", h=HPG, q=S)
                    nc.scalar.activation(dst[:, :, n, :], t1[:, (n % 2) * GT:(n % 2 + 1) * GT].rearrange("p (c q) -> p c q", q=S),
                                         ACT.Copy).then_inc(s_rh.sem, 1)
                if kind == "S":
                    j, u = s_event(i, tg, n)
                    act.wait_ge(s_sub.sem, s_sub.at(j, u))
                    nc.scalar.activation(pr[:, n * 512:(n + 1) * 512], pr[:, n * 512:(n + 1) * 512], ACT.Exp,
                                         scale=SCALE_X).then_inc(s_exp.sem, 1)
                if kind == "T":
                    u = 2 * tg + n
                    act.wait_ge(s_T.sem, s_T.at(i, u))
                    act.wait_ge(s_O.sem, s_O.at(i, max(u - 2, -1)))
                    nc.scalar.activation(pt[:, n * 512:(n + 1) * 512], psP[:, :], ACT.Copy).then_inc(s_pt.sem, 1)
                if kind == "PV":
                    u = 2 * tg + n
                    act.wait_ge(s_O.sem, s_O.at(i, u))
                    act.wait_ge(s_Y.sem, s_Y.at(i, 4 * tg - 1))
                    for b in range(2):
                        dst = ot_h[:, n * 1024:(n + 1) * 1024].rearrange("p (c q) -> p c q", q=P)[:, :, b * S:(b + 1) * S]
                        nc.scalar.activation(dst, psO[b][:, :].rearrange("p (c q) -> p c q", q=S), ACT.Copy).then_inc(s_oh.sem, 1)

            def prologue():
                ln_a(act)
                for c in range(RING):
                    split_hi(act, 0, 0, w1_h, c)

            program(act, step, prologue)

        @block.gpsimd
        def _(pool):
            start(pool, s_t2, s_fill, s_sub)
            def step(i, kind, tg, n, more):
                if kind == "q":
                    j, e = q_event(i, tg, n)
                    o = (n % 2) * GT
                    c = (tg % GROUPS) * GT
                    pool.wait_ge(s_sw.sem, s_sw.at(j, e))
                    nc.gpsimd.tensor_tensor(sw[:, o:o + GT], sw[:, o:o + GT], sinx[:, c:c + GT], ALU.mult).then_inc(s_t2.sem, 1)
                if kind == "S":
                    j, u = s_event(i, tg, n)
                    pool.wait_ge(s_T.sem, s_T.ring(j, u, 2))
                    settle(pool, m)
                    nc.gpsimd.memset(pr[:, n * 512:(n + 1) * 512], FILL_X).then_inc(s_fill.sem, 1)
                    pool.wait_ge(s_mx.sem, s_mx.at(j, u))
                    v3 = pr[:, n * 512:(n + 1) * 512].rearrange("p (c k) -> p c k", k=S)
                    mb = mx[:, n * 8:n * 8 + 8].rearrange("p (c k) -> p c k", k=1).to_broadcast([P, 8, S])
                    nc.gpsimd.tensor_tensor(v3, v3, mb, ALU.subtract).then_inc(s_sub.sem, 1)

            program(pool, step, lambda: None)

        @block.vector
        def _(v):
            start(v, w_lo, s_t1, s_r, s_rl, s_pred, s_mx, s_sum, s_ri, s_nm, s_ol, s_xr, s_st)
            def step(i, kind, tg, n, more):
                if kind == "w1":
                    split_lo(v, i + 1, 0, w1_h, w1_l, n)
                if kind == "w2":
                    split_lo(v, i, 1, w2_h, w2_l, n)
                if kind == "q":
                    j, e = q_event(i, tg, n)
                    o, c = (n % 2) * GT, (tg % GROUPS) * GT
                    v.wait_ge(s_sw.sem, s_sw.at(j, e))
                    v.wait_ge(s_rl.sem, s_rl.at(j, e - 2))
                    nc.vector.tensor_tensor(t1[:, o:o + GT], psQ[n % 2][:, :], cosx[:, c:c + GT], ALU.mult).then_inc(s_t1.sem, 1)
                if kind == "rope":
                    j, e = q_event(i, tg, n)
                    o = (n % 2) * GT
                    v.wait_ge(s_t2.sem, s_t2.at(j, e))
                    v.wait_ge(s_t1.sem, s_t1.at(j, e))
                    nc.vector.tensor_tensor(t1[:, o:o + GT], t1[:, o:o + GT], sw[:, o:o + GT], ALU.add).then_inc(s_r.sem, 1)
                    sl = slice((tg % 2) * 2048, (tg % 2 + 1) * 2048)
                    hi = q_h[:, sl].rearrange("p (c h q) -> p c h q", h=HPG, q=S)[:, :, n, :]
                    lo = q_l[:, sl].rearrange("p (c h q) -> p c h q", h=HPG, q=S)[:, :, n, :]
                    v.wait_ge(s_rh.sem, s_rh.at(j, e))
                    v.wait_ge(s_r.sem, s_r.at(j, e))
                    nc.vector.tensor_tensor(lo, t1[:, o:o + GT].rearrange("p (c q) -> p c q", q=S), hi,
                                            ALU.subtract).then_inc(s_rl.sem, 1)
                if kind == "S":
                    j, u = s_event(i, tg, n)
                    c = (tg % GROUPS * 8 + n * 4) * S
                    mk = mask8[:, c:c + 256].rearrange("p (t x c) -> p t x c", t=2, x=1).to_broadcast([P, 2, 2, P])
                    p4 = lambda ap: ap.rearrange("p (t x c) -> p t x c", t=2, x=2)
                    v.wait_ge(s_S.sem, s_S.at(j, u))
                    v.wait_ge(s_fill.sem, s_fill.at(j, u))
                    settle(v, m)
                    nc.vector.copy_predicated(p4(pr[:, n * 512:(n + 1) * 512]), mk, p4(psS[:, :])).then_inc(s_pred.sem, 1)
                    v.wait_ge(s_pred.sem, s_pred.at(j, u))
                    v.wait_ge(s_sub.sem, s_sub.ring(j, u, 2))
                    nc.vector.tensor_reduce(mx[:, n * 8:n * 8 + 8], pr[:, n * 512:(n + 1) * 512].rearrange("p (c k) -> p c k", k=S),
                                            AX_X, ALU.max).then_inc(s_mx.sem, 1)
                if kind == "N":
                    j, u = s_event(i, tg, n)
                    v3 = pr[:, n * 512:(n + 1) * 512].rearrange("p (c k) -> p c k", k=S)
                    v.wait_ge(s_exp.sem, s_exp.at(j, u))
                    nc.vector.tensor_reduce(sums[:, n * 8:n * 8 + 8], v3, AX_X, ALU.add).then_inc(s_sum.sem, 1)
                    v.wait_ge(s_sum.sem, s_sum.at(j, u))
                    nc.vector.reciprocal(rinv[:, n * 8:n * 8 + 8], sums[:, n * 8:n * 8 + 8]).then_inc(s_ri.sem, 1)
                    v.wait_ge(s_ri.sem, s_ri.at(j, u))
                    rb = rinv[:, n * 8:n * 8 + 8].rearrange("p (c k) -> p c k", k=1).to_broadcast([P, 8, S])
                    nc.vector.tensor_tensor(v3, v3, rb, ALU.mult).then_inc(s_nm.sem, 1)
                if kind == "PV":
                    u = 2 * tg + n
                    for b in range(2):
                        v.wait_ge(s_oh.sem, s_oh.at(i, 2 * u + b))
                        sl = slice(n * 1024, (n + 1) * 1024)
                        hi = ot_h[:, sl].rearrange("p (c q) -> p c q", q=P)[:, :, b * S:(b + 1) * S]
                        lo = ot_l[:, sl].rearrange("p (c q) -> p c q", q=P)[:, :, b * S:(b + 1) * S]
                        last = nc.vector.tensor_tensor(lo, psO[b][:, :].rearrange("p (c q) -> p c q", q=S), hi.bitcast(F32),
                                                       ALU.subtract)
                    last.then_inc(s_ol.sem, 1)
                if kind == "Y":
                    y = tg * 4 + n
                    v.wait_ge(s_Y.sem, s_Y.at(i, y))
                    nc.vector.tensor_tensor(xr(y), psY[n % 2][:, :], xr(y), ALU.add).then_inc(s_xr.sem, 1)
                    if not more:
                        v.wait_ge(s_xr.sem, s_xr.at(i, y))
                        nc.vector.bn_stats(stats[:, 6 * y:6 * y + 6], xr(y)).then_inc(s_st.sem, 1)

            def prologue():
                ln_v(v)
                for c in range(RING):
                    split_lo(v, 0, 0, w1_h, w1_l, c)

            program(v, step, prologue)
            v.wait_ge(s_st.sem, s_st.at(0, TILES - 1))


def feed_forward(nc, at, io, out, m):
    WR, XT, ER, F0 = m["WR"], m["XT"], m["ER"], m["F0"]
    xr, x_res = m["xr"], m["x_res"]
    xt_h = at("xtf_h", XT, [KT * T], F32R)
    xt_l = at("xtf_l", XT + 32, [KT * T], F32R)
    wgu_h, wgu_l = at("wgu_h", WR, [2 * KT * 256], F32R), at("wgu_l", WR + 8, [2 * KT * 256], F32R)
    wdn_h, wdn_l = at("wdn_h", WR + 16, [2 * D], F32R), at("wdn_l", WR + 20, [2 * D], F32R)
    h_h, h_l = at("h_h", ER, [2 * 2 * GT], F32R), at("h_l", ER + 8, [2 * 2 * GT], F32R)
    NCH = 6
    q_st = at("q_stage", F0, [NCH * 512], I32)
    s_st = at("s_stage", F0 + 12, [NCH * 512], F32)
    w32 = at("w32", F0 + 24, [2 * 512], F32)
    xn = at("xn_f", F0 + 28, [2 * D], F32)
    sg = at("silu", F0 + 32, [2 * GT], F32)
    hf = at("hf", F0 + 36, [2 * GT], F32)

    with ExitStack() as ctx:
        ps = [ctx.enter_context(nc.psum_tensor(f"psF{n}", [P, 512], F32)) for n in range(8)]
        psG, psU, psY = ps[0:2], ps[2:4], ps[4:6]

        def sig(name, per, step=1):
            return Signal(nc, ctx, name, per, step, base=1)

        w_in = [sig(f"f_w_in{c}", 2, 16) for c in range(NCH)]
        w_32, w_hi, w_lo = sig("f_w", NCH), sig("f_w_hi", NCH), sig("f_w_lo", NCH)
        s_gp, s_up, s_sg, s_h, s_hh, s_hl = (sig(f"f_{n}", 8) for n in ("gate", "up", "silu", "hidden", "hidden_hi", "hidden_lo"))
        s_Y, s_xr = sig("f_out_psum", 16), sig("f_residual", 16)
        s_out = Signal(nc, ctx, "stored", 0, 16)
        ln_v, ln_a, ln_p = normalise_and_transpose(nc, ctx, m, xt_h, xt_l, xn, ps[0:4], "f_ln")
        block = ctx.enter_context(nc.Block())

        def section(tg, more):
            out_ = [("Y", tg, 0), ("Y", tg, 1), ("gu", tg + 1, 1), ("Y", tg, 2), ("Y", tg, 3)]
            if tg < GROUPS - 1 or more:
                out_.insert(0, ("gu", tg + 1, 0))
            else:
                out_.remove(("gu", tg + 1, 1))
            if tg == GROUPS - 1 and more:
                out_ = [("Y", tg, 0), ("w", 0, 0), ("Y", tg, 1), ("Y", tg, 2), ("Y", tg, 3), ("wd", 0, 0),
                        ("gu", tg + 1, 0), ("gu", tg + 1, 1)]
            return out_

        def program(eng, step, prologue):
            prologue()
            for n in range(2):
                step(-1, "gu", GROUPS, n, True)

            def turn(i, more):
                for tg in range(GROUPS):
                    for kind, g_, n in section(tg, more):
                        step(i, kind, g_, n, more)

            with eng.Fori(0, FCH - 1) as i:
                turn(i, True)
            turn(FCH - 1, False)

        def event(i, tg, n):
            return (i + 1, n) if tg == GROUPS else (i, tg * 2 + n)

        def halves(c):
            h, l = (wgu_h, wgu_l) if c < 4 else (wdn_h, wdn_l)
            o = c * 512 if c < 4 else (c - 4) * 512
            return h[:, o:o + 512], l[:, o:o + 512]

        @block.sync
        def _(sp):
            start(sp, *w_in)
            def load(i, c):
                o = slice(c * 512, (c + 1) * 512)
                if c < 4:
                    q, s_ = (("gate_q", "gate_s"), ("up_q", "up_s"))[c // 2]
                    k = 2 * (c % 2)
                    sp.dma_start(q_st[:, o].rearrange("p (k n) -> p k n", k=2),
                                 io[q].rearrange("(k p) n -> p k n", p=P)[:, k:k + 2, bass.ds(i * 256, 256)]).then_inc(w_in[c].sem, 16)
                    sp.dma_start(s_st[:, o].rearrange("p (k n) -> p k n", k=2),
                                 io[s_][k:k + 2, bass.ds(i * 256, 256)].partition_broadcast(P)).then_inc(w_in[c].sem, 16)
                else:
                    sp.dma_start(q_st[:, o], io["down_q"][bass.ds(i * 256 + (c - 4) * P, P), :]).then_inc(w_in[c].sem, 16)
                    sp.dma_start(s_st[:, o], io["down_s"][bass.ds(i * 2 + (c - 4), 1), :].rearrange("a n -> (a n)").partition_broadcast(P)
                                 ).then_inc(w_in[c].sem, 16)

            for c in range(NCH):
                load(0, c)
            with sp.Fori(0, FCH - 1) as i:
                for c in range(NCH):
                    sp.wait_ge(w_32.sem, w_32.at(i, c))
                    load(i + 1, c)
            for y in range(TILES):
                sp.wait_ge(s_xr.sem, s_xr.at(FCH - 1, y))
                sp.dma_start(out[y * P:(y + 1) * P, :], xr(y)).then_inc(s_out.sem, 16)
            sp.wait_ge(s_out.sem, TILES * 16)

        @block.tensor
        def _(pe):
            start(pe, s_gp, s_up, s_Y)
            def step(i, kind, tg, n, more):
                if kind == "gu":
                    j, e = event(i, tg, n)
                    if tg == GROUPS:
                        pe.wait_ge(w_lo.sem, w_lo.at(j, 3))
                    pe.wait_ge(s_h.sem, s_h.at(j, e - 2))
                    for bank, w0, s_ in ((psG[n], 0, s_gp), (psU[n], 1024, s_up)):
                        for k in range(KT):
                            c, w = k * T + (tg % GROUPS) * GT, w0 + k * 256 + n * P
                            last = split3(nc, bank[:, :], wgu_h[:, w:w + P], wgu_l[:, w:w + P],
                                          xt_h[:, c:c + GT], xt_l[:, c:c + GT], k == 0, k == KT - 1)
                        last.then_inc(s_.sem, 1)
                if kind == "Y":
                    y = tg * 4 + n
                    if n == 0:
                        pe.wait_ge(s_hl.sem, s_hl.at(i, tg * 2 + 1))
                        pe.wait_ge(w_lo.sem, w_lo.at(i, NCH - 1))
                    pe.wait_ge(s_xr.sem, s_xr.at(i, max(y - 2, -1)))
                    for k in range(2):
                        c = (tg % 2) * 1024 + k * GT + n * P
                        last = split3(nc, psY[n % 2][:, :], h_h[:, c:c + P], h_l[:, c:c + P],
                                      wdn_h[:, k * D:(k + 1) * D], wdn_l[:, k * D:(k + 1) * D], k == 0, k == 1)
                    last.then_inc(s_Y.sem, 1)

            program(pe, step, lambda: ln_p(pe))

        @block.scalar
        def _(act):
            start(act, w_hi, s_sg, s_hh)
            def split_hi(turn, chunks):
                for c in chunks:
                    act.wait_ge(w_32.sem, w_32.at(turn, c))
                    nc.scalar.activation(halves(c)[0], w32[:, (c % 2) * 512:(c % 2 + 1) * 512], ACT.Copy).then_inc(w_hi.sem, 1)

            def step(i, kind, tg, n, more):
                if kind == "w":
                    act.wait_ge(s_up.sem, s_up.at(i, 7))
                    split_hi(i + 1, range(4))
                if kind == "wd":
                    act.wait_ge(s_Y.sem, s_Y.at(i, 15))
                    split_hi(i + 1, range(4, NCH))
                if kind == "gu":
                    j, e = event(i, tg, n)
                    o = n * GT
                    act.wait_ge(s_gp.sem, s_gp.at(j, e))
                    act.wait_ge(s_h.sem, s_h.at(j, e - 2))
                    nc.scalar.activation(sg[:, o:o + GT], psG[n][:, :], ACT.Silu).then_inc(s_sg.sem, 1)
                    act.wait_ge(s_h.sem, s_h.at(j, e))
                    if not (type(i) is int and i < 0):
                        act.wait_ge(s_Y.sem, s_Y.at(i, 4 * (tg - 1) - 1))
                    c = (tg % 2) * 1024 + n * GT
                    nc.scalar.activation(h_h[:, c:c + GT], hf[:, o:o + GT], ACT.Copy).then_inc(s_hh.sem, 1)

            def prologue():
                ln_a(act)
                split_hi(0, range(NCH))

            program(act, step, prologue)

        @block.vector
        def _(v):
            start(v, w_32, w_lo, s_h, s_hl, s_xr)
            def dequantise(turn, chunks):
                for c in chunks:
                    sl, w = slice(c * 512, (c + 1) * 512), w32[:, (c % 2) * 512:(c % 2 + 1) * 512]
                    v.wait_ge(w_in[c].sem, w_in[c].at(turn, 1))
                    if c >= 2:
                        v.wait_ge(w_lo.sem, w_lo.at(turn, c - 2))
                    nc.vector.tensor_tensor(w, q_st[:, sl], s_st[:, sl], ALU.mult).then_inc(w_32.sem, 1)
                    v.wait_ge(w_hi.sem, w_hi.at(turn, c))
                    hi, lo = halves(c)
                    nc.vector.tensor_tensor(lo, w, hi.bitcast(F32), ALU.subtract).then_inc(w_lo.sem, 1)

            def step(i, kind, tg, n, more):
                if kind == "w":
                    dequantise(i + 1, range(4))
                if kind == "wd":
                    dequantise(i + 1, range(4, NCH))
                if kind == "gu":
                    j, e = event(i, tg, n)
                    o = n * GT
                    v.wait_ge(s_sg.sem, s_sg.at(j, e))
                    v.wait_ge(s_up.sem, s_up.at(j, e))
                    nc.vector.tensor_tensor(hf[:, o:o + GT], psU[n][:, :], sg[:, o:o + GT], ALU.mult).then_inc(s_h.sem, 1)
                    v.wait_ge(s_hh.sem, s_hh.at(j, e))
                    c = (tg % 2) * 1024 + n * GT
                    nc.vector.tensor_tensor(h_l[:, c:c + GT], hf[:, o:o + GT], h_h[:, c:c + GT].bitcast(F32),
                                            ALU.subtract).then_inc(s_hl.sem, 1)
                if kind == "Y":
                    y = tg * 4 + n
                    v.wait_ge(s_Y.sem, s_Y.at(i, y))
                    nc.vector.tensor_tensor(xr(y), psY[n % 2][:, :], xr(y), ALU.add).then_inc(s_xr.sem, 1)

            def prologue():
                ln_v(v)
                dequantise(0, range(NCH))

            program(v, step, prologue)


def kernel(**inputs):
    import concourse.bacc as bacc
    from concourse.bass_utils import run_bass_kernel_spmd as run

    a = {n: np.asarray(v) for n, v in inputs.items()}
    p = np.arange(P)
    half, head, d8 = p // 64, p % 64 // 8, p % 8
    g = lambda j: 2 * j + head // HPG
    q_rows = np.concatenate([g(j) * 96 + head % HPG * 16 + half * 8 + d8 for j in range(4)])
    k_rows = np.concatenate([g(j) * 96 + 64 + half * 8 + d8 for j in range(4)])
    v_rows = (np.arange(G)[:, None] * 96 + 80 + np.arange(16)[None, :]).ravel()
    rows = np.concatenate([q_rows, k_rows, v_rows])
    d_rows = np.concatenate([((gh * 4 + p // 32) * 4 + p % 32 // 16 * 2 + par) * 16 + p % 16
                             for gh in range(2) for par in range(2)])
    swap = (p + 64) % P
    b = a["L0_attn_b_qkv"]
    bq, bk = b[q_rows].reshape(4, P).T, b[k_rows].reshape(4, P).T
    hmask = (head[:, None] == np.arange(8)[None, :]).astype(np.float32)
    iota = (p[:, None] + P * np.arange(4)[None, :]).astype(np.float32)
    small = np.concatenate([bq, bk, bq[swap], bk[swap], hmask, iota], axis=1).astype(np.float32)

    def angles(n, dim, base):
        inv = np.float32(1.0) / np.float32(base) ** (np.arange(0, dim, 2, dtype=np.float32) / np.float32(dim))
        return np.arange(n, dtype=np.float32)[:, None] * inv[None, :].astype(np.float32)

    an = angles(S, HD_SELF, 1000000.0).T[d8]
    sign = np.where(half == 0, -1.0, 1.0).astype(np.float32)[:, None]
    rope_self = np.stack([np.cos(an), sign * np.sin(an)]).astype(np.float32)
    ax = angles(MAX_POS, HD_X, 10000.0)
    rope_x = np.concatenate([np.cos(ax), np.cos(ax), -np.sin(ax), np.sin(ax)], axis=1).astype(np.float32)
    causal = (np.arange(S)[None, :] <= (p % S)[:, None]).astype(np.int32)

    arrays = {
        "x": a["x"].reshape(T, D), "ctx": a["ctx_4096"].reshape(T, D), "pos": a["pos_BxS2"].reshape(T),
        "mask": a["mask_BxSxS2_ik0"], "w_qkv": a["L0_attn_w_qkv"].T[:, rows], "b_v": b[v_rows],
        "w_dense": a["L0_attn_w_dense"].T[d_rows], "b_dense": a["L0_attn_b_dense"],
        "wq": a["L0_xattn_Wq"], "wk": a["L0_xattn_Wk"], "wv": a["L0_xattn_Wv"], "wo": a["L0_xattn_Wo"],
        "gate_q": a["L0_ffn_gate_q"].T, "gate_s": a["L0_ffn_gate_s"].T, "up_q": a["L0_ffn_up_q"].T,
        "up_s": a["L0_ffn_up_s"].T, "down_q": a["L0_ffn_down_q"].T, "down_s": a["L0_ffn_down_s"].T,
        "small": small, "ident": np.eye(P, dtype=np.float32), "rope_self": rope_self, "rope_x": rope_x,
        "causal": causal,
    }
    arrays = {n: np.ascontiguousarray(v) for n, v in arrays.items()}
    nc = bacc.Bacc("TRN2", target_bir_lowering=False, num_devices=1, dynamic_dma_scratch_size=1024)
    io = {n: nc.dram_tensor("in_" + n, v.shape, mybir.dt.from_np(v.dtype), kind="ExternalInput").ap()
          for n, v in arrays.items()}
    out = nc.dram_tensor("out_x", (T, D), F32, kind="ExternalOutput").ap()
    build(nc, io, out)
    r = run(nc, [{"in_" + n: v for n, v in arrays.items()}], core_ids=[0])
    return r.results[0]["out_x"].reshape(B, S, D)
```

```python
from contextlib import ExitStack

import numpy as np

import concourse.bass as bass
from concourse import mybir

F32 = mybir.dt.float32
F32R = mybir.dt.float32r
F16 = mybir.dt.float16
I32 = mybir.dt.int32
U8 = mybir.dt.uint8
ALU = mybir.AluOpType
ACT = mybir.ActivationFunctionType
AX_X = mybir.AxisListType.X

P = 128
B, S, D = 32, 64, 512
T = B * S
TILES = T // P
GROUP = 4
GROUPS = TILES // GROUP
GT = GROUP * P
KT = D // P
G = 8
HPG = 4
HD_SELF, HD_X = 16, 128
SCALE_SELF = 1.0 / HD_SELF
SCALE_X = float(np.float32(1.0) / np.sqrt(np.float32(HD_X)))
FILL_SELF = float(np.finfo(np.float32).min)
FILL_X = -1.0e9 / SCALE_X
MAX_POS = 512
FF = 1792
FCH = FF // 256
EPS = 1e-5


class Signal:

    def __init__(self, nc, ctx, name, per=0, step=1, base=0):
        self.sem = ctx.enter_context(nc.semaphore(name))
        self.per, self.step, self.base = per, step, base

    def at(self, turn, n):
        value = (turn * self.per + n + 1 + self.base) * self.step
        return max(value, self.base * self.step) if type(value) is int else value

    def ring(self, turn, n, slots):
        return self.at(turn, max(n - slots, -1))

    def back(self, turn, n, slots):
        assert self.base >= slots
        return self.at(turn, n - slots)


def start(eng, *signals):
    for signal in signals:
        assert signal.base > 0
        eng.sem_inc(signal.sem, signal.base * signal.step)


class Banks:

    def __init__(self, banks, order, readers):
        self.banks, self.order, self.readers = banks, order, readers

    def __getitem__(self, use):
        return self.banks[self.order.index(use) % len(self.banks)]

    def last_reads(self, turn, use):
        turn = turn - use[2]
        n = self.order.index(use) - len(self.banks)
        if n >= 0:
            signal, event, ahead = self.readers(self.order[n])
            return [(signal.sem, signal.at(turn + ahead, event))]
        found = {}
        for old in self.order[-len(self.banks):]:
            signal, _, ahead = self.readers(old)
            found[signal.sem.name] = (signal.sem, signal.at(turn + ahead, -1))
        return list(found.values())


CONSTS = 6


def settle(eng, m):
    eng.sem_inc(m["settled"][eng.engine].sem, 1)


def split3(nc, out, wh, wl, xh, xl, first, last):
    nc.tensor.matmul(out, wh, xh, start=first, stop=False)
    nc.tensor.matmul(out, wh, xl, start=False, stop=False)
    return nc.tensor.matmul(out, wl, xh, start=False, stop=last)


def build(nc, io, out):
    KB = 1024
    BASE = 2 * KB
    outer = ExitStack()
    with outer:
        def at(name, kb, shape, dt):
            n = 1
            for s in shape:
                n *= s
            assert BASE + kb * KB + n * mybir.dt.size(dt) <= 229368, name
            return nc.alloc_sbuf_tensor_at(name, [P, n], dt, offset=int(BASE + kb * KB))

        XR, XT, WR, ER, FR = 0, 32, 96, 128, 160
        x_res = at("x_res", XR, [TILES * D], F32)
        ident = at("ident", FR, [P], F32)
        small = at("small", FR + 0.5, [128], F32)
        mask8 = at("mask8", FR + 1, [B * S], U8)
        cosx = at("cosx", FR + 3, [T], F32)
        sinx = at("sinx", FR + 11, [T], F32)
        F0 = FR + 19
        stats = at("stats", FR + 61, [TILES * 6], F32)
        mv = at("mv", FR + 61.375, [TILES * 2], F32)
        rstd = at("rstd", FR + 61.5, [TILES], F32)
        kscr = nc.dram_tensor("k_scratch", (G, P, 2, T), F16, kind="Internal").ap()
        vscr = nc.dram_tensor("v_scratch", (T, G * HD_X), F32, kind="Internal").ap()

        q_b = small[:, 0:4]
        k_b = small[:, 4:8]
        q_bs = small[:, 8:12]
        k_bs = small[:, 12:16]
        hmask = small[:, 16:24]
        iota = small[:, 24:28]
        v_b = small[:, 28:29]
        xr = lambda tile: x_res[:, bass.ds(tile * D, D)]

        wqk_h = at("wqk_h", WR, [KT * 1024], F32R)
        wqk_l = at("wqk_l", WR + 16, [KT * 1024], F32R)
        wd_h = at("wd_h", XT, [KT * D], F32R)
        wd_l = at("wd_l", XT + 8, [KT * D], F32R)
        wv_h = at("wv_h", XT + 48, [KT * P], F32R)
        wv_l = at("wv_l", XT + 50, [KT * P], F32R)
        cos_a = at("cos_a", F0, [S], F32)
        sin_a = at("sin_a", F0 + 0.25, [S], F32)
        causal = at("causal", F0 + 0.5, [S], I32)
        bd_row = at("bd_row", F0 + 1.25, [D], F32)
        A0 = F0 + 3.25

        consts_in = Signal(nc, outer, "consts_in", step=16)

        settled = {e.engine: Signal(nc, outer, n) for e, n in (
            (nc.gpsimd, "settled_pool"), (nc.vector, "settled_dve"), (nc.sync, "settled_sp"))}

        with ExitStack() as ctx:
            NCH = 15
            RING = 8
            TABLE = (3, 5, 7, 9)
            stage = at("stage0", XT + 32, [RING * 512], F32)
            pos_i = at("pos_i", ER + 8, [T], I32)
            pos_f = at("pos_f", ER + 16, [T], F32)
            pos_n = at("pos_n", A0, [T], F32)
            onehot = at("onehot", XT + 16, [4 * 512], F32R)
            tab_h = at("tab_h", XT + 24, [1024], F32R)
            tab_l = at("tab_l", XT + 28, [1024], F32R)
            mask_i = at("mask_i", ER + 24, [T], I32)
            psT = [ctx.enter_context(nc.psum_tensor(f"psT{n}", [P, 512], F32)) for n in range(4)]
            loaded = Signal(nc, ctx, "setup_loaded", step=16)
            pos_in = Signal(nc, ctx, "pos_in", step=16)
            mask_in = Signal(nc, ctx, "mask_in", step=16)
            x_in = [Signal(nc, ctx, f"x_in{q}", step=16) for q in range(GROUPS)]
            w_in = [Signal(nc, ctx, f"w_in{r}", step=16) for r in range(RING)]
            w_hi = Signal(nc, ctx, "w_hi")
            w_lo = Signal(nc, ctx, "w_lo")
            poss = Signal(nc, ctx, "pos_ready")
            oh = Signal(nc, ctx, "onehot_ready")
            tabp = Signal(nc, ctx, "tables_in_psum")
            cosd = Signal(nc, ctx, "cos_ready")
            sind = Signal(nc, ctx, "sin_ready")
            dve = Signal(nc, ctx, "stats_step")
            rt = Signal(nc, ctx, "sqrt_ready")
            block = ctx.enter_context(nc.Block())

            chunks = []
            tabv = io["rope_x"].rearrange("(k p) n -> p k n", p=P)
            for k2 in range(2):
                chunks.append((tabv[:, 2 * k2:2 * k2 + 2, :], (2, 256), tab_h[:, k2 * 512:k2 * 512 + 512],
                               tab_l[:, k2 * 512:k2 * 512 + 512]))
            for k in range(KT):
                for h in range(2):
                    c = k * 1024 + h * 512
                    chunks.append((io["w_qkv"][k * P:(k + 1) * P, h * 512:(h + 1) * 512], None,
                                   wqk_h[:, c:c + 512], wqk_l[:, c:c + 512]))
            chunks.append((io["w_qkv"].rearrange("(k p) n -> p k n", p=P)[:, :, 1024:1152], (KT, P),
                           wv_h[:, :], wv_l[:, :]))
            for k in range(KT):
                chunks.append((io["w_dense"][k * P:(k + 1) * P, :], None,
                               wd_h[:, k * D:(k + 1) * D], wd_l[:, k * D:(k + 1) * D]))
            assert len(chunks) == NCH
            st = lambda c: stage[:, (c % RING) * 512:(c % RING) * 512 + 512]

            @block.sync
            def _(sp):
                sp.dma_start(pos_i[:, :], io["pos"].partition_broadcast(P)).then_inc(pos_in.sem, 16)
                xv = io["x"].rearrange("(t p) d -> p t d", p=P)
                for c, (src, shape, hi, lo) in enumerate(chunks):
                    if c % 2 == 0 and c // 2 in range(1, 1 + GROUPS):
                        q = c // 2 - 1
                        sp.dma_start(x_res[:, q * 4 * D:(q + 1) * 4 * D].rearrange("p (t d) -> p t d", d=D),
                                     xv[:, 4 * q:4 * q + 4, :]).then_inc(x_in[q].sem, 16)
                    if c >= RING:
                        sp.wait_ge(w_lo.sem, w_lo.at(0, c - RING))
                    dst = st(c) if shape is None else st(c).rearrange("p (a b) -> p a b", a=shape[0])
                    sp.dma_start(dst, src).then_inc(w_in[c % RING].sem, 16)

            @block.scalar
            def _(act):
                act.dma_start(ident[:, :], io["ident"]).then_inc(consts_in.sem, 16)
                act.dma_start(small[:, 0:29], io["small"]).then_inc(consts_in.sem, 16)
                act.dma_start(cos_a[:, :], io["rope_self"][0]).then_inc(consts_in.sem, 16)
                act.dma_start(sin_a[:, :], io["rope_self"][1]).then_inc(consts_in.sem, 16)
                act.dma_start(causal[:, :], io["causal"]).then_inc(consts_in.sem, 16)
                act.dma_start(bd_row[:, :], io["b_dense"].partition_broadcast(P)).then_inc(consts_in.sem, 16)
                for b in range(2):
                    act.dma_start(mask_i[b * S:(b + 1) * S, :].rearrange("q (b k) -> q b k", k=S),
                                  io["mask"].rearrange("b q k -> q b k")).then_inc(mask_in.sem, 16)
                for c, (src, shape, hi, lo) in enumerate(chunks):
                    act.wait_ge(w_in[c % RING].sem, w_in[c % RING].at(0, c // RING))
                    nc.scalar.activation(hi, st(c), ACT.Copy).then_inc(w_hi.sem, 1)
                    if c in TABLE:
                        q = TABLE.index(c)
                        act.wait_ge(tabp.sem, tabp.at(0, 2 * q))
                        nc.scalar.activation(cosx[:, q * GT:(q + 1) * GT], psT[2 * (q % 2)][:, :], ACT.Copy).then_inc(cosd.sem, 1)
                act.wait_ge(dve.sem, TILES * 2 + 1)
                nc.scalar.activation(rstd[:, :], rstd[:, :], ACT.Sqrt).then_inc(rt.sem, 1)
                act.wait_ge(consts_in.sem, CONSTS * 16)

            @block.vector
            def _(v):
                def one_hots(q):
                    for k in range(4):
                        nc.vector.tensor_scalar(onehot[:, k * 512:(k + 1) * 512], pos_f[:, q * GT:(q + 1) * GT],
                                                iota[:, k:k + 1], None, ALU.is_equal).then_inc(oh.sem, 1)

                v.wait_ge(pos_in.sem, pos_in.at(0, 0))
                nc.vector.tensor_copy(pos_f[:, :], pos_i[:, :]).then_inc(poss.sem, 1)
                v.wait_ge(poss.sem, poss.at(0, 0))
                nc.vector.tensor_scalar(pos_n[:, :], pos_f[:, :], 0.0, float(MAX_POS), ALU.is_lt, ALU.mult).then_inc(poss.sem, 1)
                v.wait_ge(poss.sem, poss.at(0, 1))
                nc.vector.tensor_tensor(pos_f[:, :], pos_f[:, :], pos_n[:, :], ALU.add).then_inc(poss.sem, 1)
                v.wait_ge(poss.sem, poss.at(0, 2))
                nc.vector.tensor_scalar(pos_f[:, :], pos_f[:, :], 0.0, float(MAX_POS - 1), ALU.max, ALU.min).then_inc(poss.sem, 1)
                v.wait_ge(poss.sem, poss.at(0, 3))
                for c, (src, shape, hi, lo) in enumerate(chunks):
                    v.wait_ge(w_hi.sem, w_hi.at(0, c))
                    nc.vector.tensor_tensor(lo, st(c), hi.bitcast(F32), ALU.subtract).then_inc(w_lo.sem, 1)
                    if c == 1:
                        v.wait_ge(consts_in.sem, CONSTS * 16)
                        one_hots(0)
                    if c in TABLE:
                        q = TABLE.index(c)
                        v.wait_ge(tabp.sem, tabp.at(0, 2 * q + 1))
                        if q + 1 < GROUPS:
                            one_hots(q + 1)
                        nc.vector.tensor_copy(sinx[:, q * GT:(q + 1) * GT], psT[2 * (q % 2) + 1][:, :]).then_inc(sind.sem, 1)
                    if c in range(2, 2 + 2 * GROUPS, 2):
                        q = c // 2 - 1
                        v.wait_ge(x_in[q].sem, 16)
                        for t in range(4 * q, 4 * q + 4):
                            nc.vector.bn_stats(stats[:, 6 * t:6 * t + 6], xr(t)).then_inc(dve.sem, 1)
                v.wait_ge(mask_in.sem, 32)
                nc.vector.tensor_scalar(mask8[:, :], mask_i[:, :], 0.0, None, ALU.not_equal).then_inc(sind.sem, 1)
                for t in range(TILES):
                    v.wait_ge(dve.sem, t + 1)
                    nc.vector.bn_aggr(mv[:, 2 * t:2 * t + 2], stats[:, 6 * t:6 * t + 6]).then_inc(dve.sem, 1)
                v.wait_ge(dve.sem, 2 * TILES)
                nc.vector.tensor_scalar_add(rstd[:, :], mv[:, 1:2 * TILES:2], EPS).then_inc(dve.sem, 1)
                v.wait_ge(rt.sem, rt.at(0, 0))
                nc.vector.reciprocal(rstd[:, :], rstd[:, :]).then_inc(dve.sem, 1)

            @block.tensor
            def _(pe):
                pe.wait_ge(w_lo.sem, w_lo.at(0, 1))
                for q in range(GROUPS):
                    pe.wait_ge(oh.sem, oh.at(0, 4 * q + 3))
                    for m in range(2):
                        if q >= 2:
                            pe.wait_ge((cosd, sind)[m].sem, (cosd, sind)[m].at(0, q - 2))
                        for k in range(4):
                            c = k * 256 + m * P
                            nc.tensor.matmul(psT[2 * (q % 2) + m][:, :], tab_h[:, c:c + P], onehot[:, k * 512:(k + 1) * 512],
                                             start=(k == 0), stop=False)
                            last = nc.tensor.matmul(psT[2 * (q % 2) + m][:, :], tab_l[:, c:c + P], onehot[:, k * 512:(k + 1) * 512],
                                                    start=False, stop=(k == 3))
                        last.then_inc(tabp.sem, 1)

        self_attention(nc, at, io, locals())
        cross_keys_values(nc, at, io, locals())
        ffn_rstd = Rstd(nc, outer, locals(), "f_ln")
        cross_attention(nc, at, io, locals())
        feed_forward(nc, at, io, out, locals())


def self_attention(nc, at, io, m):
    WR, XT, ER, A0 = m["WR"], m["XT"], m["ER"], m["A0"]
    wqk_h, wqk_l, wd_h, wd_l, wv_h, wv_l = (m[n] for n in ("wqk_h", "wqk_l", "wd_h", "wd_l", "wv_h", "wv_l"))
    xr, mv, rstd, stats, ident = m["xr"], m["mv"], m["rstd"], m["stats"], m["ident"]
    xt_h = at("xta_h", XT + 16, [KT * GT], F32R)
    xt_l = at("xta_l", XT + 24, [KT * GT], F32R)
    ct_h = at("cta_h", XT + 32, [2 * KT * P], F32R)
    ct_l = at("cta_l", XT + 36, [2 * KT * P], F32R)
    on = at("ona", XT + 40, [GROUP * D], F32)
    r16 = {n: at(n, A0 + 4 * i, [4 * GT], F16) for i, n in enumerate(("qa_h", "qa_l", "ka_h", "ka_l"))}
    A1 = A0 + 16
    t1 = at("t1a", A1, [2 * GT], F32)
    sw = at("swa", A1 + 4, [2 * GT], F32)
    VW = HD_SELF + 1
    va_h = at("va_h", A1 + 8, [GROUP * G * VW], F16)
    va_l = at("va_l", A1 + 9.125, [GROUP * G * VW], F16)
    v32 = at("v32a", A1 + 10.25, [GT], F32)
    xn = at("xna", A1 + 12.25, [2 * D], F32)
    rinv = at("rinv_a", A1 + 16.25, [16], F32)
    mx = at("mx_a", A1 + 16.5, [4 * 8], F32)
    qm_h = at("qm_h", ER, [2 * 2048], F16)
    qm_l = at("qm_l", ER + 8, [2 * 2048], F16)
    pr = at("pr_a", ER + 16, [4 * 512], F32)
    pt_h = at("pta_h", ER + 24, [4 * 512], F16)
    pt_l = at("pta_l", ER + 28, [4 * 512], F16)

    with ExitStack() as ctx:
        ps = [ctx.enter_context(nc.psum_tensor(f"psA{n}", [P, 512], F32)) for n in range(8)]
        psQ, psS, psP, psO = ps[0:2], ps[2:4], ps[4:6], ps[6:8]

        def sig(name, per):
            return Signal(nc, ctx, name, per, base=4)

        s_xn, s_xp, s_xh, s_xl = sig("a_xn", 4), sig("a_xnT_psum", 4), sig("a_xT_hi", 4), sig("a_xT_lo", 4)
        s_bd = sig("a_bias_added", 4)
        s_vp, s_v32, s_vt, s_vh, s_vl = sig("a_v_psum", 1), sig("a_v", 1), sig("a_v_turned", 1), sig("a_v_hi", 1), sig("a_v_lo", 1)
        s_qp = sig("a_proj_psum", 8)
        s_sw, s_t1, s_t2, s_r = sig("a_swapped", 8), sig("a_cos_term", 8), sig("a_sin_term", 8), sig("a_roped", 8)
        s_rh, s_rl = sig("a_roped_hi", 8), sig("a_roped_lo", 8)
        s_qmh, s_qml = sig("a_q_masked_hi", 16), sig("a_q_masked_lo", 16)
        s_S = sig("a_scores_psum", 16)
        s_fill, s_pred, s_mx, s_sub = sig("a_filled", 16), sig("a_causal", 16), sig("a_max", 16), sig("a_less_max", 16)
        s_exp, s_T, s_ones = sig("a_exp", 16), sig("a_pT_psum", 16), sig("a_v_ones", 0)
        s_ph, s_pl, s_O = sig("a_pT_hi", 16), sig("a_pT_lo", 16), sig("a_o_psum", 16)
        s_ri, s_on = sig("a_inv_sum", 8), sig("a_o_normal", 8)
        s_cp, s_ch, s_cl = sig("a_oT_psum", 4), sig("a_oT_hi", 4), sig("a_oT_lo", 4)
        s_Y, s_xr, s_st = sig("a_dense_psum", 4), sig("a_residual", 4), sig("a_stats", 4)
        block = ctx.enter_context(nc.Block())

        UNITS, FIRST = 16, 5
        LN, LN_T, LN_LO = (5, 5, 6, 7), (6, 6, 7, 8), (7, 7, 8, 9)
        PROJ = (10, 11, 11, 13, 14, 15, 17, 18)
        V, V_TURN = 9, 17
        steps = []
        for s in range(FIRST, FIRST + UNITS):
            def unit(kind, lag, count=UNITS, every=1):
                for ahead in range(2):
                    n, off = divmod(s - ahead * UNITS - lag, every)
                    if off == 0 and 0 <= n < count:
                        steps.append((kind, n, ahead))

            unit("norm", 4, 8, 2)
            unit("turn", 1)
            unit("fill", -1)
            unit("split_pT", 2)
            unit("pv", 2)
            unit("softmax", 0)
            if s == V_TURN:
                steps.append(("v_turn", 0, 1))
            unit("score", -1)
            unit("mask", -2)
            steps += [("rope_lo", n, 1) for n in range(8) if PROJ[n] + 2 == s]
            if s == V:
                steps.append(("v", 0, 1))
            if s == V + 1:
                steps.append(("v32", 0, 1))
            steps += [("lnT", n, 1) for n in range(4) if LN_T[n] == s]
            steps += [("rope", n, 1) for n in range(8) if PROJ[n] + 1 == s]
            unit("dense", 16, 4)
            steps += [("ln", n, 1) for n in range(4) if LN[n] == s]
            steps += [("ln_lo", n, 1) for n in range(4) if LN_LO[n] == s]
            unit("y", 17, 4)
            steps += [("proj", n, 1) for n in range(8) if PROJ[n] == s]

        def turn_steps(i):
            if type(i) is int:
                return [x for x in steps if x[2] == (1 if i < 0 else 0)]
            return steps

        def readers(kind, n):
            return {"lnT": (s_xl, n), "v": (s_v32, n), "v_turn": (s_vl, n), "proj": (s_t1, n), "dense": (s_cl, n), "y": (s_xr, n)}[kind]

        class Products:

            def __init__(self, i):
                self.turn = i
                self.uses = [x for x in turn_steps(i) if x[0] in ("lnT", "v", "v_turn", "proj", "dense", "y")]

            def __getitem__(self, use):
                return psQ[self.uses.index(use) % 2]

            def last_reads(self, use):
                n = self.uses.index(use) - 2
                if n >= 0:
                    kind, event, ahead = self.uses[n]
                    signal, event = readers(kind, event)
                    return [(signal.sem, signal.at(self.turn + ahead, event))]
                return [(s_t1.sem, s_t1.at(self.turn + 1, -1)), (s_cl.sem, s_cl.at(self.turn, -1)),
                        (s_xr.sem, s_xr.at(self.turn, -1))]

        def program(eng, step):
            def turn(i):
                bank = Products(i)
                for kind, n, ahead in turn_steps(i):
                    step(i + ahead, kind, n, bank, (kind, n, ahead))

            turn(-1)
            with eng.Fori(0, GROUPS - 1) as i:
                turn(i)
            turn(GROUPS - 1)

        def features(t):
            return t[:, :].rearrange("p (c d) -> p c d", d=VW)[:, :, 0:HD_SELF]

        def turned(bank):
            return bank[:, :].rearrange("p (c d) -> p c d", d=HD_SELF)

        COL = lambda t, hp, b: ((t * 2 + hp) * 2 + b) * S

        @block.tensor
        def _(pe):
            start(pe, s_xp, s_vp, s_vt, s_qp, s_S, s_T, s_O, s_cp, s_Y)

            def step(i, kind, n, bank, use):
                if kind in ("lnT", "v", "v_turn", "proj", "dense", "y"):
                    for read, value in bank.last_reads(use):
                        pe.wait_ge(read, value)
                if kind == "lnT":
                    pe.wait_ge(s_xn.sem, s_xn.at(i, n))
                    for k in range(KT):
                        c = (n % 2) * D + k * P
                        last = nc.tensor.transpose(bank[use][:, k * P:(k + 1) * P], xn[:, c:c + P], ident[:, :])
                    last.then_inc(s_xp.sem, 1)
                if kind == "v":
                    pe.wait_ge(s_xl.sem, s_xl.at(i, 3))
                    for k in range(KT):
                        last = split3(nc, bank[use][:, :], wv_h[:, k * P:(k + 1) * P], wv_l[:, k * P:(k + 1) * P],
                                      xt_h[:, k * GT:(k + 1) * GT], xt_l[:, k * GT:(k + 1) * GT], k == 0, k == KT - 1)
                    last.then_inc(s_vp.sem, 1)
                if kind == "v_turn":
                    pe.wait_ge(s_v32.sem, s_v32.at(i, 0))
                    for t in range(4):
                        last = nc.tensor.transpose(bank[use][:, t * P:(t + 1) * P], v32[:, t * P:(t + 1) * P], ident[:, :])
                    last.then_inc(s_vt.sem, 1)
                if kind == "proj":
                    for k in range(KT):
                        c = k * 1024 + (n % 2) * 512 + (n // 2) * P
                        last = split3(nc, bank[use][:, :], wqk_h[:, c:c + P], wqk_l[:, c:c + P],
                                      xt_h[:, k * GT:(k + 1) * GT], xt_l[:, k * GT:(k + 1) * GT], k == 0, k == KT - 1)
                    last.then_inc(s_qp.sem, 1)
                if kind == "score":
                    j, u, g, ring = n // 4, n // 2 % 2, n % 2, n // 2 % 2
                    pe.wait_ge(s_qmh.sem, s_qmh.at(i, n))
                    pe.wait_ge(s_qml.sem, s_qml.at(i, n))
                    if n % 4 == 0:
                        pe.wait_ge(s_rl.sem, s_rl.at(i, 2 * j + 1))
                    pe.wait_ge(s_pred.sem, s_pred.back(i, n, 2))
                    for t in range(2):
                        for hp in range(2):
                            for b in range(2):
                                q = ring * 2048 + (t * 2 + b) * 512 + (4 * g + 2 * hp) * S
                                kk = j * GT + (2 * u + t) * P + b * S
                                last = split3(nc, psS[n % 2][:, COL(t, hp, b):COL(t, hp, b) + S],
                                              qm_h[:, q:q + P], qm_l[:, q:q + P],
                                              r16["ka_h"][:, kk:kk + S], r16["ka_l"][:, kk:kk + S], True, True)
                    last.then_inc(s_S.sem, 1)
                if kind == "turn":
                    pe.wait_ge(s_exp.sem, s_exp.at(i, n))
                    pe.wait_ge(s_pl.sem, s_pl.back(i, n, 2))
                    for c in range(4):
                        last = nc.tensor.transpose(psP[n % 2][:, c * P:(c + 1) * P],
                                                   pr[:, (n % 4) * 512 + c * P:(n % 4) * 512 + (c + 1) * P], ident[:, :])
                    last.then_inc(s_T.sem, 1)
                if kind == "pv":
                    j, u, g = n // 4, n // 2 % 2, n % 2
                    pe.wait_ge(s_pl.sem, s_pl.at(i, n))
                    if n == 0:
                        pe.wait_ge(s_vl.sem, s_vl.at(i, 0))
                    if g == 0:
                        pe.wait_ge(s_on.sem, s_on.back(i, n // 2, 1))
                    for t in range(2):
                        for hp in range(2):
                            for b in range(2):
                                rows = slice(b * S, (b + 1) * S)
                                o = ((t * 2 + g) * 2 + hp) * VW
                                c = (n % 4) * 512 + (t * 2 + hp) * P
                                vc = ((2 * u + t) * G + 2 * j + g) * VW
                                last = split3(nc, psO[b][:, o:o + VW], pt_h[rows, c:c + P], pt_l[rows, c:c + P],
                                              va_h[rows, vc:vc + VW], va_l[rows, vc:vc + VW], True, True)
                    last.then_inc(s_O.sem, 1)
                if kind == "dense":
                    pe.wait_ge(s_on.sem, s_on.at(i, 6 + n // 2))
                    src = on[:, n * D:(n + 1) * D].rearrange("p (b g c) -> p b g c", b=2, g=2)
                    for gh in range(2):
                        for b in range(2):
                            dst = bank[use][:, gh * 256:(gh + 1) * 256].rearrange("p (h t) -> p h t", h=2)
                            last = nc.tensor.transpose(dst[:, :, b * S:(b + 1) * S], src[:, b, gh, :], ident[:, :])
                    last.then_inc(s_cp.sem, 1)
                if kind == "y":
                    pe.wait_ge(s_cl.sem, s_cl.at(i, n))
                    for k in range(KT):
                        c = (n % 2) * 512 + k * P
                        last = split3(nc, bank[use][:, :], ct_h[:, c:c + P], ct_l[:, c:c + P],
                                      wd_h[:, k * D:(k + 1) * D], wd_l[:, k * D:(k + 1) * D], k == 0, k == KT - 1)
                    last.then_inc(s_Y.sem, 1)

            program(pe, step)

        def mask_heads(engine_op, half, qm, n):
            j, u, g, ring = n // 4, n // 2 % 2, n % 2, n // 2 % 2
            src = r16[half][:, j * GT + u * 256:j * GT + (u + 1) * 256].rearrange("p (c q) -> p c q", q=S)
            dst = qm[:, ring * 2048:(ring + 1) * 2048].rearrange("p (c h q) -> p c h q", h=8, q=S)
            for h in range(4 * g, 4 * g + 4):
                last = engine_op(dst[:, :, h, :], src, m["hmask"][:, h:h + 1])
            return last

        @block.scalar
        def _(act):
            start(act, s_xh, s_vh, s_sw, s_rh, s_exp, s_ph, s_ch, s_qml)

            def step(i, kind, n, bank, use):
                if kind == "lnT":
                    act.wait_ge(s_xp.sem, s_xp.at(i, n))
                    act.wait_ge(s_qp.sem, s_qp.at(i, -1))
                    dst = xt_h[:, :].rearrange("p (k t) -> p k t", k=KT)[:, :, n * P:(n + 1) * P]
                    nc.scalar.activation(dst, bank[use][:, :].rearrange("p (k t) -> p k t", k=KT), ACT.Copy).then_inc(s_xh.sem, 1)
                if kind == "v_turn":
                    act.wait_ge(s_vt.sem, s_vt.at(i, 0))
                    act.wait_ge(s_O.sem, s_O.at(i, -1))
                    act.wait_ge(s_ones.sem, s_ones.at(0, 1))
                    nc.scalar.activation(features(va_h), turned(bank[use]), ACT.Copy).then_inc(s_vh.sem, 1)
                if kind == "proj":
                    act.wait_ge(s_qp.sem, s_qp.at(i, n))
                    act.wait_ge(s_r.sem, s_r.back(i, n, 2))
                    o = (n % 2) * GT
                    nc.scalar.activation(sw[0:64, o:o + GT], bank[use][64:128, :], ACT.Copy)
                    nc.scalar.activation(sw[64:128, o:o + GT], bank[use][0:64, :], ACT.Copy).then_inc(s_sw.sem, 1)
                if kind == "rope":
                    o, j = (n % 2) * GT, n // 2
                    dst = r16["qa_h" if n % 2 == 0 else "ka_h"]
                    act.wait_ge(s_r.sem, s_r.at(i, n))
                    act.wait_ge(s_S.sem, s_S.at(i - 1, 4 * j + 3))
                    act.wait_ge(s_qmh.sem, s_qmh.at(i - 1, 4 * j + 3))
                    nc.scalar.activation(dst[:, j * GT:(j + 1) * GT], t1[:, o:o + GT], ACT.Copy).then_inc(s_rh.sem, 1)
                if kind == "mask":
                    act.wait_ge(s_rl.sem, s_rl.at(i, n // 4 * 2))
                    act.wait_ge(s_S.sem, s_S.back(i, n, 4))
                    mask_heads(lambda dst, src, h: nc.scalar.activation(dst, src, ACT.Copy, scale=h), "qa_l", qm_l, n
                               ).then_inc(s_qml.sem, 1)
                if kind == "softmax":
                    o = (n % 4) * 512
                    act.wait_ge(s_sub.sem, s_sub.at(i, n))
                    nc.scalar.activation(pr[:, o:o + 512], pr[:, o:o + 512], ACT.Exp, scale=SCALE_SELF).then_inc(s_exp.sem, 1)
                if kind == "turn":
                    o = (n % 4) * 512
                    act.wait_ge(s_T.sem, s_T.at(i, n))
                    act.wait_ge(s_O.sem, s_O.back(i, n, 4))
                    nc.scalar.activation(pt_h[:, o:o + 512], psP[n % 2][:, :], ACT.Copy).then_inc(s_ph.sem, 1)
                if kind == "dense":
                    act.wait_ge(s_cp.sem, s_cp.at(i, n))
                    act.wait_ge(s_Y.sem, s_Y.back(i, n, 2))
                    c = (n % 2) * 512
                    nc.scalar.activation(ct_h[:, c:c + 512], bank[use][:, :], ACT.Copy).then_inc(s_ch.sem, 1)

            program(act, step)

        @block.gpsimd
        def _(pool):
            start(pool, s_bd, s_r, s_rl, s_fill, s_sub, s_ones)
            nc.gpsimd.memset(va_h[:, :], 1.0).then_inc(s_ones.sem, 1)
            nc.gpsimd.memset(va_l[:, :], 0.0).then_inc(s_ones.sem, 1)

            def step(i, kind, n, bank, use):
                if kind == "lnT":
                    pool.wait_ge(s_xn.sem, s_xn.at(i, n))
                    settle(pool, m)
                    nc.gpsimd.tensor_tensor(xr(i * 4 + n), xr(i * 4 + n), m["bd_row"][:, :], ALU.add).then_inc(s_bd.sem, 1)
                if kind == "rope":
                    o = (n % 2) * GT
                    pool.wait_ge(s_t1.sem, s_t1.at(i, n))
                    pool.wait_ge(s_t2.sem, s_t2.at(i, n))
                    nc.gpsimd.tensor_tensor(t1[:, o:o + GT], t1[:, o:o + GT], sw[:, o:o + GT], ALU.add).then_inc(s_r.sem, 1)
                if kind == "rope_lo":
                    o, jj = (n % 2) * GT, slice(n // 2 * GT, (n // 2 + 1) * GT)
                    pool.wait_ge(s_rh.sem, s_rh.at(i, n))
                    if n % 2 == 0:
                        pool.wait_ge(s_qml.sem, s_qml.at(i - 1, 2 * n + 3))
                    hi, lo = ("qa_h", "qa_l") if n % 2 == 0 else ("ka_h", "ka_l")
                    nc.gpsimd.tensor_tensor(r16[lo][:, jj], t1[:, o:o + GT], r16[hi][:, jj], ALU.subtract).then_inc(s_rl.sem, 1)
                if kind == "fill":
                    o = (n % 4) * 512
                    pool.wait_ge(s_T.sem, s_T.back(i, n, 4))
                    settle(pool, m)
                    nc.gpsimd.memset(pr[:, o:o + 512], FILL_SELF).then_inc(s_fill.sem, 1)
                if kind == "softmax":
                    o = (n % 4) * 512
                    pool.wait_ge(s_mx.sem, s_mx.at(i, n))
                    v3 = pr[:, o:o + 512].rearrange("p (c k) -> p c k", k=S)
                    mb = mx[:, (n % 4) * 8:(n % 4) * 8 + 8].rearrange("p (c k) -> p c k", k=1).to_broadcast([P, 8, S])
                    nc.gpsimd.tensor_tensor(v3, v3, mb, ALU.subtract).then_inc(s_sub.sem, 1)

            program(pool, step)

        @block.vector
        def _(v):
            start(v, s_xn, s_xl, s_v32, s_vl, s_t1, s_t2, s_qmh, s_pred, s_mx, s_pl, s_ri, s_on, s_cl, s_xr, s_st)

            def step(i, kind, n, bank, use):
                if kind == "ln":
                    v.wait_ge(s_xp.sem, s_xp.back(i, n, 2))
                    mcol = mv[:, bass.ds((i * 4 + n) * 2, 1)]
                    rcol = rstd[:, bass.ds(i * 4 + n, 1)]
                    nc.vector.tensor_scalar(xn[:, (n % 2) * D:(n % 2 + 1) * D], xr(i * 4 + n), mcol, rcol,
                                            ALU.subtract, ALU.mult).then_inc(s_xn.sem, 1)
                if kind == "ln_lo":
                    v.wait_ge(s_xh.sem, s_xh.at(i, n))
                    hi = xt_h[:, :].rearrange("p (k t) -> p k t", k=KT)[:, :, n * P:(n + 1) * P]
                    lo = xt_l[:, :].rearrange("p (k t) -> p k t", k=KT)[:, :, n * P:(n + 1) * P]
                    nc.vector.tensor_tensor(lo, bank["lnT", n, 1][:, :].rearrange("p (k t) -> p k t", k=KT), hi.bitcast(F32),
                                            ALU.subtract).then_inc(s_xl.sem, 1)
                if kind == "v32":
                    v.wait_ge(s_vp.sem, s_vp.at(i, 0))
                    v.wait_ge(s_vl.sem, s_vl.at(i, -1))
                    nc.vector.tensor_scalar(v32[:, :], bank["v", 0, 1][:, :], m["v_b"], None, ALU.add).then_inc(s_v32.sem, 1)
                if kind == "v_turn":
                    v.wait_ge(s_vh.sem, s_vh.at(i, 0))
                    nc.vector.tensor_tensor(features(va_l), turned(bank[use]), features(va_h), ALU.subtract).then_inc(s_vl.sem, 1)
                if kind == "rope":
                    o = (n % 2) * GT
                    j = n // 2
                    bias = (m["q_b"], m["k_b"])[n % 2][:, j:j + 1]
                    bias_s = (m["q_bs"], m["k_bs"])[n % 2][:, j:j + 1]
                    b3 = lambda tab: tab[:, :].rearrange("p (c s) -> p c s", c=1).to_broadcast([P, 8, S])
                    r3 = lambda ap: ap.rearrange("p (c s) -> p c s", s=S)
                    v.wait_ge(s_sw.sem, s_sw.at(i, n))
                    v.wait_ge(s_rl.sem, s_rl.back(i, n, 2))
                    nc.vector.scalar_tensor_tensor(r3(t1[:, o:o + GT]), r3(bank["proj", n, 1][:, :]), bias, b3(m["cos_a"]),
                                                   ALU.add, ALU.mult).then_inc(s_t1.sem, 1)
                    nc.vector.scalar_tensor_tensor(r3(sw[:, o:o + GT]), r3(sw[:, o:o + GT]), bias_s, b3(m["sin_a"]),
                                                   ALU.add, ALU.mult).then_inc(s_t2.sem, 1)
                if kind == "mask":
                    v.wait_ge(s_rl.sem, s_rl.at(i, n // 4 * 2))
                    v.wait_ge(s_S.sem, s_S.back(i, n, 4))
                    mask_heads(lambda dst, src, h: nc.vector.tensor_scalar(dst, src, h, None, ALU.mult), "qa_h", qm_h, n
                               ).then_inc(s_qmh.sem, 1)
                if kind == "softmax":
                    o = (n % 4) * 512
                    v.wait_ge(s_S.sem, s_S.at(i, n))
                    v.wait_ge(s_fill.sem, s_fill.at(i, n))
                    cm = m["causal"][:, :].rearrange("p (c k) -> p c k", c=1).to_broadcast([P, 8, S])
                    v3 = pr[:, o:o + 512].rearrange("p (c k) -> p c k", k=S)
                    settle(v, m)
                    nc.vector.copy_predicated(v3, cm, psS[n % 2][:, :].rearrange("p (c k) -> p c k", k=S)).then_inc(s_pred.sem, 1)
                    v.wait_ge(s_pred.sem, s_pred.at(i, n))
                    v.wait_ge(s_sub.sem, s_sub.back(i, n, 4))
                    nc.vector.tensor_reduce(mx[:, (n % 4) * 8:(n % 4) * 8 + 8], v3, AX_X, ALU.max).then_inc(s_mx.sem, 1)
                if kind == "split_pT":
                    o = (n % 4) * 512
                    v.wait_ge(s_ph.sem, s_ph.at(i, n))
                    nc.vector.tensor_tensor(pt_l[:, o:o + 512], psP[n % 2][:, :], pt_h[:, o:o + 512],
                                            ALU.subtract).then_inc(s_pl.sem, 1)
                if kind == "norm":
                    j, u = n // 2, n % 2
                    v.wait_ge(s_O.sem, s_O.at(i, 2 * n + 1))
                    v.wait_ge(s_on.sem, s_on.back(i, n, 1))
                    o3 = [psO[b][:, 0:8 * VW].rearrange("p (c d) -> p c d", d=VW) for b in range(2)]
                    r3 = [rinv[:, b * 8:(b + 1) * 8].rearrange("p (c x) -> p c x", x=1) for b in range(2)]
                    for b in range(2):
                        last = nc.vector.reciprocal(r3[b], o3[b][:, :, HD_SELF:VW])
                    last.then_inc(s_ri.sem, 1)
                    v.wait_ge(s_ri.sem, s_ri.at(i, n))
                    v.wait_ge(s_cp.sem, s_cp.at(i, -1))
                    for b in range(2):
                        dst = on[:, 2 * u * D:(2 * u + 2) * D].rearrange("p (t b j c) -> p t b j c", t=2, b=2, j=4)[:, :, b, j, :]
                        last = nc.vector.tensor_tensor(dst.rearrange("p t (c d) -> p t c d", d=HD_SELF),
                                                       o3[b][:, :, 0:HD_SELF].rearrange("p (t c) d -> p t c d", t=2),
                                                       r3[b].rearrange("p (t c) x -> p t c x", t=2).to_broadcast([P, 2, 4, HD_SELF]),
                                                       ALU.mult)
                    last.then_inc(s_on.sem, 1)
                if kind == "dense":
                    c = (n % 2) * 512
                    v.wait_ge(s_ch.sem, s_ch.at(i, n))
                    nc.vector.tensor_tensor(ct_l[:, c:c + 512], bank[use][:, :], ct_h[:, c:c + 512].bitcast(F32),
                                            ALU.subtract).then_inc(s_cl.sem, 1)
                if kind == "y":
                    v.wait_ge(s_Y.sem, s_Y.at(i, n))
                    v.wait_ge(s_bd.sem, s_bd.at(i, n))
                    nc.vector.tensor_tensor(xr(i * 4 + n), bank[use][:, :], xr(i * 4 + n), ALU.add).then_inc(s_xr.sem, 1)
                    v.wait_ge(s_xr.sem, s_xr.at(i, n))
                    nc.vector.bn_stats(stats[:, bass.ds((i * 4 + n) * 6, 6)], xr(i * 4 + n)).then_inc(s_st.sem, 1)

            program(v, step)
            v.wait_ge(s_st.sem, s_st.at(0, TILES - 1))


def cross_keys_values(nc, at, io, m):
    WR, XT, ER, F0 = m["WR"], m["XT"], m["ER"], m["F0"]
    cosx, sinx, ident, kscr, vscr = m["cosx"], m["sinx"], m["ident"], m["kscr"], m["vscr"]
    wk_h = at("wkx_h", WR, [G * KT * P], F32R)
    wk_l = at("wkx_l", WR + 16, [G * KT * P], F32R)
    wv_h = at("wvx_h", ER, [KT * 1024], F32R)
    wv_l = at("wvx_l", ER + 16, [KT * 1024], F32R)
    ct_h = at("ctx_h", XT, [KT * GT], F32R)
    ct_l = at("ctx_l", XT + 8, [KT * GT], F32R)
    cin = at("ctx_in", F0, [4 * D], F32)
    RING = 4
    stage = at("stage_kv", F0 + 8, [RING * 512], F32)
    t1 = at("t1k", F0 + 16, [2 * GT], F32)
    sw = at("swk", F0 + 20, [2 * GT], F32)
    ks = at("k_out", F0 + 24, [2 * 2 * GT], F16)
    vs = at("v_out", F0 + 28, [2 * 512], F32)
    with ExitStack() as ctx:
        ps = [ctx.enter_context(nc.psum_tensor(f"psK{n}", [P, 512], F32)) for n in range(4)]

        def sig(name, per, step=1):
            return Signal(nc, ctx, name, per, step, base=1)

        w_in = [sig(f"k_w_in{r}", 0, 16) for r in range(RING)]
        w_hi, w_lo = sig("k_w_hi", 0), sig("k_w_lo", 0)
        c_in = [sig(f"ctx_in{t}", 1, 16) for t in range(4)]
        s_cp, s_ch, s_cl = sig("k_ctxT_psum", 4), sig("k_ctxT_hi", 4), sig("k_ctxT_lo", 4)
        s_kp, s_sw, s_t1, s_t2, s_r = sig("k_psum", 8), sig("k_swapped", 8), sig("k_cos_term", 8), sig("k_sin_term", 8), sig("k_roped", 8)
        s_rh, s_rl = sig("k_hi", 8), sig("k_lo", 8)
        s_ko = [sig(f"k_stored{r}", 4, 16) for r in range(2)]
        s_vp, s_v = sig("v_psum", 8), sig("v_sbuf", 8)
        s_vo = [sig(f"v_stored{r}", 4, 16) for r in range(2)]
        norm = Rstd(nc, ctx, m, "k_ln")
        block = ctx.enter_context(nc.Block())

        steps = [("v", 0, 0), ("k", 0, 0), ("k", 1, 0), ("rope", 0, 0)]
        for n in range(2, 8):
            steps += [("k", n, 0), ("rope", n - 1, 0), ("v", n - 1, 0)]
        steps += [("rope", 7, 0), ("v", 7, 0)]
        steps += [("ct", t, 1) for t in range(4)]

        def readers(use):
            kind, n, ahead = use
            return {"ct": (s_cl, n), "k": (s_t1, n), "v": (s_v, n)}[kind] + (ahead,)

        bank = Banks(ps, [use for use in steps if use[0] != "rope"], readers)

        def program(eng, step, weights=lambda: None, rstd=lambda: None):
            for use in steps[-4:]:
                step(0, use[0], use[1], use)
            weights()
            with eng.Fori(0, GROUPS - 1) as i:
                for use in steps:
                    step(i + use[2], use[0], use[1], use)
            rstd()
            for use in steps[:-4]:
                step(GROUPS - 1, use[0], use[1], use)

        chunk_order = [("v", 2 * k) for k in range(KT)] + [("k", g) for g in range(3)]
        chunk_order += [("v", 2 * k + 1) for k in range(KT)] + [("k", g) for g in range(3, G)]
        chunks = []
        for kind, c in chunk_order:
            cols = slice(c * 512, (c + 1) * 512)
            if kind == "k":
                src = io["wk"].rearrange("(k p) n -> p k n", p=P)[:, :, c * P:(c + 1) * P]
                chunks.append((src, KT, wk_h[:, cols], wk_l[:, cols]))
            else:
                src = io["wv"][(c // 2) * P:(c // 2 + 1) * P, (c % 2) * 512:(c % 2 + 1) * 512]
                chunks.append((src, 1, wv_h[:, cols], wv_l[:, cols]))
        st = lambda c: stage[:, (c % RING) * 512:(c % RING + 1) * 512]

        @block.sync
        def _(sp):
            start(sp, *c_in, *w_in, *s_ko, *s_vo)
            def load_ctx(tile, t):
                sp.dma_start(cin[:, t * D:(t + 1) * D], io["ctx"][bass.ds(tile * P, P), :]).then_inc(c_in[t].sem, 16)

            for t in range(4):
                load_ctx(t, t)
            for c, (src, a, hi, lo) in enumerate(chunks):
                sp.wait_ge(w_lo.sem, w_lo.at(0, c - RING))
                dst = st(c) if a == 1 else st(c).rearrange("p (a b) -> p a b", a=a)
                sp.dma_start(dst, src).then_inc(w_in[c % RING].sem, 16)

            def turn(i, more):
                for n in range(4 if more else 0):
                    sp.wait_ge(s_cp.sem, s_cp.at(i, n))
                    load_ctx((i + 1) * 4 + n, n)
                for kind, n, _ in steps[:-4]:
                    if kind == "rope":
                        sp.wait_ge(s_rl.sem, s_rl.at(i, n))
                        settle(sp, m)
                        sp.dma_start(kscr[n][:, :, bass.ds(i * GT, GT)],
                                     ks[:, (n % 2) * 2 * GT:(n % 2 + 1) * 2 * GT].rearrange("p (a t) -> p a t", a=2)
                                     ).then_inc(s_ko[n % 2].sem, 16)
                    if kind == "v":
                        sp.wait_ge(s_v.sem, s_v.at(i, n))
                        settle(sp, m)
                        sp.dma_start(vscr[bass.ds(i * GT + (n // 2) * P, P), (n % 2) * 512:(n % 2 + 1) * 512],
                                     vs[:, (n % 2) * 512:(n % 2 + 1) * 512]).then_inc(s_vo[n % 2].sem, 16)

            with sp.Fori(0, GROUPS - 1) as i:
                turn(i, True)
            turn(GROUPS - 1, False)
            for r in range(2):
                sp.wait_ge(s_ko[r].sem, s_ko[r].at(GROUPS, -1))
                sp.wait_ge(s_vo[r].sem, s_vo[r].at(GROUPS, -1))

        @block.gpsimd
        def _(pool):
            start(pool, s_t2)

            def step(i, kind, n, use):
                if kind == "k":
                    o = (n % 2) * GT
                    pool.wait_ge(s_sw.sem, s_sw.at(i, n))
                    settle(pool, m)
                    nc.gpsimd.tensor_tensor(sw[:, o:o + GT], sw[:, o:o + GT], sinx[:, bass.ds(i * GT, GT)],
                                            ALU.mult).then_inc(s_t2.sem, 1)

            program(pool, step)

        @block.scalar
        def _(act):
            start(act, w_hi, s_ch, s_sw, s_rh, s_v)

            def weights():
                for c, (src, a, hi, lo) in enumerate(chunks):
                    act.wait_ge(w_in[c % RING].sem, w_in[c % RING].at(0, c // RING))
                    nc.scalar.activation(hi, st(c), ACT.Copy).then_inc(w_hi.sem, 1)

            def step(i, kind, n, use):
                if kind == "ct":
                    act.wait_ge(s_cp.sem, s_cp.at(i, n))
                    act.wait_ge(s_vp.sem, s_vp.at(i, -1))
                    dst = ct_h[:, :].rearrange("p (k t) -> p k t", k=KT)[:, :, n * P:(n + 1) * P]
                    nc.scalar.activation(dst, bank[use][:, :].rearrange("p (k t) -> p k t", k=KT),
                                         ACT.Copy).then_inc(s_ch.sem, 1)
                if kind == "k":
                    o = (n % 2) * GT
                    act.wait_ge(s_kp.sem, s_kp.at(i, n))
                    act.wait_ge(s_r.sem, s_r.ring(i, n, 2))
                    nc.scalar.activation(sw[0:64, o:o + GT], bank[use][64:128, :], ACT.Copy)
                    nc.scalar.activation(sw[64:128, o:o + GT], bank[use][0:64, :], ACT.Copy).then_inc(s_sw.sem, 1)
                if kind == "v":
                    act.wait_ge(s_vp.sem, s_vp.at(i, n))
                    act.wait_ge(s_vo[n % 2].sem, s_vo[n % 2].at(i, n // 2 - 1))
                    nc.scalar.activation(vs[:, (n % 2) * 512:(n % 2 + 1) * 512], bank[use][:, :],
                                         ACT.Copy).then_inc(s_v.sem, 1)
                if kind == "rope":
                    act.wait_ge(s_r.sem, s_r.at(i, n))
                    act.wait_ge(s_ko[n % 2].sem, s_ko[n % 2].at(i, n // 2 - 1))
                    nc.scalar.activation(ks[:, (n % 2) * 2 * GT:(n % 2) * 2 * GT + GT], t1[:, (n % 2) * GT:(n % 2 + 1) * GT],
                                         ACT.Copy).then_inc(s_rh.sem, 1)

            program(act, step, weights, lambda: norm.scalar(act))

        @block.vector
        def _(v):
            start(v, w_lo, s_cl, s_t1, s_r, s_rl)

            def weights():
                for c, (src, a, hi, lo) in enumerate(chunks):
                    v.wait_ge(w_hi.sem, w_hi.at(0, c))
                    nc.vector.tensor_tensor(lo, st(c), hi.bitcast(F32), ALU.subtract).then_inc(w_lo.sem, 1)

            def rstd():
                for t in range(TILES):
                    norm.aggregate(v, t)
                norm.vector(v)

            def step(i, kind, n, use):
                if kind == "ct":
                    v.wait_ge(s_ch.sem, s_ch.at(i, n))
                    hi = ct_h[:, :].rearrange("p (k t) -> p k t", k=KT)[:, :, n * P:(n + 1) * P]
                    lo = ct_l[:, :].rearrange("p (k t) -> p k t", k=KT)[:, :, n * P:(n + 1) * P]
                    nc.vector.tensor_tensor(lo, bank[use][:, :].rearrange("p (k t) -> p k t", k=KT), hi.bitcast(F32),
                                            ALU.subtract).then_inc(s_cl.sem, 1)
                if kind == "k":
                    o = (n % 2) * GT
                    v.wait_ge(s_sw.sem, s_sw.at(i, n))
                    v.wait_ge(s_rl.sem, s_rl.ring(i, n, 2))
                    nc.vector.tensor_tensor(t1[:, o:o + GT], bank[use][:, :], cosx[:, bass.ds(i * GT, GT)],
                                            ALU.mult).then_inc(s_t1.sem, 1)
                if kind == "rope":
                    o = (n % 2) * GT
                    v.wait_ge(s_t2.sem, s_t2.at(i, n))
                    v.wait_ge(s_t1.sem, s_t1.at(i, n))
                    nc.vector.tensor_tensor(t1[:, o:o + GT], t1[:, o:o + GT], sw[:, o:o + GT], ALU.add).then_inc(s_r.sem, 1)
                    v.wait_ge(s_rh.sem, s_rh.at(i, n))
                    v.wait_ge(s_r.sem, s_r.at(i, n))
                    nc.vector.tensor_tensor(ks[:, 2 * o + GT:2 * o + 2 * GT], t1[:, o:o + GT], ks[:, 2 * o:2 * o + GT],
                                            ALU.subtract).then_inc(s_rl.sem, 1)

            program(v, step, weights, rstd)

        @block.tensor
        def _(pe):
            start(pe, s_cp, s_kp, s_vp)

            def step(i, kind, n, use):
                for read, value in (bank.last_reads(i, use) if kind != "rope" else ()):
                    pe.wait_ge(read, value)
                if kind == "ct":
                    pe.wait_ge(c_in[n].sem, c_in[n].at(i, 0))
                    for k in range(KT):
                        last = nc.tensor.transpose(bank[use][:, k * P:(k + 1) * P],
                                                   cin[:, n * D + k * P:n * D + (k + 1) * P], ident[:, :])
                    last.then_inc(s_cp.sem, 1)
                if kind == "k":
                    pe.wait_ge(w_lo.sem, w_lo.at(0, chunk_order.index(("k", n))))
                    pe.wait_ge(s_cl.sem, s_cl.at(i, 3))
                    for k in range(KT):
                        c = (n * KT + k) * P
                        last = split3(nc, bank[use][:, :], wk_h[:, c:c + P], wk_l[:, c:c + P],
                                      ct_h[:, k * GT:(k + 1) * GT], ct_l[:, k * GT:(k + 1) * GT], k == 0, k == KT - 1)
                    last.then_inc(s_kp.sem, 1)
                if kind == "v":
                    t, h = n // 2, n % 2
                    pe.wait_ge(s_cl.sem, s_cl.at(i, t))
                    pe.wait_ge(w_lo.sem, w_lo.at(0, chunk_order.index(("v", 2 * (KT - 1) + h))))
                    for k in range(KT):
                        c, w = k * GT + t * P, k * 1024 + h * 512
                        last = split3(nc, bank[use][:, :], ct_h[:, c:c + P], ct_l[:, c:c + P],
                                      wv_h[:, w:w + 512], wv_l[:, w:w + 512], k == 0, k == KT - 1)
                    last.then_inc(s_vp.sem, 1)

            program(pe, step)


class Rstd:

    def __init__(self, nc, ctx, m, tag):
        self.nc, self.mv, self.rstd, self.stats = nc, m["mv"], m["rstd"], m["stats"]
        self.s_var, self.s_sqrt, self.s_rstd = (Signal(nc, ctx, f"{tag}_{n}") for n in ("var", "sqrt", "rstd"))

    def aggregate(self, v, t):
        self.nc.vector.bn_aggr(self.mv[:, 2 * t:2 * t + 2], self.stats[:, 6 * t:6 * t + 6]).then_inc(self.s_var.sem, 1)

    def vector(self, v):
        v.wait_ge(self.s_var.sem, TILES)
        self.nc.vector.tensor_scalar_add(self.rstd[:, :], self.mv[:, 1:2 * TILES:2], EPS).then_inc(self.s_var.sem, 1)
        v.wait_ge(self.s_sqrt.sem, 1)
        self.nc.vector.reciprocal(self.rstd[:, :], self.rstd[:, :]).then_inc(self.s_rstd.sem, 1)
        v.wait_ge(self.s_rstd.sem, 1)

    def scalar(self, act):
        act.wait_ge(self.s_var.sem, TILES + 1)
        self.nc.scalar.activation(self.rstd[:, :], self.rstd[:, :], ACT.Sqrt).then_inc(self.s_sqrt.sem, 1)


class Normalise:

    def __init__(self, nc, ctx, m, xt_h, xt_l, xn, banks, tag):
        self.nc, self.m, self.xt_h, self.xt_l, self.xn, self.banks = nc, m, xt_h, xt_l, xn, banks
        self.s_xn, self.s_xp, self.s_xh, self.s_xl = (Signal(nc, ctx, f"{tag}_{n}") for n in ("xn", "xnT_psum", "xT_hi", "xT_lo"))

    def half(self, dst, n):
        return dst[:, :].rearrange("p (k t) -> p k t", k=KT)[:, :, n * P:(n + 1) * P]

    def bank(self, n):
        return self.banks[n % 2][:, :]

    def vector(self, v, kind, n):
        m, o = self.m, (n % 2) * D
        if kind == "ln":
            if n >= 2:
                v.wait_ge(self.s_xp.sem, n - 1)
            self.nc.vector.tensor_scalar(self.xn[:, o:o + D], m["xr"](n), m["mv"][:, 2 * n:2 * n + 1], m["rstd"][:, n:n + 1],
                                         ALU.subtract, ALU.mult).then_inc(self.s_xn.sem, 1)
        if kind == "ln_lo":
            v.wait_ge(self.s_xh.sem, n + 1)
            self.nc.vector.tensor_tensor(self.half(self.xt_l, n), self.bank(n).rearrange("p (k t) -> p k t", k=KT),
                                         self.half(self.xt_h, n).bitcast(F32), ALU.subtract).then_inc(self.s_xl.sem, 1)

    def scalar(self, act, kind, n):
        if kind == "lnT":
            act.wait_ge(self.s_xp.sem, n + 1)
            self.nc.scalar.activation(self.half(self.xt_h, n), self.bank(n).rearrange("p (k t) -> p k t", k=KT),
                                      ACT.Copy).then_inc(self.s_xh.sem, 1)

    def tensor(self, pe, kind, n):
        if kind == "lnT":
            pe.wait_ge(self.s_xn.sem, n + 1)
            if n >= 2:
                pe.wait_ge(self.s_xl.sem, n - 1)
            for k in range(KT):
                c = (n % 2) * D + k * P
                last = self.nc.tensor.transpose(self.bank(n)[:, k * P:(k + 1) * P], self.xn[:, c:c + P], self.m["ident"][:, :])
            last.then_inc(self.s_xp.sem, 1)
        if kind == "ready":
            pe.wait_ge(self.s_xl.sem, n)


def tiles_through(first, last):
    out = []
    for n in range(first, last + 1):
        if n < last:
            out += [("ln", n), ("lnT", n)]
        if n > first:
            out.append(("ln_lo", n - 1))
    return out


def cross_attention(nc, at, io, m):
    WR, XT, ER, F0 = m["WR"], m["XT"], m["ER"], m["F0"]
    cosx, sinx, ident, kscr, vscr, mask8 = (m[n] for n in ("cosx", "sinx", "ident", "kscr", "vscr", "mask8"))
    xr, stats = m["xr"], m["stats"]
    xt_h = at("xtx_h", XT, [KT * T], F32R)
    xt_l = at("xtx_l", XT + 32, [KT * T], F32R)
    w1_h, w1_l = at("wq_h", WR, [KT * 512], F32R), at("wq_l", WR + 8, [KT * 512], F32R)
    w2_h, w2_l = at("wo_h", WR + 16, [HPG * D], F32R), at("wo_l", WR + 24, [HPG * D], F32R)
    ot_h, ot_l = at("ot_h", ER, [GROUP * HPG * P], F32R), at("ot_l", ER + 8, [GROUP * HPG * P], F32R)
    q_h, q_l = at("q_h", ER + 16, [2 * HPG * GT], F16), at("q_l", ER + 24, [2 * HPG * GT], F16)
    RING = 4
    stage = at("stage_x", F0, [RING * 512], F32)
    t1, sw = at("t1x", F0 + 8, [2 * GT], F32), at("swx", F0 + 12, [2 * GT], F32)
    kt = at("k_x", F0 + 16, [2 * 2 * GT], F16)
    vt = at("v_x", F0 + 20, [2 * GROUP * HD_X], F32)
    pr = at("pr_x", F0 + 24, [2 * 512], F32)
    pt = at("pt_x", F0 + 28, [2 * 512], F32)
    xn = at("xn_x", F0 + 32, [2 * D], F32)
    sums, rinv, mx = (at(f"{n}_x", F0 + 36 + 0.0625 * i, [16], F32) for i, n in enumerate(("sums", "rinv", "mx")))

    with ExitStack() as ctx:
        ps = [ctx.enter_context(nc.psum_tensor(f"psX{n}", [P, 512], F32)) for n in range(8)]
        psQ, psS, psP, psO, psY = ps[0:2], ps[2], ps[3], ps[4:6], ps[6:8]

        def sig(name, per, step=1):
            return Signal(nc, ctx, name, per, step, base=1)

        w_in = [sig(f"x_w_in{r}", 2, 16) for r in range(RING)]
        w_hi, w_lo = sig("x_w_hi", 8), sig("x_w_lo", 8)
        kv_in = [sig(f"x_kv_in{r}", 4, 16) for r in range(2)]
        s_qp, s_sw, s_t1, s_t2, s_r = (sig(f"x_{n}", 16) for n in ("q_psum", "q_swapped", "q_cos_term", "q_sin_term", "q_roped"))
        s_rh, s_rl = sig("x_q_hi", 16), sig("x_q_lo", 16)
        s_S, s_fill, s_pred, s_mx, s_sub, s_exp = (sig(f"x_{n}", 8) for n in ("scores", "filled", "kept", "max", "less_max", "exp"))
        s_sum, s_ri, s_nm, s_T, s_pt, s_O = (sig(f"x_{n}", 8) for n in ("sum", "inv_sum", "normal", "pT_psum", "pT", "oT_psum"))
        s_oh, s_ol = sig("x_oT_hi", 16), sig("x_oT_lo", 8)
        s_Y, s_xr, s_st = sig("x_out_psum", 16), sig("x_residual", 16), sig("x_stats", 16)
        norm = Normalise(nc, ctx, m, xt_h, xt_l, xn, psY, "x_ln")
        later = m["ffn_rstd"]
        block = ctx.enter_context(nc.Block())

        def section(tg, more):
            nxt = tg + 1
            out = [("w2", tg, 0), ("N", tg, 1), ("q", nxt, 0), ("w2", tg, 1), ("T", tg, 0), ("q", nxt, 1),
                   ("w2", tg, 2), ("rope", nxt, 0), ("PV", tg, 0), ("w2", tg, 3), ("q", nxt, 2), ("T", tg, 1),
                   ("rope", nxt, 1), ("q", nxt, 3), ("rope", nxt, 2), ("PV", tg, 1), ("Y", tg, 0),
                   ("rope", nxt, 3), ("w1", tg, 0), ("Y", tg, 1), ("w1", tg, 1), ("Y", tg, 2), ("w1", tg, 2),
                   ("w1", tg, 3), ("S", nxt, 0), ("Y", tg, 3), ("S", nxt, 1), ("N", nxt, 0)]
            return [s for s in out if (s[1] < GROUPS or more) and (s[0] != "w2" or tg == 0)
                    and (s[0] != "w1" or (tg == GROUPS - 2 and more))]

        def program(eng, step, prologue=lambda kind, n: None):
            for kind, n in tiles_through(0, 4) + [("w", c) for c in range(RING)] + [("ready", 4)]:
                prologue(kind, n)
            for h in range(HPG):
                tiles = tiles_through(4 + 3 * h, 7 + 3 * h)
                for at_, (kind, n) in enumerate(tiles):
                    if at_ == (0 if eng is nc.tensor else 6):
                        step(-1, "q", GROUPS, h, True)
                    prologue(kind, n)
                step(-1, "rope", GROUPS, h, True)
            prologue("ready", TILES)
            for kind, n in (("S", 0), ("S", 1), ("N", 0)):
                step(-1, kind, GROUPS, n, True)

            def turn(i, more):
                for tg in range(GROUPS):
                    for kind, g_, n in section(tg, more):
                        step(i, kind, g_, n, more)

            with eng.Fori(0, G - 1) as i:
                turn(i, True)
            turn(G - 1, False)

        def q_event(i, tg, h):
            return (i + 1, h) if tg == GROUPS else (i, tg * HPG + h)

        def s_event(i, tg, n):
            return (i + 1, n) if tg == GROUPS else (i, 2 * tg + n)

        @block.sync
        def _(sp):
            start(sp, *w_in, *kv_in)
            def load_w1(g, c):
                sp.dma_start(stage[:, c * 512:(c + 1) * 512], io["wq"][c * P:(c + 1) * P, bass.ds(g * 512, 512)]).then_inc(w_in[c].sem, 16)

            def load_w2(g, c):
                sp.dma_start(stage[:, c * 512:(c + 1) * 512], io["wo"][bass.ds(g * 512 + c * P, P), :]).then_inc(w_in[c].sem, 16)

            def load_kv(g, tg):
                r = tg % 2
                sp.dma_start(kt[:, r * 2 * GT:(r + 1) * 2 * GT].rearrange("p (a t) -> p a t", a=2),
                             kscr[bass.ds(g, 1), :, :, tg * GT:(tg + 1) * GT].rearrange("g p a t -> (g p) a t")
                             ).then_inc(kv_in[r].sem, 16)
                sp.dma_start(vt[:, r * 512:(r + 1) * 512].rearrange("p (t d) -> p t d", t=GROUP),
                             vscr[tg * GT:(tg + 1) * GT, bass.ds(g * HD_X, HD_X)].rearrange("(t p) d -> p t d", p=P)
                             ).then_inc(kv_in[r].sem, 16)

            for c in range(RING):
                load_w1(0, c)
            load_kv(0, 0)
            for c in range(RING):
                sp.wait_ge(w_lo.sem, w_lo.at(0, c))
                load_w2(0, c)

            def turn(i, more):
                for tg in range(GROUPS):
                    if tg == 1 and more:
                        for c in range(RING):
                            sp.wait_ge(w_lo.sem, w_lo.at(i, 4 + c))
                            load_w1(i + 1, c)
                    if tg == 3 and more:
                        for c in range(RING):
                            sp.wait_ge(w_lo.sem, w_lo.at(i + 1, c))
                            load_w2(i + 1, c)
                    if tg < GROUPS - 1 or more:
                        sp.wait_ge(s_O.sem, s_O.at(i, 2 * tg - 1))
                        if tg < GROUPS - 1:
                            load_kv(i, tg + 1)
                        else:
                            load_kv(i + 1, 0)

            with sp.Fori(0, G - 1) as i:
                turn(i, True)
            turn(G - 1, False)

        @block.tensor
        def _(pe):
            start(pe, s_qp, s_S, s_T, s_O, s_Y)
            def step(i, kind, tg, n, more):
                if kind == "q":
                    j, e = q_event(i, tg, n)
                    if tg == GROUPS:
                        pe.wait_ge(w_lo.sem, w_lo.at(j, 3))
                    pe.wait_ge(s_t1.sem, s_t1.at(j, e - 2))
                    for k in range(KT):
                        c, w = k * T + (tg % GROUPS) * GT, k * 512 + n * P
                        last = split3(nc, psQ[n % 2][:, :], w1_h[:, w:w + P], w1_l[:, w:w + P],
                                      xt_h[:, c:c + GT], xt_l[:, c:c + GT], k == 0, k == KT - 1)
                    last.then_inc(s_qp.sem, 1)
                if kind == "S":
                    j, u = s_event(i, tg, n)
                    if n == 0:
                        pe.wait_ge(s_rl.sem, s_rl.at(j, 2 * u + 3))
                        pe.wait_ge(kv_in[tg % 2].sem, kv_in[tg % 2].at(j, 2 * (u // 4) + 1))
                    pe.wait_ge(s_pred.sem, s_pred.at(j, u - 1))
                    for t in range(2):
                        for hp in range(2):
                            for b in range(2):
                                tb = (2 * n + t) * 2 + b
                                q = (tg % 2) * 2048 + tb * 256 + hp * P
                                c, o = (tg % 2) * 2 * GT + tb * S, ((t * 2 + hp) * 2 + b) * S
                                last = split3(nc, psS[:, o:o + S], q_h[:, q:q + P], q_l[:, q:q + P],
                                              kt[:, c:c + S], kt[:, c + GT:c + GT + S], True, True)
                    last.then_inc(s_S.sem, 1)
                if kind == "T":
                    u = 2 * tg + n
                    pe.wait_ge(s_nm.sem, s_nm.at(i, u))
                    pe.wait_ge(s_pt.sem, s_pt.at(i, u - 1))
                    for c in range(4):
                        last = nc.tensor.transpose(psP[:, c * P:(c + 1) * P],
                                                   pr[:, n * 512 + c * P:n * 512 + (c + 1) * P], ident[:, :])
                    last.then_inc(s_T.sem, 1)
                if kind == "PV":
                    u = 2 * tg + n
                    pe.wait_ge(s_pt.sem, s_pt.at(i, u))
                    pe.wait_ge(s_ol.sem, s_ol.at(i, u - 1))
                    for b in range(2):
                        for t in range(2):
                            rows = slice(b * S, (b + 1) * S)
                            vc = (tg % 2) * 512 + (2 * n + t) * HD_X
                            last = nc.tensor.matmul(psO[b][:, t * 256:(t + 1) * 256], vt[rows, vc:vc + HD_X],
                                                    pt[rows, n * 512 + t * 256:n * 512 + (t + 1) * 256], start=True, stop=True)
                    last.then_inc(s_O.sem, 1)
                if kind == "Y":
                    y = tg * 4 + n
                    pe.wait_ge(s_ol.sem, s_ol.at(i, 2 * tg + n // 2))
                    if y == 0:
                        pe.wait_ge(w_lo.sem, w_lo.at(i, 7))
                    pe.wait_ge(s_xr.sem, s_xr.at(i, max(y - 2, -1)))
                    for h in range(HPG):
                        c = (n * HPG + h) * P
                        last = split3(nc, psY[n % 2][:, :], ot_h[:, c:c + P], ot_l[:, c:c + P],
                                      w2_h[:, h * D:(h + 1) * D], w2_l[:, h * D:(h + 1) * D], h == 0, h == HPG - 1)
                    last.then_inc(s_Y.sem, 1)

            program(pe, step, lambda kind, n: norm.tensor(pe, kind, n))

        def split_hi(act, turn, load, dst, c):
            act.wait_ge(w_in[c].sem, w_in[c].at(turn, load))
            nc.scalar.activation(dst[:, c * 512:(c + 1) * 512], stage[:, c * 512:(c + 1) * 512], ACT.Copy).then_inc(w_hi.sem, 1)

        def split_lo(v, turn, load, hi, lo, c):
            v.wait_ge(w_hi.sem, w_hi.at(turn, load * RING + c))
            sl = slice(c * 512, (c + 1) * 512)
            nc.vector.tensor_tensor(lo[:, sl], stage[:, sl], hi[:, sl].bitcast(F32), ALU.subtract).then_inc(w_lo.sem, 1)

        @block.scalar
        def _(act):
            start(act, w_hi, s_sw, s_rh, s_exp, s_pt, s_oh)
            def step(i, kind, tg, n, more):
                if kind == "w1":
                    act.wait_ge(s_qp.sem, s_qp.at(i, 15))
                    split_hi(act, i + 1, 0, w1_h, n)
                if kind == "w2":
                    act.wait_ge(s_Y.sem, s_Y.at(i, -1))
                    split_hi(act, i, 1, w2_h, n)
                if kind == "q":
                    j, e = q_event(i, tg, n)
                    o = (n % 2) * GT
                    act.wait_ge(s_qp.sem, s_qp.at(j, e))
                    act.wait_ge(s_r.sem, s_r.at(j, e - 2))
                    nc.scalar.activation(sw[0:64, o:o + GT], psQ[n % 2][64:128, :], ACT.Copy)
                    nc.scalar.activation(sw[64:128, o:o + GT], psQ[n % 2][0:64, :], ACT.Copy).then_inc(s_sw.sem, 1)
                if kind == "rope":
                    j, e = q_event(i, tg, n)
                    act.wait_ge(s_r.sem, s_r.at(j, e))
                    if not (type(i) is int and i < 0):
                        act.wait_ge(s_S.sem, s_S.at(i, 2 * (tg - 1) - 1))
                    dst = q_h[:, (tg % 2) * 2048:(tg % 2 + 1) * 2048].rearrange("p (c h q) -> p c h q", h=HPG, q=S)
                    nc.scalar.activation(dst[:, :, n, :], t1[:, (n % 2) * GT:(n % 2 + 1) * GT].rearrange("p (c q) -> p c q", q=S),
                                         ACT.Copy).then_inc(s_rh.sem, 1)
                if kind == "S":
                    j, u = s_event(i, tg, n)
                    act.wait_ge(s_sub.sem, s_sub.at(j, u))
                    nc.scalar.activation(pr[:, n * 512:(n + 1) * 512], pr[:, n * 512:(n + 1) * 512], ACT.Exp,
                                         scale=SCALE_X).then_inc(s_exp.sem, 1)
                if kind == "T":
                    u = 2 * tg + n
                    act.wait_ge(s_T.sem, s_T.at(i, u))
                    act.wait_ge(s_O.sem, s_O.at(i, max(u - 2, -1)))
                    nc.scalar.activation(pt[:, n * 512:(n + 1) * 512], psP[:, :], ACT.Copy).then_inc(s_pt.sem, 1)
                if kind == "PV":
                    u = 2 * tg + n
                    act.wait_ge(s_O.sem, s_O.at(i, u))
                    act.wait_ge(s_Y.sem, s_Y.at(i, 4 * tg - 1))
                    for b in range(2):
                        dst = ot_h[:, n * 1024:(n + 1) * 1024].rearrange("p (c q) -> p c q", q=P)[:, :, b * S:(b + 1) * S]
                        nc.scalar.activation(dst, psO[b][:, :].rearrange("p (c q) -> p c q", q=S), ACT.Copy).then_inc(s_oh.sem, 1)

            def prologue(kind, n):
                norm.scalar(act, kind, n)
                if kind == "w":
                    split_hi(act, 0, 0, w1_h, n)

            program(act, step, prologue)

        @block.gpsimd
        def _(pool):
            start(pool, s_t2, s_fill, s_sub)
            def step(i, kind, tg, n, more):
                if kind == "q":
                    j, e = q_event(i, tg, n)
                    o = (n % 2) * GT
                    c = (tg % GROUPS) * GT
                    pool.wait_ge(s_sw.sem, s_sw.at(j, e))
                    nc.gpsimd.tensor_tensor(sw[:, o:o + GT], sw[:, o:o + GT], sinx[:, c:c + GT], ALU.mult).then_inc(s_t2.sem, 1)
                if kind == "S":
                    j, u = s_event(i, tg, n)
                    pool.wait_ge(s_T.sem, s_T.ring(j, u, 2))
                    settle(pool, m)
                    nc.gpsimd.memset(pr[:, n * 512:(n + 1) * 512], FILL_X).then_inc(s_fill.sem, 1)
                    pool.wait_ge(s_mx.sem, s_mx.at(j, u))
                    v3 = pr[:, n * 512:(n + 1) * 512].rearrange("p (c k) -> p c k", k=S)
                    mb = mx[:, n * 8:n * 8 + 8].rearrange("p (c k) -> p c k", k=1).to_broadcast([P, 8, S])
                    nc.gpsimd.tensor_tensor(v3, v3, mb, ALU.subtract).then_inc(s_sub.sem, 1)

            program(pool, step)

        @block.vector
        def _(v):
            start(v, w_lo, s_t1, s_r, s_rl, s_pred, s_mx, s_sum, s_ri, s_nm, s_ol, s_xr, s_st)
            def step(i, kind, tg, n, more):
                if kind == "w1":
                    split_lo(v, i + 1, 0, w1_h, w1_l, n)
                if kind == "w2":
                    split_lo(v, i, 1, w2_h, w2_l, n)
                if kind == "q":
                    j, e = q_event(i, tg, n)
                    o, c = (n % 2) * GT, (tg % GROUPS) * GT
                    v.wait_ge(s_sw.sem, s_sw.at(j, e))
                    v.wait_ge(s_rl.sem, s_rl.at(j, e - 2))
                    nc.vector.tensor_tensor(t1[:, o:o + GT], psQ[n % 2][:, :], cosx[:, c:c + GT], ALU.mult).then_inc(s_t1.sem, 1)
                if kind == "rope":
                    j, e = q_event(i, tg, n)
                    o = (n % 2) * GT
                    v.wait_ge(s_t2.sem, s_t2.at(j, e))
                    v.wait_ge(s_t1.sem, s_t1.at(j, e))
                    nc.vector.tensor_tensor(t1[:, o:o + GT], t1[:, o:o + GT], sw[:, o:o + GT], ALU.add).then_inc(s_r.sem, 1)
                    sl = slice((tg % 2) * 2048, (tg % 2 + 1) * 2048)
                    hi = q_h[:, sl].rearrange("p (c h q) -> p c h q", h=HPG, q=S)[:, :, n, :]
                    lo = q_l[:, sl].rearrange("p (c h q) -> p c h q", h=HPG, q=S)[:, :, n, :]
                    v.wait_ge(s_rh.sem, s_rh.at(j, e))
                    v.wait_ge(s_r.sem, s_r.at(j, e))
                    nc.vector.tensor_tensor(lo, t1[:, o:o + GT].rearrange("p (c q) -> p c q", q=S), hi,
                                            ALU.subtract).then_inc(s_rl.sem, 1)
                if kind == "S":
                    j, u = s_event(i, tg, n)
                    c = (tg % GROUPS * 8 + n * 4) * S
                    mk = mask8[:, c:c + 256].rearrange("p (t x c) -> p t x c", t=2, x=1).to_broadcast([P, 2, 2, P])
                    p4 = lambda ap: ap.rearrange("p (t x c) -> p t x c", t=2, x=2)
                    v.wait_ge(s_S.sem, s_S.at(j, u))
                    v.wait_ge(s_fill.sem, s_fill.at(j, u))
                    settle(v, m)
                    nc.vector.copy_predicated(p4(pr[:, n * 512:(n + 1) * 512]), mk, p4(psS[:, :])).then_inc(s_pred.sem, 1)
                    v.wait_ge(s_pred.sem, s_pred.at(j, u))
                    v.wait_ge(s_sub.sem, s_sub.ring(j, u, 2))
                    nc.vector.tensor_reduce(mx[:, n * 8:n * 8 + 8], pr[:, n * 512:(n + 1) * 512].rearrange("p (c k) -> p c k", k=S),
                                            AX_X, ALU.max).then_inc(s_mx.sem, 1)
                if kind == "N":
                    j, u = s_event(i, tg, n)
                    v3 = pr[:, n * 512:(n + 1) * 512].rearrange("p (c k) -> p c k", k=S)
                    v.wait_ge(s_exp.sem, s_exp.at(j, u))
                    nc.vector.tensor_reduce(sums[:, n * 8:n * 8 + 8], v3, AX_X, ALU.add).then_inc(s_sum.sem, 1)
                    v.wait_ge(s_sum.sem, s_sum.at(j, u))
                    nc.vector.reciprocal(rinv[:, n * 8:n * 8 + 8], sums[:, n * 8:n * 8 + 8]).then_inc(s_ri.sem, 1)
                    v.wait_ge(s_ri.sem, s_ri.at(j, u))
                    rb = rinv[:, n * 8:n * 8 + 8].rearrange("p (c k) -> p c k", k=1).to_broadcast([P, 8, S])
                    nc.vector.tensor_tensor(v3, v3, rb, ALU.mult).then_inc(s_nm.sem, 1)
                if kind == "PV":
                    u = 2 * tg + n
                    for b in range(2):
                        v.wait_ge(s_oh.sem, s_oh.at(i, 2 * u + b))
                        sl = slice(n * 1024, (n + 1) * 1024)
                        hi = ot_h[:, sl].rearrange("p (c q) -> p c q", q=P)[:, :, b * S:(b + 1) * S]
                        lo = ot_l[:, sl].rearrange("p (c q) -> p c q", q=P)[:, :, b * S:(b + 1) * S]
                        last = nc.vector.tensor_tensor(lo, psO[b][:, :].rearrange("p (c q) -> p c q", q=S), hi.bitcast(F32),
                                                       ALU.subtract)
                    last.then_inc(s_ol.sem, 1)
                if kind == "Y":
                    y = tg * 4 + n
                    v.wait_ge(s_Y.sem, s_Y.at(i, y))
                    nc.vector.tensor_tensor(xr(y), psY[n % 2][:, :], xr(y), ALU.add).then_inc(s_xr.sem, 1)
                    if not more:
                        v.wait_ge(s_xr.sem, s_xr.at(i, y))
                        nc.vector.bn_stats(stats[:, 6 * y:6 * y + 6], xr(y)).then_inc(s_st.sem, 1)
                        v.wait_ge(s_st.sem, s_st.at(0, y))
                        later.aggregate(v, y)

            def prologue(kind, n):
                norm.vector(v, kind, n)
                if kind == "w":
                    split_lo(v, 0, 0, w1_h, w1_l, n)

            program(v, step, prologue)
            v.wait_ge(s_st.sem, s_st.at(0, TILES - 1))


def feed_forward(nc, at, io, out, m):
    WR, XT, ER, F0 = m["WR"], m["XT"], m["ER"], m["F0"]
    xr, x_res = m["xr"], m["x_res"]
    xt_h = at("xtf_h", XT, [KT * T], F32R)
    xt_l = at("xtf_l", XT + 32, [KT * T], F32R)
    wgu_h = [at(f"wgu_h{c}", o, [2 * KT * 256], F32R) for c, o in enumerate((WR, WR + 24))]
    wgu_l = [at(f"wgu_l{c}", o, [2 * KT * 256], F32R) for c, o in enumerate((WR + 8, ER + 16))]
    wdn_h = [at(f"wdn_h{c}", o, [2 * D], F32R) for c, o in enumerate((WR + 16, ER + 24))]
    wdn_l = [at(f"wdn_l{c}", o, [2 * D], F32R) for c, o in enumerate((WR + 20, ER + 28))]
    h_h, h_l = at("h_h", ER, [2 * 2 * GT], F32R), at("h_l", ER + 8, [2 * 2 * GT], F32R)
    NCH = 6
    q_st = at("q_stage", F0, [NCH * 512], I32)
    s_st = at("s_stage", F0 + 12, [NCH * 512], F32)
    w32 = at("w32", F0 + 24, [2 * 512], F32)
    xn = at("xn_f", F0 + 28, [2 * D], F32)
    sg = at("silu", F0 + 32, [2 * GT], F32)
    hf = at("hf", F0 + 36, [2 * GT], F32)

    with ExitStack() as ctx:
        ps = [ctx.enter_context(nc.psum_tensor(f"psF{n}", [P, 512], F32)) for n in range(8)]
        psG, psU, psY = ps[0:2], ps[2:4], ps[4:6]

        def sig(name, per, step=1):
            return Signal(nc, ctx, name, per, step, base=1)

        w_in = [sig(f"f_w_in{c}", 4, 16) for c in range(NCH)]
        w_32, w_hi, w_lo = sig("f_w", 2 * NCH), sig("f_w_hi", 2 * NCH), sig("f_w_lo", 2 * NCH)
        s_gp, s_up, s_sg, s_h, s_hh, s_hl = (sig(f"f_{n}", 16) for n in ("gate", "up", "silu", "hidden", "hidden_hi", "hidden_lo"))
        s_Y, s_xr = sig("f_out_psum", 32), sig("f_residual", 32)
        s_out = Signal(nc, ctx, "stored", 0, 16)
        rstd, norm = m["ffn_rstd"], Normalise(nc, ctx, m, xt_h, xt_l, xn, ps[6:8], "f_ln")
        block = ctx.enter_context(nc.Block())

        def section(pos, more):
            tg, nxt = pos % GROUPS, pos + 1
            w = [(kind, pos // GROUPS + 1, 2 * tg + c) for c in range(2) for kind in ("w", "w_lo")] if tg < 3 and more else []
            if tg == GROUPS - 1 and not more:
                return [("Y", pos, n) for n in range(GROUP)]
            return ([("gu", nxt, 0)] + w[0:1] + [("Y", pos, 0)] + w[1:2] + [("Y", pos, 1), ("gu", nxt, 1)] + w[2:3] +
                    [("Y", pos, 2)] + w[3:4] + [("Y", pos, 3)])

        def program(eng, step, prologue):
            for kind, n in [("rstd", 0)] + tiles_through(0, 4):
                prologue(kind, n)
            for c in range(NCH):
                step(-1, "w", 2, c, True)
                if c:
                    step(-1, "w_lo", 2, c - 1, True)
            step(-1, "w_lo", 2, NCH - 1, True)
            prologue("ready", 4)
            for n in range(2):
                if eng is nc.tensor:
                    step(-1, "gu", 2 * GROUPS, n, True)
                for kind, t in tiles_through(4 + 6 * n, 10 + 6 * n):
                    prologue(kind, t)
                if eng is not nc.tensor:
                    step(-1, "gu", 2 * GROUPS, n, True)
            prologue("ready", TILES)

            def turn(i, chunks, more):
                for pos in range(chunks * GROUPS):
                    for kind, pos_, n in section(pos, more):
                        step(i, kind, pos_, n, more)

            with eng.Fori(0, FCH // 2) as i:
                turn(i, 2, True)
            turn(FCH // 2, 1, False)

        def event(i, pos, n, per=2):
            return (i + 1, n) if pos == 2 * GROUPS else (i, pos * per + n)

        def w_event(i, chunk, n):
            return (i + 1, n) if chunk == 2 else (i, chunk * NCH + n)

        def halves(chunk, c):
            h, l = (wgu_h[chunk % 2], wgu_l[chunk % 2]) if c < 4 else (wdn_h[chunk % 2], wdn_l[chunk % 2])
            o = c * 512 if c < 4 else (c - 4) * 512
            return h[:, o:o + 512], l[:, o:o + 512]

        @block.sync
        def _(sp):
            start(sp, *w_in)
            def load(i, chunk, c):
                o = slice(c * 512, (c + 1) * 512)
                if c < 4:
                    q, s_ = (("gate_q", "gate_s"), ("up_q", "up_s"))[c // 2]
                    k = 2 * (c % 2)
                    sp.dma_start(q_st[:, o].rearrange("p (k n) -> p k n", k=2),
                                 io[q].rearrange("(k p) n -> p k n", p=P)[:, k:k + 2, bass.ds(i * 512 + chunk * 256, 256)]).then_inc(w_in[c].sem, 16)
                    sp.dma_start(s_st[:, o].rearrange("p (k n) -> p k n", k=2),
                                 io[s_][k:k + 2, bass.ds(i * 512 + chunk * 256, 256)].partition_broadcast(P)).then_inc(w_in[c].sem, 16)
                else:
                    sp.dma_start(q_st[:, o], io["down_q"][bass.ds(i * 512 + chunk * 256 + (c - 4) * P, P), :]).then_inc(w_in[c].sem, 16)
                    sp.dma_start(s_st[:, o], io["down_s"][bass.ds(i * 4 + chunk * 2 + (c - 4), 1), :].rearrange("a n -> (a n)").partition_broadcast(P)
                                 ).then_inc(w_in[c].sem, 16)

            for c in range(NCH):
                load(0, 0, c)
            with sp.Fori(0, FCH // 2) as i:
                for chunk in range(2):
                    for c in range(NCH):
                        sp.wait_ge(w_32.sem, w_32.at(i, chunk * NCH + c))
                        if chunk == 0:
                            load(i, 1, c)
                        else:
                            load(i + 1, 0, c)
            for y in range(TILES):
                sp.wait_ge(s_xr.sem, s_xr.at(FCH // 2, y))
                sp.dma_start(out[y * P:(y + 1) * P, :], xr(y)).then_inc(s_out.sem, 16)
            sp.wait_ge(s_out.sem, TILES * 16)

        @block.tensor
        def _(pe):
            start(pe, s_gp, s_up, s_Y)
            def step(i, kind, tg, n, more):
                if kind == "gu":
                    j, e = event(i, tg, n)
                    if tg % GROUPS == 0:
                        pe.wait_ge(w_lo.sem, w_lo.at(j, e // 8 * NCH + 3))
                    c2 = tg // GROUPS % 2
                    pe.wait_ge(s_h.sem, s_h.at(j, e - 2))
                    for bank, w0, s_ in ((psG[n], 0, s_gp), (psU[n], 1024, s_up)):
                        for k in range(KT):
                            c, w = k * T + (tg % GROUPS) * GT, w0 + k * 256 + n * P
                            last = split3(nc, bank[:, :], wgu_h[c2][:, w:w + P], wgu_l[c2][:, w:w + P],
                                          xt_h[:, c:c + GT], xt_l[:, c:c + GT], k == 0, k == KT - 1)
                        last.then_inc(s_.sem, 1)
                if kind == "Y":
                    y = tg * 4 + n
                    if n == 0:
                        pe.wait_ge(s_hl.sem, s_hl.at(i, tg * 2 + 1))
                        pe.wait_ge(w_lo.sem, w_lo.at(i, tg // GROUPS * NCH + NCH - 1))
                    pe.wait_ge(s_xr.sem, s_xr.ring(i, y, 2))
                    for k in range(2):
                        c = (tg % 2) * 1024 + k * GT + n * P
                        last = split3(nc, psY[n % 2][:, :], h_h[:, c:c + P], h_l[:, c:c + P],
                                      wdn_h[tg // GROUPS][:, k * D:(k + 1) * D], wdn_l[tg // GROUPS][:, k * D:(k + 1) * D], k == 0, k == 1)
                    last.then_inc(s_Y.sem, 1)

            program(pe, step, lambda kind, n: norm.tensor(pe, kind, n))

        @block.scalar
        def _(act):
            start(act, w_hi, s_sg, s_hh)
            def step(i, kind, tg, n, more):
                if kind == "w":
                    j, e = w_event(i, tg, n)
                    act.wait_ge(w_32.sem, w_32.at(j, e))
                    if not (type(i) is int and i < 0):
                        act.wait_ge(s_Y.sem, s_Y.at(i, (tg - 1) * 4 * GROUPS - 1))
                    nc.scalar.activation(halves(tg, n)[0], w32[:, (n % 2) * 512:(n % 2 + 1) * 512], ACT.Copy).then_inc(w_hi.sem, 1)
                if kind == "gu":
                    j, e = event(i, tg, n)
                    o = n * GT
                    act.wait_ge(s_gp.sem, s_gp.at(j, e))
                    act.wait_ge(s_h.sem, s_h.at(j, e - 2))
                    nc.scalar.activation(sg[:, o:o + GT], psG[n][:, :], ACT.Silu).then_inc(s_sg.sem, 1)
                    act.wait_ge(s_h.sem, s_h.at(j, e))
                    if not (type(i) is int and i < 0):
                        act.wait_ge(s_Y.sem, s_Y.at(i, 4 * (tg - 1) - 1))
                    c = (tg % 2) * 1024 + n * GT
                    nc.scalar.activation(h_h[:, c:c + GT], hf[:, o:o + GT], ACT.Copy).then_inc(s_hh.sem, 1)

            def prologue(kind, n):
                norm.scalar(act, kind, n)
                if kind == "rstd":
                    rstd.scalar(act)

            program(act, step, prologue)

        @block.vector
        def _(v):
            start(v, w_32, w_lo, s_h, s_hl, s_xr)
            def step(i, kind, tg, n, more):
                if kind == "w":
                    j, e = w_event(i, tg, n)
                    sl, w = slice(n * 512, (n + 1) * 512), w32[:, (n % 2) * 512:(n % 2 + 1) * 512]
                    v.wait_ge(w_in[n].sem, w_in[n].at(j, e // NCH * 2 + 1))
                    v.wait_ge(w_lo.sem, w_lo.ring(j, e, 2))
                    nc.vector.tensor_tensor(w, q_st[:, sl], s_st[:, sl], ALU.mult).then_inc(w_32.sem, 1)
                if kind == "w_lo":
                    j, e = w_event(i, tg, n)
                    w = w32[:, (n % 2) * 512:(n % 2 + 1) * 512]
                    v.wait_ge(w_hi.sem, w_hi.at(j, e))
                    hi, lo = halves(tg, n)
                    nc.vector.tensor_tensor(lo, w, hi.bitcast(F32), ALU.subtract).then_inc(w_lo.sem, 1)
                if kind == "gu":
                    j, e = event(i, tg, n)
                    o = n * GT
                    v.wait_ge(s_sg.sem, s_sg.at(j, e))
                    v.wait_ge(s_up.sem, s_up.at(j, e))
                    nc.vector.tensor_tensor(hf[:, o:o + GT], psU[n][:, :], sg[:, o:o + GT], ALU.mult).then_inc(s_h.sem, 1)
                    v.wait_ge(s_hh.sem, s_hh.at(j, e))
                    c = (tg % 2) * 1024 + n * GT
                    nc.vector.tensor_tensor(h_l[:, c:c + GT], hf[:, o:o + GT], h_h[:, c:c + GT].bitcast(F32),
                                            ALU.subtract).then_inc(s_hl.sem, 1)
                if kind == "Y":
                    y = tg * 4 + n
                    v.wait_ge(s_Y.sem, s_Y.at(i, y))
                    nc.vector.tensor_tensor(xr(y % TILES), psY[n % 2][:, :], xr(y % TILES), ALU.add).then_inc(s_xr.sem, 1)

            def prologue(kind, n):
                norm.vector(v, kind, n)
                if kind == "rstd":
                    rstd.vector(v)

            program(v, step, prologue)


def kernel(**inputs):
    import concourse.bacc as bacc
    from concourse.bass_utils import run_bass_kernel_spmd as run

    a = {n: np.asarray(v) for n, v in inputs.items()}
    p = np.arange(P)
    half, head, d8 = p // 64, p % 64 // 8, p % 8
    g = lambda j: 2 * j + head // HPG
    q_rows = np.concatenate([g(j) * 96 + head % HPG * 16 + half * 8 + d8 for j in range(4)])
    k_rows = np.concatenate([g(j) * 96 + 64 + half * 8 + d8 for j in range(4)])
    v_rows = (np.arange(G)[:, None] * 96 + 80 + np.arange(16)[None, :]).ravel()
    rows = np.concatenate([q_rows, k_rows, v_rows])
    d_rows = np.concatenate([((gh * 4 + p // 32) * 4 + p % 32 // 16 * 2 + par) * 16 + p % 16
                             for gh in range(2) for par in range(2)])
    swap = (p + 64) % P
    b = a["L0_attn_b_qkv"]
    bq, bk = b[q_rows].reshape(4, P).T, b[k_rows].reshape(4, P).T
    hmask = (head[:, None] == np.arange(8)[None, :]).astype(np.float32)
    iota = (p[:, None] + P * np.arange(4)[None, :]).astype(np.float32)
    small = np.concatenate([bq, bk, bq[swap], bk[swap], hmask, iota, b[v_rows][:, None]], axis=1).astype(np.float32)

    def angles(n, dim, base):
        inv = np.float32(1.0) / np.float32(base) ** (np.arange(0, dim, 2, dtype=np.float32) / np.float32(dim))
        return np.arange(n, dtype=np.float32)[:, None] * inv[None, :].astype(np.float32)

    an = angles(S, HD_SELF, 1000000.0).T[d8]
    sign = np.where(half == 0, -1.0, 1.0).astype(np.float32)[:, None]
    rope_self = np.stack([np.cos(an), sign * np.sin(an)]).astype(np.float32)
    ax = angles(MAX_POS, HD_X, 10000.0)
    rope_x = np.concatenate([np.cos(ax), np.cos(ax), -np.sin(ax), np.sin(ax)], axis=1).astype(np.float32)
    causal = (np.arange(S)[None, :] <= (p % S)[:, None]).astype(np.int32)

    arrays = {
        "x": a["x"].reshape(T, D), "ctx": a["ctx_4096"].reshape(T, D), "pos": a["pos_BxS2"].reshape(T),
        "mask": a["mask_BxSxS2_ik0"], "w_qkv": a["L0_attn_w_qkv"].T[:, rows],
        "w_dense": a["L0_attn_w_dense"].T[d_rows], "b_dense": a["L0_attn_b_dense"],
        "wq": a["L0_xattn_Wq"], "wk": a["L0_xattn_Wk"], "wv": a["L0_xattn_Wv"], "wo": a["L0_xattn_Wo"],
        "gate_q": a["L0_ffn_gate_q"].T, "gate_s": a["L0_ffn_gate_s"].T, "up_q": a["L0_ffn_up_q"].T,
        "up_s": a["L0_ffn_up_s"].T, "down_q": a["L0_ffn_down_q"].T, "down_s": a["L0_ffn_down_s"].T,
        "small": small, "ident": np.eye(P, dtype=np.float32), "rope_self": rope_self, "rope_x": rope_x,
        "causal": causal,
    }
    arrays = {n: np.ascontiguousarray(v) for n, v in arrays.items()}
    nc = bacc.Bacc("TRN2", target_bir_lowering=False, num_devices=1, dynamic_dma_scratch_size=1024)
    io = {n: nc.dram_tensor("in_" + n, v.shape, mybir.dt.from_np(v.dtype), kind="ExternalInput").ap()
          for n, v in arrays.items()}
    out = nc.dram_tensor("out_x", (T, D), F32, kind="ExternalOutput").ap()
    build(nc, io, out)
    r = run(nc, [{"in_" + n: v for n, v in arrays.items()}], core_ids=[0])
    return r.results[0]["out_x"].reshape(B, S, D)
```
